# Optimizing a Trainium2 kernel written in Bass

```python
import numpy as np
import jax
import jax.numpy as jnp

def _softmax(x, axis=-1):
    return jax.nn.softmax(x, axis=axis)

def _gelu(x):
    return jax.nn.gelu(x, approximate=True)

def _silu(x):
    return jax.nn.silu(x)

def _sigmoid(x):
    return jax.nn.sigmoid(x)

def _layernorm(x, axis=-1, eps=1e-05):
    m = jnp.mean(x, axis=axis, keepdims=True)
    v = jnp.var(x, axis=axis, keepdims=True)
    return (x - m) / jnp.sqrt(v + eps)

def _scatter_add(tgt, idx, src, axis=0):
    return tgt.at[idx].add(src)

def _segment_sum(src, seg, n):
    return jax.ops.segment_sum(src, seg, n)
kernel_name = 'mk_sandwich_d1_jaxref_r8_4b8934'

def setup_inputs(seed: int=0):
    np.random.seed(seed)
    _w = jnp.asarray

    def _L0_attn_setup():
        import jax, jax.numpy as jnp
        import numpy as np
        from jax import lax
        B, T, D, H, K = (2, 256, 128, 16, 4)
        HD = D // H
        CONV_DIM = 3 * D

        def _l2norm(x, eps=1e-06):
            return x * lax.rsqrt(jnp.sum(x * x, axis=-1, keepdims=True) + eps)

        def _forward(x, W_qkv, conv_w, W_z, W_b, W_a, dt_bias, A_log, W_out):
            b_, t_, d_ = x.shape
            mixed = jnp.einsum('btd,cd->btc', x, W_qkv)
            c = mixed.transpose(0, 2, 1)
            c = lax.conv_general_dilated(c, conv_w, window_strides=(1,), padding=[(K - 1, 0)], dimension_numbers=('NCH', 'OIH', 'NCH'), feature_group_count=CONV_DIM)
            mixed = jax.nn.silu(c).transpose(0, 2, 1)
            q, k, v = jnp.split(mixed, [d_, 2 * d_], axis=-1)
            q = q.reshape(b_, t_, H, HD)
            k = k.reshape(b_, t_, H, HD)
            v = v.reshape(b_, t_, H, HD)
            z = jnp.einsum('btd,ed->bte', x, W_z).reshape(b_, t_, H, HD)
            beta = jax.nn.sigmoid(jnp.einsum('btd,hd->bth', x, W_b))
            g = -jnp.exp(A_log) * jax.nn.softplus(jnp.einsum('btd,hd->bth', x, W_a) + dt_bias)
            q = _l2norm(q) * HD ** (-0.5)
            k = _l2norm(k)
            qs = q.transpose(1, 0, 2, 3)
            ks_ = k.transpose(1, 0, 2, 3)
            vs = v.transpose(1, 0, 2, 3)
            bs = beta.transpose(1, 0, 2)
            gs = g.transpose(1, 0, 2)

            def step(S, inp):
                q_t, k_t, v_t, b_t, g_t = inp
                S = S * jnp.exp(g_t)[..., None, None]
                S = S + jnp.einsum('bhd,bhv->bhdv', k_t, v_t * b_t[..., None])
                o_t = jnp.einsum('bhd,bhdv->bhv', q_t, S)
                return (S, o_t)
            S0 = jnp.zeros((b_, H, HD, HD), x.dtype)
            _, out = lax.scan(step, S0, (qs, ks_, vs, bs, gs))
            out = out.transpose(1, 0, 2, 3)
            var = jnp.mean(out * out, axis=-1, keepdims=True)
            out = out * lax.rsqrt(var + 1e-06) * jax.nn.silu(z)
            out = out.reshape(b_, t_, d_)
            return jnp.einsum('btd,ed->bte', out, W_out)
        key = jax.random.key(seed)
        ks = jax.random.split(key, 8)
        s = 0.02
        return {'x': jax.random.normal(ks[0], (B, T, D), jnp.float32), 'W_qkv': jax.random.normal(ks[1], (CONV_DIM, D), jnp.float32) * s, 'conv_w': jax.random.normal(ks[2], (CONV_DIM, 1, K), jnp.float32) * 0.25, 'W_z': jax.random.normal(ks[3], (D, D), jnp.float32) * s, 'W_b': jax.random.normal(ks[4], (H, D), jnp.float32) * s, 'W_a': jax.random.normal(ks[5], (H, D), jnp.float32) * s, 'dt_bias': jnp.ones((H,), jnp.float32), 'A_log': jnp.log(jnp.arange(1, H + 1, dtype=jnp.float32)), 'W_out': jax.random.normal(ks[6], (D, D), jnp.float32) * s}
    _L0_attn_in = _L0_attn_setup()

    def _L0_ffn_setup():
        import jax, jax.numpy as jnp
        import numpy as np
        B, S, D = (1, 256, 128)
        I = 256
        E = 8
        K = 2
        LIMIT = 7.0
        ALPHA = 1.702
        EPS = 1e-05

        def _swiglu(h):
            x_glu = jnp.minimum(h[..., ::2], LIMIT)
            x_lin = jnp.clip(h[..., 1::2], -LIMIT, LIMIT)
            return x_glu * jax.nn.sigmoid(ALPHA * x_glu) * (x_lin + 1.0)

        def _moe(t, gate_w, gate_b, mlp1_w, mlp1_b, mlp2_w, mlp2_b):
            T = t.shape[0]
            logits = t @ gate_w + gate_b
            top_v, top_i = jax.lax.top_k(logits, K)
            probs = jax.nn.softmax(top_v, axis=-1)
            w = jnp.zeros((T, E), t.dtype).at[jnp.arange(T)[:, None], top_i].set(probs)

            def body(acc, ew):
                w1, b1, w2, b2, we = ew
                h = _swiglu(t @ w1 + b1)
                y = h @ w2 + b2
                return (acc + we[:, None] * y, None)
            acc0 = jnp.zeros((T, t.shape[1]), t.dtype)
            acc, _ = jax.lax.scan(body, acc0, (mlp1_w, mlp1_b, mlp2_w, mlp2_b, w.T))
            return acc
        key = jax.random.key(seed)
        ks = jax.random.split(key, 4)
        s = 0.02
        return {'x': jax.random.normal(ks[0], (B, S, D), jnp.float32), 'norm_scale': jnp.ones((D,), jnp.float32), 'gate_w': jax.random.normal(ks[1], (D, E), jnp.float32) * s, 'gate_b': jnp.zeros((E,), jnp.float32), 'mlp1_w': jax.random.normal(ks[2], (E, D, 2 * I), jnp.float32) * s, 'mlp1_b': jnp.zeros((E, 2 * I), jnp.float32), 'mlp2_w': jax.random.normal(ks[3], (E, I, D), jnp.float32) * s, 'mlp2_b': jnp.zeros((E, D), jnp.float32)}
    _L0_ffn_in = _L0_ffn_setup()
    _d = {'L0_attn_x': _L0_attn_in['x'], 'L0_attn_W_qkv': _L0_attn_in['W_qkv'], 'L0_attn_conv_w': _L0_attn_in['conv_w'], 'L0_attn_W_z': _L0_attn_in['W_z'], 'L0_attn_W_b': _L0_attn_in['W_b'], 'L0_attn_W_a': _L0_attn_in['W_a'], 'L0_attn_dt_bias': _L0_attn_in['dt_bias'], 'L0_attn_A_log': _L0_attn_in['A_log'], 'L0_attn_W_out': _L0_attn_in['W_out'], 'L0_ffn_norm_scale': _L0_ffn_in['norm_scale'], 'L0_ffn_gate_w': _L0_ffn_in['gate_w'], 'L0_ffn_gate_b': _L0_ffn_in['gate_b'], 'L0_ffn_mlp1_w': _L0_ffn_in['mlp1_w'], 'L0_ffn_mlp1_b': _L0_ffn_in['mlp1_b'], 'L0_ffn_mlp2_w': _L0_ffn_in['mlp2_w'], 'L0_ffn_mlp2_b': _L0_ffn_in['mlp2_b']}
    _x0 = _d['L0_attn_x']
    _d['L0_attn_x'] = jax.random.normal(jax.random.fold_in(jax.random.key(seed), 1), (16, 512, 128), dtype=_x0.dtype)
    del _x0
    return _d

def reference(L0_attn_x, L0_attn_W_qkv, L0_attn_conv_w, L0_attn_W_z, L0_attn_W_b, L0_attn_W_a, L0_attn_dt_bias, L0_attn_A_log, L0_attn_W_out, L0_ffn_norm_scale, L0_ffn_gate_w, L0_ffn_gate_b, L0_ffn_mlp1_w, L0_ffn_mlp1_b, L0_ffn_mlp2_w, L0_ffn_mlp2_b):

    def _L0_attn_ref(x, W_qkv, conv_w, W_z, W_b, W_a, dt_bias, A_log, W_out):
        import jax, jax.numpy as jnp
        import numpy as np
        from jax import lax
        B, T, D, H, K = (2, 256, 128, 16, 4)
        HD = D // H
        CONV_DIM = 3 * D

        def _l2norm(x, eps=1e-06):
            return x * lax.rsqrt(jnp.sum(x * x, axis=-1, keepdims=True) + eps)

        def _forward(x, W_qkv, conv_w, W_z, W_b, W_a, dt_bias, A_log, W_out):
            b_, t_, d_ = x.shape
            mixed = jnp.einsum('btd,cd->btc', x, W_qkv)
            c = mixed.transpose(0, 2, 1)
            c = lax.conv_general_dilated(c, conv_w, window_strides=(1,), padding=[(K - 1, 0)], dimension_numbers=('NCH', 'OIH', 'NCH'), feature_group_count=CONV_DIM)
            mixed = jax.nn.silu(c).transpose(0, 2, 1)
            q, k, v = jnp.split(mixed, [d_, 2 * d_], axis=-1)
            q = q.reshape(b_, t_, H, HD)
            k = k.reshape(b_, t_, H, HD)
            v = v.reshape(b_, t_, H, HD)
            z = jnp.einsum('btd,ed->bte', x, W_z).reshape(b_, t_, H, HD)
            beta = jax.nn.sigmoid(jnp.einsum('btd,hd->bth', x, W_b))
            g = -jnp.exp(A_log) * jax.nn.softplus(jnp.einsum('btd,hd->bth', x, W_a) + dt_bias)
            q = _l2norm(q) * HD ** (-0.5)
            k = _l2norm(k)
            qs = q.transpose(1, 0, 2, 3)
            ks_ = k.transpose(1, 0, 2, 3)
            vs = v.transpose(1, 0, 2, 3)
            bs = beta.transpose(1, 0, 2)
            gs = g.transpose(1, 0, 2)

            def step(S, inp):
                q_t, k_t, v_t, b_t, g_t = inp
                S = S * jnp.exp(g_t)[..., None, None]
                S = S + jnp.einsum('bhd,bhv->bhdv', k_t, v_t * b_t[..., None])
                o_t = jnp.einsum('bhd,bhdv->bhv', q_t, S)
                return (S, o_t)
            S0 = jnp.zeros((b_, H, HD, HD), x.dtype)
            _, out = lax.scan(step, S0, (qs, ks_, vs, bs, gs))
            out = out.transpose(1, 0, 2, 3)
            var = jnp.mean(out * out, axis=-1, keepdims=True)
            out = out * lax.rsqrt(var + 1e-06) * jax.nn.silu(z)
            out = out.reshape(b_, t_, d_)
            return jnp.einsum('btd,ed->bte', out, W_out)
        return _forward(x, W_qkv, conv_w, W_z, W_b, W_a, dt_bias, A_log, W_out)

    def _L0_ffn_ref(x, norm_scale, gate_w, gate_b, mlp1_w, mlp1_b, mlp2_w, mlp2_b):
        import jax, jax.numpy as jnp
        import numpy as np
        B, S, D = (1, 256, 128)
        I = 256
        E = 8
        K = 2
        LIMIT = 7.0
        ALPHA = 1.702
        EPS = 1e-05

        def _swiglu(h):
            x_glu = jnp.minimum(h[..., ::2], LIMIT)
            x_lin = jnp.clip(h[..., 1::2], -LIMIT, LIMIT)
            return x_glu * jax.nn.sigmoid(ALPHA * x_glu) * (x_lin + 1.0)

        def _moe(t, gate_w, gate_b, mlp1_w, mlp1_b, mlp2_w, mlp2_b):
            T = t.shape[0]
            logits = t @ gate_w + gate_b
            top_v, top_i = jax.lax.top_k(logits, K)
            probs = jax.nn.softmax(top_v, axis=-1)
            w = jnp.zeros((T, E), t.dtype).at[jnp.arange(T)[:, None], top_i].set(probs)

            def body(acc, ew):
                w1, b1, w2, b2, we = ew
                h = _swiglu(t @ w1 + b1)
                y = h @ w2 + b2
                return (acc + we[:, None] * y, None)
            acc0 = jnp.zeros((T, t.shape[1]), t.dtype)
            acc, _ = jax.lax.scan(body, acc0, (mlp1_w, mlp1_b, mlp2_w, mlp2_b, w.T))
            return acc
        Bx, Sx, Dx = x.shape
        ms = jnp.mean(x * x, axis=-1, keepdims=True)
        t = (x * jax.lax.rsqrt(ms + EPS) * norm_scale).reshape(Bx * Sx, Dx)
        y = _moe(t, gate_w, gate_b, mlp1_w, mlp1_b, mlp2_w, mlp2_b)
        return x + y.reshape(Bx, Sx, Dx)
    x = L0_attn_x
    x = x + _layernorm(_L0_attn_ref(_layernorm(x, axis=-1), L0_attn_W_qkv, L0_attn_conv_w, L0_attn_W_z, L0_attn_W_b, L0_attn_W_a, L0_attn_dt_bias, L0_attn_A_log, L0_attn_W_out), axis=-1)
    x = x + _layernorm(_L0_ffn_ref(_layernorm(x, axis=-1), L0_ffn_norm_scale, L0_ffn_gate_w, L0_ffn_gate_b, L0_ffn_mlp1_w, L0_ffn_mlp1_b, L0_ffn_mlp2_w, L0_ffn_mlp2_b), axis=-1)
    return x

_drawn_inputs = setup_inputs


def setup_inputs(seed=0):
    import zlib

    import numpy as np

    out = dict(_drawn_inputs(seed))
    spreads = {'L0_attn_dt_bias': (1.0, 0.6),
     'L0_ffn_norm_scale': (1.0, 0.6),
     'L0_ffn_gate_b': (0.0, 0.356),
     'L0_ffn_mlp1_b': (0.0, 0.8),
     'L0_ffn_mlp2_b': (0.0, 0.271)}
    factors = {'L0_attn_W_a': 3.766, 'L0_ffn_mlp1_w': 4.817, 'L0_ffn_mlp2_w': 4.368}
    for name, (base, spread) in spreads.items():
        noise = np.random.default_rng([zlib.crc32(name.encode()), seed]).standard_normal(out[name].shape)
        drawn = base * np.exp(spread * noise) if base else spread * noise
        out[name] = jnp.asarray(drawn.astype(out[name].dtype))
    for name, factor in factors.items():
        out[name] = (out[name] * factor).astype(out[name].dtype)
    return out
```

```python
from contextlib import ExitStack

import concourse.bass as bass
from concourse import mybir

F32 = mybir.dt.float32
F16 = mybir.dt.float16
BF16 = mybir.dt.bfloat16
I32 = mybir.dt.int32
ALU = mybir.AluOpType
ACT = mybir.ActivationFunctionType
AX = mybir.AxisListType

P = 128
EPS_LN = 1e-5
EPS_L2 = 1e-6
EPS_MS = 1e-6
EPS_RMS = 1e-5
LIMIT = 7.0
ALPHA = 1.702
GUARD = -25.0
FAR = float(1 << 20)


def build_program(nc, x, W_qkv, conv_w, W_z, W_b, W_a, dt_bias, A_log, W_out,
                  norm_scale, gate_w, gate_b, mlp1_w, mlp1_b, mlp2_w, mlp2_b, out):
    NB, T, D = x.shape
    H = W_a.shape[0]
    HD = D // H
    K = conv_w.shape[2]
    E = mlp1_w.shape[0]
    HID = mlp2_w.shape[1]
    C = T // P
    N = NB * T
    NT = N // P
    TOP = 2
    W = P + 2
    REGION = N + P
    TILES = (TOP * N + E * (P - 1)) // P + 1
    TILES += TILES % 2
    SPARE = TILES - TOP * NT
    assert D == P and T == 512 and HD == 8 and K == 4 and 2 * HID == 512 and NB % 2 == 0

    rows = nc.dram_tensor("routed_rows", [E * REGION + SPARE * P, W], F32, kind="Internal").ap()
    results = nc.dram_tensor("expert_results", [TOP * N, P], F32, kind="Internal").ap()

    xv = x.rearrange("b (c p) d -> p (b c) d", p=P)
    ov = out.rearrange("b (c p) d -> p (b c) d", p=P)
    rv = results.rearrange("(k n p) d -> p k n d", k=TOP, p=P)

    with ExitStack() as ctx:
        def sb(name, shape, dt=F32):
            return ctx.enter_context(nc.sbuf_tensor(name, shape, dt))

        def sem(name):
            return ctx.enter_context(nc.semaphore(name))

        def sems(names):
            return {n: sem(n) for n in names.split()}

        bank = [ctx.enter_context(nc.psum_tensor(f"bank{i}", [P, 512], F32)) for i in range(8)]
        B_T, B_P0, B_P1, B_N, B_B0, B_B1, B_O, B_W = bank

        X = sb("X", [P, NT, P])
        NORM3 = sb("NORM3", [P, NT, 2])
        w1hi = sb("w1hi", [P, E, 512], F16)
        w1lo = sb("w1lo", [P, E, 512], F16)
        w2hi = sb("w2hi", [P, E, 2, P], F16)
        w2lo = sb("w2lo", [P, E, 2, P], F16)
        b1p = sb("b1p", [P, E, 512], F16)
        b2p = sb("b2p", [P, E, P], F16)
        ones16 = sb("ones16", [P, P], F16)
        ident = sb("ident", [P, P])
        wchi = sb("wchi", [P, K, 3, P], F16)
        wclo = sb("wclo", [P, K, 3, P], F16)
        wphi = sb("wphi", [P, 3, P], F16)
        wplo = sb("wplo", [P, 3, P], F16)
        woT = sb("woT", [P, P])
        gw = sb("gw", [P, E])
        gb = sb("gb", [P, E])
        block = sb("block", [P, H, HD])
        blockms = sb("blockms", [P, H, HD])
        sel = sb("sel", [P, HD, H, HD], F16)
        red = sb("red", [P, HD, H, HD])
        rep = sb("rep", [H, H, HD])
        hb = sb("hb", [P, 2])
        negA = sb("negA", [P, 1])
        tri = sb("tri", [P, P], BF16)
        ones_b = sb("ones_b", [P, P], BF16)
        rank = sb("rank", [P, C, E])
        region0 = sb("region0", [P, E])
        token = sb("token", [P, C, TOP])
        count = sb("count", [P, E])

        s = sems(
            "x_in w_in const_pool setup_pe setup_act setup_dve wstage bias_row "
            "f_stats f_rstd f_u f_uT f_xhi f_xlo f_pa f_pb f_pv f_pk f_pq f_pz "
            "f_ea f_dec f_eb f_beta f_ev f_sv f_ek f_sk f_eq f_sq f_ez f_sz f_vs f_vb f_ks f_qs f_zs "
            "f_vhi f_vlo f_k2 f_q2 f_nk f_nq f_lk f_lq f_rk f_rq f_kn f_qn "
            "e_o2 e_no e_lo e_ro e_og e_gz e_wo e_st2 e_rs2 e_y e_x1 e_st3 e_rs3 e_ms e_rr e_tsc e_t e_t2 "
            "e_tT e_tTs e_lg e_top e_pd e_p1 e_mask e_pos e_slot e_meta "
        )
        s_bc = [sem(f"s_bc{v}") for v in range(2)]
        s_kv, s_scan, s_qs, s_red = sem("s_kv"), sem("s_scan"), sem("s_qs"), sem("s_red")
        r_chain = sem("r_chain")
        s_sent = [sem(f"s_sent{p}") for p in range(2)]
        passed = sem("passed")

        def sent(n, p):
            return 8 * C * TOP * (n - 1 - p)

        def fence(eng, semaphore, n):
            if isinstance(n, int) and n <= 0:
                return
            eng.wait_ge(semaphore, n)
            eng.sem_inc(passed, 1)

        def after(eng, semaphore, n):
            if isinstance(n, int) and n <= 0:
                return
            eng.wait_ge(semaphore, n)

        with ExitStack() as stage:
            def st(name, shape, dt=F32):
                return stage.enter_context(nc.sbuf_tensor(name, shape, dt))

            wq = st("wq", [P, 3, P])
            cw = st("cw", [P, 3, K])
            wt = st("wt", [P, K, 3, P])
            wz = st("wz", [P, P])
            wo = st("wo", [P, P])
            wab = st("wab", [H, 2, P])
            hb0 = st("hb0", [H, 2])
            ns = st("ns", [P, 1])
            gw0 = st("gw0", [P, E])
            w1 = st("w1", [P, E, 512])
            w2 = st("w2", [P, E, 2, P])
            b1 = st("b1", [1, E, 512])
            b2 = st("b2", [1, E, P])
            b1l = st("b1l", [1, E, 512], F16)
            b2l = st("b2l", [1, E, P], F16)
            pad = st("pad", [P, W])

            with nc.Block() as blk:
                @blk.sync
                def _(sp):
                    loads = [
                        (wq[:], W_qkv.rearrange("(g p) d -> p g d", p=P)),
                        (cw[:], conv_w.rearrange("(g p) o k -> p g (o k)", p=P)),
                        (wz[:], W_z), (wo[:], W_out), (wab[:, 0, :], W_a), (wab[:, 1, :], W_b),
                        (hb0[:, 0:1], dt_bias.rearrange("(h a) -> h a", a=1)),
                        (hb0[:, 1:2], A_log.rearrange("(h a) -> h a", a=1)),
                        (ns[:], norm_scale.rearrange("(d a) -> d a", a=1)),
                        (gw0[:], gate_w), (gb[:], gate_b.rearrange("(a e) -> a e", a=1).to_broadcast([P, E])),
                        (w1[:], mlp1_w.rearrange("e d f -> d e f")),
                        (w2[:], mlp2_w.rearrange("e (c p) d -> p e c d", p=P)),
                        (b1[:], mlp1_b.rearrange("(a e) f -> a e f", a=1)),
                        (b2[:], mlp2_b.rearrange("(a e) f -> a e f", a=1)),
                    ]
                    assert len(loads) == 15
                    for to, of in loads:
                        sp.dma_start(to, of).then_inc(s["w_in"], 16)
                    for q in range(4):
                        a, b = q * NT // 4, (q + 1) * NT // 4
                        sp.dma_start(X[:, a:b, :], xv[:, a:b, :]).then_inc(s["x_in"], 16)
                    sp.wait_ge(s["setup_dve"], 3)
                    sp.dma_start(b1p[1:2], b1l[:]).then_inc(s["bias_row"], 16)
                    sp.dma_start(b2p[1:2], b2l[:]).then_inc(s["bias_row"], 16)
                    sp.wait_ge(s["const_pool"], 2)
                    for n in range(SPARE):
                        a = E * REGION + n * P
                        sp.dma_start(rows[a:a + P, :], pad[:]).then_inc(s["bias_row"], 16)
                    sp.wait_ge(s["bias_row"], 16 * (2 + SPARE))
                    sp.wait_ge(s["w_in"], 16 * len(loads))
                    sp.wait_ge(s["x_in"], 64)

                @blk.gpsimd
                def _(pool):
                    n = 0

                    def step(ins):
                        nonlocal n
                        n += 1
                        ins.then_inc(s["wstage"], 1)

                    step(pool.memset(pad[:], 0.0))
                    pool.wait_ge(s["wstage"], n)
                    pool.memset(pad[:, P + 1:P + 2], FAR).then_inc(s["const_pool"], 2)
                    step(pool.memset(ident[:], 0.0))
                    step(pool.memset(block[:], 1.0))
                    step(pool.memset(sel[:], 0.0))
                    step(pool.memset(red[:], 0.0))
                    step(pool.memset(rep[:], 1.0))
                    step(pool.memset(ones_b[:], 1.0))
                    step(pool.memset(tri[:], 1.0))
                    step(pool.memset(ones16[:], 1.0))
                    step(pool.memset(b1p[:], 0.0))
                    step(pool.memset(b2p[:], 0.0))
                    step(pool.memset(count[:], 0.0))
                    pool.wait_ge(s["wstage"], n)
                    step(pool.affine_select(out=ident[:], in_=ident[:], compare_op=ALU.not_equal, fill=1.0,
                                            base=0, pattern=[[-1, P]], channel_multiplier=1))
                    step(pool.affine_select(out=block[:], in_=block[:], compare_op=ALU.is_ge, fill=0.0,
                                            base=0, pattern=[[-HD, H], [0, HD]], channel_multiplier=1))
                    step(pool.affine_select(out=rep[:], in_=rep[:], compare_op=ALU.is_equal, fill=0.0,
                                            base=0, pattern=[[-1, H], [0, HD]], channel_multiplier=1))
                    step(pool.affine_select(out=tri[:], in_=tri[:], compare_op=ALU.is_gt, fill=0.0,
                                            base=0, pattern=[[1, P]], channel_multiplier=-1))
                    for v in range(HD):
                        step(pool.affine_select(out=sel[:, v], in_=sel[:, v], compare_op=ALU.not_equal, fill=1.0,
                                                base=-v, pattern=[[-HD, H], [0, HD]], channel_multiplier=1))
                    step(pool.iota(rank[:], pattern=[[0, C], [-1, E]], base=E, channel_multiplier=0,
                                   allow_small_or_imprecise_dtypes=True))
                    for e in range(E):
                        step(pool.memset(region0[:, e:e + 1], float(e * REGION)))
                    for k in range(TOP):
                        step(pool.iota(token[:, :, k:k + 1], pattern=[[P, C], [0, 1]], base=k * N,
                                       channel_multiplier=1, allow_small_or_imprecise_dtypes=True))
                    pool.wait_ge(s["wstage"], n)
                    step(pool.affine_select(out=block[:], in_=block[:], compare_op=ALU.is_ge, fill=0.0,
                                            base=HD - 1, pattern=[[HD, H], [0, HD]], channel_multiplier=-1))
                    pool.wait_ge(s["wstage"], n)
                    for v in range(HD):
                        step(pool.tensor_copy(red[:, v, :, v:v + 1], block[:, :, v:v + 1]))
                    step(pool.tensor_scalar(blockms[:], block[:], 1.0 / HD, None, ALU.mult))
                    pool.wait_ge(s["wstage"], n)
                    pool.memset(ones16[:, 0:1], 1.0).then_inc(s["const_pool"], 1)

                @blk.vector
                def _(dve):
                    dve.wait_ge(s["w_in"], 16 * 15)
                    for j in range(K):
                        for g in range(3):
                            dve.tensor_scalar(wt[:, j, g, :], wq[:, g, :], cw[:, g, j:j + 1], None, ALU.mult)
                    dve.tensor_scalar(gw[:], gw0[:], ns[:, 0:1], None, ALU.mult)
                    dve.tensor_scalar(w1[:], w1[:], ns[:, 0:1], None, ALU.mult).then_inc(s["setup_dve"], 1)
                    dve.wait_ge(s["const_pool"], 3)
                    dve.wait_ge(s["setup_dve"], 1)
                    dve.tensor_copy(b2p[0:1], b2[:])
                    for h in range(2):
                        last = dve.tensor_copy(b1p[0:1, :, h * HID:(h + 1) * HID],
                                               b1[:, :, h:512:2])
                    last.then_inc(s["setup_dve"], 1)
                    dve.wait_ge(s["setup_dve"], 2)
                    dve.tensor_tensor(b2l[:], b2[:], b2p[0:1], ALU.subtract)
                    for h in range(2):
                        last = dve.tensor_tensor(b1l[:, :, h * HID:(h + 1) * HID], b1[:, :, h:512:2],
                                                 b1p[0:1, :, h * HID:(h + 1) * HID], ALU.subtract)
                    last.then_inc(s["setup_dve"], 1)
                    dve.wait_ge(s["setup_act"], 3)
                    for h in range(2):
                        cut = slice(h * HID, (h + 1) * HID)
                        dve.tensor_tensor(w1lo[:, :, cut], w1[:, :, h:512:2], w1hi[:, :, cut], ALU.subtract)
                    dve.tensor_tensor(w2lo[:], w2[:], w2hi[:], ALU.subtract)
                    for j in range(K):
                        dve.wait_ge(s["setup_act"], 4 + j)
                        dve.tensor_tensor(wclo[:, j], bank[j][:, 0:3 * P], wchi[:, j], ALU.subtract)
                    dve.wait_ge(s["setup_act"], 4 + K)
                    dve.tensor_tensor(wplo[:], bank[4][:, 0:3 * P], wphi[:], ALU.subtract)

                @blk.scalar
                def _(act):
                    act.preload_act_table_set("natural_log_exp_and_others")
                    act.wait_ge(s["setup_dve"], 1)
                    for h in range(2):
                        act.activation(w1hi[:, :, h * HID:(h + 1) * HID], w1[:, :, h:512:2],
                                       ACT.Copy).then_inc(s["setup_act"], 1)
                    act.activation(w2hi[:], w2[:], ACT.Copy).then_inc(s["setup_act"], 1)
                    for j in range(K):
                        act.wait_ge(s["setup_pe"], j + 1)
                        act.activation(wchi[:, j], bank[j][:, 0:3 * P], ACT.Copy).then_inc(s["setup_act"], 1)
                    act.wait_ge(s["setup_pe"], K + 1)
                    act.activation(wphi[:], bank[4][:, 0:3 * P], ACT.Copy).then_inc(s["setup_act"], 1)
                    act.wait_ge(s["setup_pe"], K + 2)
                    act.activation(woT[:], bank[5][:, 0:P], ACT.Copy)
                    act.activation(hb[:], bank[5][:, P:P + 2], ACT.Copy).then_inc(s["setup_act"], 1)
                    act.wait_ge(s["setup_act"], 5 + K)
                    act.activation(negA[:], hb[:, 1:2], ACT.Exp).then_inc(s["setup_act"], 1)
                    act.wait_ge(s["setup_act"], 6 + K)
                    act.activation(negA[:], negA[:], ACT.Copy, scale=-1.0).then_inc(s["setup_act"], 1)

                @blk.tensor
                def _(pe):
                    pe.wait_ge(s["const_pool"], 3)
                    pe.wait_ge(s["setup_dve"], 1)
                    for j in range(K):
                        for g in range(3):
                            last = pe.transpose(bank[j][:, g * P:(g + 1) * P], wt[:, j, g, :], ident[:])
                        last.then_inc(s["setup_pe"], 1)
                    for a in range(2):
                        pe.matmul(bank[4][:, a * P:(a + 1) * P], wab[:, a, :],
                                  rep[:].rearrange("h a b -> h (a b)"), start=True, stop=True)
                    pe.transpose(bank[4][:, 2 * P:3 * P], wz[:], ident[:]).then_inc(s["setup_pe"], 1)
                    pe.transpose(bank[5][:, 0:P], wo[:], ident[:])
                    pe.matmul(bank[5][:, P:P + 2], rep[:].rearrange("h a b -> h (a b)"), hb0[:],
                              start=True, stop=True).then_inc(s["setup_pe"], 1)

        with ExitStack() as stage:
            def st(name, shape, dt=F32):
                return stage.enter_context(nc.sbuf_tensor(name, shape, dt))

            stats = st("stats", [P, C, 6])
            mv1 = st("mv1", [P, C, 2])
            rs1 = st("rs1", [P, C])
            U = st("U", [P, C, P])
            xhi = st("xhi", [P, 2, K - 1 + T], F16)
            xlo = st("xlo", [P, 2, K - 1 + T], F16)
            dec = st("dec", [P, 2, T])
            beta = st("beta", [P, T])
            sg = [st(f"sg{i}", [P, T]) for i in range(4)]
            vs, vb, ks, qs, sq1, sq2 = (st(n, [P, T]) for n in ("vs", "vb", "ks", "qs", "sq1", "sq2"))
            rk, rq = st("rk", [P, T]), st("rq", [P, T])
            kn, qn, zs = (st(n, [P, 2, T]) for n in ("kn", "qn", "zs"))
            vhi = st("vhi", [P, 2, T], F16)
            vlo = st("vlo", [P, 2, T], F16)
            kv = st("kv", [P, 2, T])
            Sv = st("Sv", [P, 2, T])
            qS = st("qS", [P, 2, T])
            osq, ro, og, gz = (st(n, [P, T]) for n in ("osq", "ro", "og", "gz"))
            st2 = st("st2", [P, C, 6])
            mv2 = st("mv2", [P, C, 2])
            rs2 = st("rs2", [P, C])
            st3 = st("st3", [P, C, 6])
            mv3 = st("mv3", [P, C, 2])
            rs3 = st("rs3", [P, C])
            yn = st("yn", [P, C, P])
            ms, rr, tsc = st("ms", [P, C]), st("rr", [P, C]), st("tsc", [P, C])
            tr = st("tr", [P, 2, C, TOP, W])
            tTs = st("tTs", [P, T])
            lg = st("lg", [P, C, E])
            lg2 = st("lg2", [P, C, E])
            eq, one1, one2 = st("eq", [P, C, E]), st("one1", [P, C, E]), st("one2", [P, C, E])
            mask = st("mask", [P, C, E], BF16)
            place = st("place", [P, C, E])
            m1, m2, wm, pd, p0 = (st(n, [P, C]) for n in ("m1", "m2", "wm", "pd", "p0"))
            slot = st("slot", [P, 2, C, TOP], I32)
            slotf = st("slotf", [P, C, TOP])
            dest = st("dest", [P, C, TOP])

            NR = 19

            def F_dve_a(dve, n, p, b):
                if isinstance(b, int):
                    dve.wait_ge(s["x_in"], 64)
                after(dve, s["f_rstd"], n - 1)
                for c in range(C):
                    dve.bn_stats(stats[:, c, :], X[:, bass.ds(b * C + c, 1), :]).then_inc(s["f_stats"], 1)
                fence(dve, s["f_stats"], n * 8 - 4)
                for c in range(C):
                    dve.bn_aggr(mv1[:, c, :], stats[:, c, :]).then_inc(s["f_stats"], 1)

            def F_dve_b(dve, n, p, b):
                dve.wait_ge(s["f_rstd"], n)
                after(dve, s["f_uT"], n - 1)
                for c in range(C):
                    last = dve.tensor_scalar(U[:, c, :], X[:, bass.ds(b * C + c, 1), :], mv1[:, c, 0:1],
                                             rs1[:, c:c + 1], ALU.subtract, ALU.mult)
                last.then_inc(s["f_u"], 1)

            def F_dve_c(dve, n, p):
                dve.wait_ge(s["f_xhi"], n)
                after(dve, s["f_pz"], n - 2)
                dve.tensor_tensor(xlo[:, p, K - 1:], B_T[:], xhi[:, p, K - 1:], ALU.subtract).then_inc(s["f_xlo"], 1)

            def F_dve_d(dve, n, p):
                dve.wait_ge(s["f_sv"], n)
                dve.tensor_tensor(vs[:], B_P0[:], sg[0][:], ALU.mult).then_inc(s["f_vs"], 1)
                dve.wait_ge(s["f_sk"], n)
                dve.tensor_tensor(ks[:], B_P1[:], sg[1][:], ALU.mult).then_inc(s["f_ks"], 1)
                dve.wait_ge(s["f_vs"], n)
                dve.wait_ge(s["f_beta"], n)
                dve.tensor_tensor(vb[:], vs[:], beta[:], ALU.mult).then_inc(s["f_vb"], 1)
                dve.wait_ge(s["f_sq"], n)
                dve.tensor_tensor(qs[:], B_P0[:], sg[2][:], ALU.mult).then_inc(s["f_qs"], 1)
                dve.wait_ge(s["f_sz"], n)
                dve.tensor_tensor(zs[:, p], B_P1[:], sg[3][:], ALU.mult).then_inc(s["f_zs"], 1)
                dve.wait_ge(s["f_vhi"], n)
                dve.tensor_tensor(vlo[:, p], vb[:], vhi[:, p], ALU.subtract).then_inc(s["f_vlo"], 1)
                dve.wait_ge(s["f_rk"], n)
                dve.tensor_tensor(kn[:, p], ks[:], rk[:], ALU.mult).then_inc(s["f_kn"], 1)
                dve.wait_ge(s["f_rq"], n)
                after(dve, s_qs, (n - 2) * HD)
                dve.tensor_tensor(qn[:, p], qs[:], rq[:], ALU.mult).then_inc(s["f_qn"], 1)

            def F_act(act, n, p):
                act.wait_ge(s["f_stats"], n * 8)
                after(act, s["f_u"], n - 1)
                act.activation(rs1[:], mv1[:, :, 1], ACT.Ln, bias=epsc[:, 0:1]).then_inc(s["f_ea"], 1)
                act.wait_ge(s["f_ea"], n * 2 - 1)
                act.activation(rs1[:], rs1[:], ACT.Exp, scale=-0.5).then_inc(s["f_rstd"], 1)
                act.wait_ge(s["f_uT"], n)
                after(act, s["f_pz"], n - 2)
                act.activation(xhi[:, p, K - 1:], B_T[:], ACT.Copy).then_inc(s["f_xhi"], 1)

            def F_act_b(act, n, p):
                act.wait_ge(s["f_pa"], n)
                after(act, s_scan, (n - 2) * HD)
                act.activation(dec[:, p], B_P0[:], ACT.Exp, bias=hb[:, 0:1]).then_inc(s["f_ea"], 1)
                act.wait_ge(s["f_pb"], n)
                after(act, s["f_vb"], n - 1)
                act.activation(beta[:], B_P1[:], ACT.Exp, scale=-1.0).then_inc(s["f_eb"], 1)
                act.wait_ge(s["f_ea"], n * 2)
                act.activation(dec[:, p], dec[:, p], ACT.Ln, bias=1.0).then_inc(s["f_dec"], 1)
                act.wait_ge(s["f_eb"], n)
                act.activation(beta[:], beta[:], ACT.Ln, bias=1.0).then_inc(s["f_beta"], 1)
                act.wait_ge(s["f_dec"], 2 * n - 1)
                act.activation(dec[:, p], dec[:, p], ACT.Exp, scale=negA[:, 0:1]).then_inc(s["f_dec"], 1)
                act.wait_ge(s["f_beta"], 2 * n - 1)
                act.activation(beta[:], beta[:], ACT.Exp, scale=-1.0).then_inc(s["f_beta"], 1)

            def F_act2(act, n, p):
                for ready, src, used, first, second, third, at in (
                    ((s["f_pv"], s["f_pk"]), (B_P0, B_P1), (s["f_vs"], s["f_ks"]), (s["f_ev"], s["f_ek"]), None, (s["f_sv"], s["f_sk"]), 0),
                    ((s["f_pq"], s["f_pz"]), (B_P0, B_P1), (s["f_qs"], s["f_zs"]), (s["f_eq"], s["f_ez"]), None, (s["f_sq"], s["f_sz"]), 2),
                ):
                    for i in range(2):
                        act.wait_ge(ready[i], n)
                        after(act, used[i], n - 1)
                        act.activation(sg[at + i][:], src[i][:], ACT.Exp, scale=-1.0).then_inc(first[i], 1)
                    for i in range(2):
                        act.wait_ge(first[i], 2 * n - 1)
                        act.activation(sg[at + i][:], sg[at + i][:], ACT.Ln, bias=1.0).then_inc(first[i], 1)
                    for i in range(2):
                        act.wait_ge(first[i], 2 * n)
                        act.activation(sg[at + i][:], sg[at + i][:], ACT.Exp, scale=-1.0).then_inc(third[i], 1)
                act.wait_ge(s["f_vb"], n)
                after(act, s_bc[1], (n - 2) * HD // 2)
                act.activation(vhi[:, p], vb[:], ACT.Copy).then_inc(s["f_vhi"], 1)
                act.wait_ge(s["f_ks"], n)
                after(act, s["f_nk"], n - 1)
                act.activation(sq1[:], ks[:], ACT.Square).then_inc(s["f_k2"], 1)
                act.wait_ge(s["f_qs"], n)
                after(act, s["f_nq"], n - 1)
                act.activation(sq2[:], qs[:], ACT.Square).then_inc(s["f_q2"], 1)
                act.wait_ge(s["f_nk"], n)
                after(act, s["f_kn"], n - 1)
                act.activation(rk[:], B_N[:], ACT.Ln, bias=epsc[:, 1:2]).then_inc(s["f_lk"], 1)
                act.wait_ge(s["f_nq"], n)
                after(act, s["f_qn"], n - 1)
                act.activation(rq[:], B_N[:], ACT.Ln, bias=epsc[:, 1:2]).then_inc(s["f_lq"], 1)
                act.wait_ge(s["f_lk"], n)
                act.activation(rk[:], rk[:], ACT.Exp, scale=-0.5).then_inc(s["f_rk"], 1)
                act.wait_ge(s["f_lq"], n)
                act.activation(rq[:], rq[:], ACT.Exp, scale=-0.5, bias=epsc[:, 2:3]).then_inc(s["f_rq"], 1)

            def F_pe_a(pe, n, p):
                pe.wait_ge(s["f_u"], n)
                after(pe, s["f_xlo"], n - 1)
                for c in range(C):
                    last = pe.transpose(B_T[:, c * P:(c + 1) * P], U[:, c, :], ident[:])
                last.then_inc(s["f_uT"], 1)

            def project(pe, to, hi, lo, xh, xl, first, last):
                pe.matmul(to, hi, xh, start=first, stop=False)
                pe.matmul(to, hi, xl, start=False, stop=False)
                return pe.matmul(to, lo, xh, start=False, stop=last)

            def F_pe_b(pe, n, p):
                pe.wait_ge(s["f_xhi"], n)
                pe.wait_ge(s["f_xlo"], n)
                now = slice(K - 1, K - 1 + T)
                after(pe, s["f_qs"], n - 1)
                project(pe, B_P0[:], wphi[:, 0], wplo[:, 0], xhi[:, p, now], xlo[:, p, now],
                        True, True).then_inc(s["f_pa"], 1)
                after(pe, s["f_zs"], n - 1)
                project(pe, B_P1[:], wphi[:, 1], wplo[:, 1], xhi[:, p, now], xlo[:, p, now],
                        True, True).then_inc(s["f_pb"], 1)

                def conv(to, g, done):
                    for j in range(K):
                        last = project(pe, to[:], wchi[:, j, g], wclo[:, j, g], xhi[:, p, j:j + T],
                                       xlo[:, p, j:j + T], j == 0, j == K - 1)
                    last.then_inc(done, 1)

                pe.wait_ge(s["f_ea"], n * 2)
                conv(B_P0, 2, s["f_pv"])
                pe.wait_ge(s["f_eb"], n)
                conv(B_P1, 1, s["f_pk"])
                pe.wait_ge(s["f_vs"], n)
                conv(B_P0, 0, s["f_pq"])
                pe.wait_ge(s["f_ks"], n)
                project(pe, B_P1[:], wphi[:, 2], wplo[:, 2], xhi[:, p, now], xlo[:, p, now],
                        True, True).then_inc(s["f_pz"], 1)

            def F_pe_c(pe, n, p):
                pe.wait_ge(s["f_k2"], n)
                after(pe, s["e_lo"], n - 2)
                pe.matmul(B_N[:], block[:].rearrange("p a b -> p (a b)"), sq1[:],
                          start=True, stop=True).then_inc(s["f_nk"], 1)
                pe.wait_ge(s["f_q2"], n)
                pe.wait_ge(s["f_lk"], n)
                pe.matmul(B_N[:], block[:].rearrange("p a b -> p (a b)"), sq2[:],
                          start=True, stop=True).then_inc(s["f_nq"], 1)

            BC = (B_B0, B_B1)

            def S_pe(pe, n, p):
                base = (n - 1) * HD
                pe.wait_ge(s["f_vhi"], n)
                pe.wait_ge(s["f_vlo"], n)

                def bcast(v):
                    after(pe, s_kv, base + v - 1)
                    lhs = sel[:, v].rearrange("p a b -> p (a b)")
                    pe.matmul(BC[v % 2][:], lhs, vhi[:, p], start=True, stop=False)
                    pe.matmul(BC[v % 2][:], lhs, vlo[:, p], start=False, stop=True).then_inc(s_bc[v % 2], 1)

                def reduce(v):
                    pe.wait_ge(s_qs, base + v + 1)
                    if v == 0:
                        after(pe, s["e_og"], n - 1)
                    return pe.matmul(B_O[:], red[:, v].rearrange("p a b -> p (a b)"), qS[:, v % 2],
                                     start=v == 0, stop=v == HD - 1).then_inc(s_red, 1)

                bcast(0)
                bcast(1)
                for v in range(HD):
                    if v + 2 < HD:
                        bcast(v + 2)
                    reduce(v)

            def S_dve(dve, n, p):
                base = (n - 1) * HD
                dve.wait_ge(s["f_kn"], n)
                dve.wait_ge(s["f_dec"], 2 * n)

                def product(v):
                    dve.wait_ge(s_bc[v % 2], (n - 1) * (HD // 2) + v // 2 + 1)
                    after(dve, s_scan, base + v - 1)
                    dve.tensor_tensor(kv[:, v % 2], BC[v % 2][:], kn[:, p], ALU.mult).then_inc(s_kv, 1)

                product(0)
                for v in range(HD):
                    if v + 1 < HD:
                        product(v + 1)
                    dve.wait_ge(s_kv, base + v + 1)
                    after(dve, s_qs, base + v - 1)
                    dve.tensor_tensor_scan(Sv[:, v % 2], dec[:, p], kv[:, v % 2], 0.0,
                                           ALU.mult, ALU.add).then_inc(s_scan, 1)

            def S_pool(pool, n, p):
                base = (n - 1) * HD
                pool.wait_ge(s["f_qn"], n)
                for v in range(HD):
                    pool.wait_ge(s_scan, base + v + 1)
                    after(pool, s_red, base + v - 1)
                    pool.tensor_tensor(qS[:, v % 2], Sv[:, v % 2], qn[:, p], ALU.mult).then_inc(s_qs, 1)

            def E_act_a(act, n, p):
                act.wait_ge(s_red, n * HD)
                after(act, s["e_no"], n - 1)
                act.activation(osq[:], B_O[:], ACT.Square).then_inc(s["e_o2"], 1)
                act.wait_ge(s["e_no"], n)
                after(act, s["e_og"], n - 1)
                act.activation(ro[:], B_N[:], ACT.Ln, bias=epsc[:, 1:2]).then_inc(s["e_lo"], 1)
                act.wait_ge(s["e_lo"], n)
                act.activation(ro[:], ro[:], ACT.Exp, scale=-0.5).then_inc(s["e_ro"], 1)

            def E_pe_a(pe, n, p):
                pe.wait_ge(s["e_o2"], n)
                pe.wait_ge(s["f_lq"], min(n + 1, NB) if isinstance(n, int) else n + 1)
                pe.matmul(B_N[:], blockms[:].rearrange("p a b -> p (a b)"), osq[:],
                          start=True, stop=True).then_inc(s["e_no"], 1)

            def E_dve_a(dve, n, p):
                dve.wait_ge(s["e_ro"], n)
                dve.wait_ge(s["f_zs"], n)
                after(dve, s["e_gz"], n - 1)
                dve.tensor_tensor(og[:], B_O[:], ro[:], ALU.mult).then_inc(s["e_og"], 1)
                dve.wait_ge(s["e_og"], n)
                after(dve, s["e_wo"], n - 1)
                dve.tensor_tensor(gz[:], og[:], zs[:, p], ALU.mult).then_inc(s["e_gz"], 1)

            def E_pe_b(pe, n, p):
                pe.wait_ge(s["e_gz"], n)
                after(pe, s["e_slot"], n - 1)
                for c in range(C):
                    last = pe.matmul(B_W[:, c * P:(c + 1) * P], gz[:, c * P:(c + 1) * P], woT[:],
                                     start=True, stop=True)
                last.then_inc(s["e_wo"], 1)

            def E_dve_b(dve, n, p):
                dve.wait_ge(s["e_wo"], n)
                for c in range(C):
                    dve.bn_stats(st2[:, c, :], B_W[:, c * P:(c + 1) * P]).then_inc(s["e_st2"], 1)
                after(dve, s["e_rs2"], 2 * (n - 1))
                fence(dve, s["e_st2"], n * 8 - 4)
                for c in range(C):
                    dve.bn_aggr(mv2[:, c, :], st2[:, c, :]).then_inc(s["e_st2"], 1)

            def E_act_b(act, n, p):
                act.wait_ge(s["e_st2"], n * 8)
                after(act, s["e_y"], n - 1)
                act.activation(rs2[:], mv2[:, :, 1], ACT.Ln, bias=epsc[:, 0:1]).then_inc(s["e_rs2"], 1)
                act.wait_ge(s["e_rs2"], 2 * n - 1)
                act.activation(rs2[:], rs2[:], ACT.Exp, scale=-0.5).then_inc(s["e_rs2"], 1)

            def E_dve_c(dve, n, p):
                dve.wait_ge(s["e_rs2"], 2 * n)
                after(dve, s["e_x1"], n - 1)
                for c in range(C):
                    last = dve.tensor_scalar(yn[:, c, :], B_W[:, c * P:(c + 1) * P], mv2[:, c, 0:1],
                                             rs2[:, c:c + 1], ALU.subtract, ALU.mult)
                last.then_inc(s["e_y"], 1)

            def E_pool_a(pool, n, p, b):
                pool.wait_ge(s["e_y"], n)
                at = X[:, bass.ds(b * C, C), :]
                pool.tensor_tensor(at, at, yn[:], ALU.add).then_inc(s["e_x1"], 1)

            def E_dve_d(dve, n, p, b):
                dve.wait_ge(s["e_x1"], n)
                for c in range(C):
                    dve.bn_stats(st3[:, c, :], X[:, bass.ds(b * C + c, 1), :]).then_inc(s["e_st3"], 1)
                after(dve, s["e_t"], n - 1)
                fence(dve, s["e_st3"], n * 8 - 4)
                for c in range(C):
                    dve.bn_aggr(mv3[:, c, :], st3[:, c, :]).then_inc(s["e_st3"], 1)

            def E_act_c(act, n, p, b):
                act.wait_ge(s["e_st3"], n * 8)
                after(act, s["e_t"], n - 1)
                act.activation(rs3[:], mv3[:, :, 1], ACT.Ln, bias=epsc[:, 0:1]).then_inc(s["e_rs3"], 1)
                act.wait_ge(s["e_rs3"], 2 * n - 1)
                act.activation(rs3[:], rs3[:], ACT.Exp, scale=-0.5).then_inc(s["e_rs3"], 1)
                act.wait_ge(s["e_ms"], 2 * n)
                after(act, s["e_tsc"], n - 1)
                act.activation(rr[:], ms[:], ACT.Ln, bias=epsc[:, 0:1]).then_inc(s["e_rr"], 1)
                act.wait_ge(s["e_rr"], 2 * n - 1)
                act.activation(rr[:], rr[:], ACT.Exp, scale=-0.5).then_inc(s["e_rr"], 1)

            def E_dve_e(dve, n, p, b):
                dve.wait_ge(s["e_rs3"], 2 * n)
                dve.tensor_copy(NORM3[:, bass.ds(b * C, C), 0], mv3[:, :, 0])
                dve.tensor_copy(NORM3[:, bass.ds(b * C, C), 1], rs3[:])
                after(dve, s["e_rr"], 2 * (n - 1))
                dve.tensor_tensor(ms[:], rs3[:], rs3[:], ALU.mult).then_inc(s["e_ms"], 1)
                dve.wait_ge(s["e_ms"], 2 * n - 1)
                dve.tensor_tensor(ms[:], ms[:], mv3[:, :, 1], ALU.mult).then_inc(s["e_ms"], 1)
                dve.wait_ge(s["e_rr"], 2 * n)
                after(dve, s["e_t"], n - 1)
                dve.tensor_tensor(tsc[:], rr[:], rs3[:], ALU.mult).then_inc(s["e_tsc"], 1)
                dve.wait_ge(s["e_tsc"], n)
                after(dve, s_sent[p], sent(n, p))
                after(dve, s["e_t2"], n - 1)
                for c in range(C):
                    last = dve.tensor_scalar(tr[:, p, c, 0, 0:P], X[:, bass.ds(b * C + c, 1), :],
                                             mv3[:, c, 0:1], tsc[:, c:c + 1],
                                             ALU.subtract, ALU.mult)
                last.then_inc(s["e_t"], 1)

            def E_pe_c(pe, n, p):
                pe.wait_ge(s["e_t"], n)
                pe.wait_ge(s["e_y"], n)
                for c in range(C):
                    last = pe.transpose(B_W[:, c * P:(c + 1) * P], tr[:, p, c, 0, 0:P], ident[:])
                last.then_inc(s["e_tT"], 1)
                pe.wait_ge(s["e_tTs"], n)
                for c in range(C):
                    last = pe.matmul(B_W[:, c * E:(c + 1) * E], tTs[:, c * P:(c + 1) * P], gw[:],
                                     start=True, stop=True)
                last.then_inc(s["e_lg"], 1)

            def E_act_d(act, n, p):
                act.wait_ge(s["e_tT"], n)
                after(act, s["e_lg"], n - 1)
                act.activation(tTs[:], B_W[:], ACT.Copy).then_inc(s["e_tTs"], 1)
                act.wait_ge(s["e_t"], n)
                after(act, s_sent[p], sent(n, p))
                act.activation(tr[:, p, :, 1, 0:P], tr[:, p, :, 0, 0:P], ACT.Copy).then_inc(s["e_t2"], 1)

            def E_act_e(act, n, p):
                act.wait_ge(s["e_pd"], n)
                after(act, s["e_meta"], n - 1)
                act.activation(p0[:], pd[:], ACT.Exp).then_inc(s["e_p1"], 1)

            def wide(ap):
                return ap[:].unsqueeze(2).to_broadcast([P, C, E])

            def E_dve_f(dve, n, p, b):
                link = [0]

                def then(ins):
                    link[0] += 1
                    ins.then_inc(r_chain, 1)
                    dve.wait_ge(r_chain, (n - 1) * NR + link[0])

                dve.wait_ge(s["e_lg"], n)
                after(dve, s["e_pos"], n - 1)
                then(dve.tensor_tensor(lg[:], B_W[:, 0:C * E].rearrange("p (c e) -> p c e", e=E),
                                       gb[:].unsqueeze(1).to_broadcast([P, C, E]), ALU.add))
                then(dve.tensor_reduce(m1[:], lg[:], AX.X, ALU.max))
                then(dve.tensor_tensor(eq[:], lg[:], wide(m1), ALU.is_equal))
                then(dve.tensor_tensor(eq[:], eq[:], rank[:], ALU.mult))
                then(dve.tensor_reduce(wm[:], eq[:], AX.X, ALU.max))
                then(dve.tensor_tensor(one1[:], rank[:], wide(wm), ALU.is_equal))
                then(dve.scalar_tensor_tensor(lg2[:], one1[:], -3e38, lg[:], ALU.mult, ALU.add))
                then(dve.tensor_reduce(m2[:], lg2[:], AX.X, ALU.max))
                after(dve, s["e_p1"], n - 1)
                dve.tensor_tensor(pd[:], m2[:], m1[:], ALU.subtract).then_inc(s["e_pd"], 1)
                then(dve.tensor_tensor(eq[:], lg2[:], wide(m2), ALU.is_equal))
                then(dve.tensor_tensor(eq[:], eq[:], rank[:], ALU.mult))
                then(dve.tensor_reduce(wm[:], eq[:], AX.X, ALU.max))
                then(dve.tensor_tensor(one2[:], rank[:], wide(wm), ALU.is_equal))
                dve.tensor_tensor(mask[:], one1[:], one2[:], ALU.add).then_inc(s["e_mask"], 1)
                dve.wait_ge(s["e_p1"], n)
                then(dve.tensor_scalar(m1[:], p0[:], 1.0, None, ALU.add))
                then(dve.reciprocal(m2[:], m1[:]))
                after(dve, s_sent[p], sent(n, p))
                dve.tensor_copy(tr[:, p, :, 0, P], m2[:])
                dve.tensor_tensor(tr[:, p, :, 1, P], m2[:], p0[:], ALU.mult)
                then(dve.tensor_copy(tr[:, p, :, :, P + 1], dest[:]))
                then(dve.tensor_scalar(dest[:], dest[:], float(T), None, ALU.add))
                dve.wait_ge(s["e_pos"], n)
                then(dve.tensor_tensor(place[:], B_W[:, 64:64 + C * E].rearrange("p (c e) -> p c e", e=E),
                                       count[:].unsqueeze(1).to_broadcast([P, C, E]), ALU.add))
                dve.tensor_tensor(count[:], count[:], B_W[:, 128:128 + E], ALU.add).then_inc(s["e_slot"], 1)
                dve.tensor_tensor(one1[:], one1[:], place[:], ALU.mult)
                then(dve.tensor_tensor(one2[:], one2[:], place[:], ALU.mult))
                dve.tensor_reduce(slotf[:, :, 0], one1[:], AX.X, ALU.add)
                then(dve.tensor_reduce(slotf[:, :, 1], one2[:], AX.X, ALU.add))
                dve.tensor_copy(slot[:, p], slotf[:]).then_inc(s["e_meta"], 1)
                assert link[0] == NR, link[0]

            def E_pe_d(pe, n, p):
                pe.wait_ge(s["e_mask"], n)
                flat = mask[:].rearrange("p c e -> p (c e)")
                at = B_W[:, 64:64 + C * E]
                pe.matmul(at, tri[:], flat, start=True, stop=True, skip_group_check=True)
                for c in range(1, C):
                    pe.matmul(at[:, c * E:], ones_b[:], flat[:, 0:(C - c) * E],
                              start=False, stop=True, skip_group_check=True)
                for c in range(C):
                    last = pe.matmul(B_W[:, 128:128 + E], ones_b[:], mask[:, c], start=False, stop=True,
                                     skip_group_check=True)
                last.then_inc(s["e_pos"], 1)

            def E_pool_b(pool, n, p):
                pool.wait_ge(s["e_meta"], n)
                fence(pool, s["e_t2"], n)
                for c in range(C):
                    for k in range(TOP):
                        pool.indirect_dma_start(
                            rows, bass.IndirectOffsetOnAxis(ap=slot[:, p, c, k:k + 1], axis=0),
                            tr[:, p, c, k, :], None).then_inc(s_sent[p], 16)

            def iterations(eng, step):
                step(-1, True, False, False, 1)
                step(0, True, True, False, 0)
                step(1, True, True, True, 1)
                step(2, True, True, True, 0)
                with eng.Fori(1, NB // 2 - 1) as i:
                    kk = 2 * i + 1
                    step(kk, True, True, True, 1)
                    step(kk + 1, True, True, True, 0)
                step(NB - 1, False, True, True, 1)
                step(NB, False, False, True, 0)

            epsc = st("epsc", [P, 3])
            s_eps = s["const_pool"]

            with nc.Block() as blk:
                @blk.vector
                def _(dve):
                    for i, value in enumerate((EPS_LN, EPS_L2, -0.5 * 2.0794415416798357)):
                        dve.memset(epsc[:, i:i + 1], value)
                    dve.tensor_tensor(count[:], count[:], region0[:], ALU.add)
                    dve.tensor_copy(dest[:], token[:])
                    dve.memset(xhi[:, :, 0:K - 1], 0.0)
                    dve.memset(xlo[:, :, 0:K - 1], 0.0).then_inc(s_eps, 1)
                    dve.wait_ge(s_eps, 4)

                    def step(k, f, sc, e, par):
                        if e:
                            E_dve_a(dve, k, 1 - par)
                            E_dve_b(dve, k, 1 - par)
                        if f:
                            F_dve_a(dve, k + 2, 1 - par, k + 1)
                            F_dve_b(dve, k + 2, 1 - par, k + 1)
                        if e:
                            E_dve_c(dve, k, 1 - par)
                            E_dve_d(dve, k, 1 - par, k - 1)
                        if f:
                            F_dve_c(dve, k + 2, 1 - par)
                        if sc:
                            S_dve(dve, k + 1, par)
                        if e:
                            E_dve_e(dve, k, 1 - par, k - 1)
                            E_dve_f(dve, k, 1 - par, k - 1)
                        if f:
                            F_dve_d(dve, k + 2, 1 - par)

                    iterations(dve, step)

                @blk.scalar
                def _(act):
                    act.wait_ge(s_eps, 4)

                    def step(k, f, sc, e, par):
                        if e:
                            E_act_a(act, k, 1 - par)
                            E_act_b(act, k, 1 - par)
                        if f:
                            F_act(act, k + 2, 1 - par)
                        if e:
                            E_act_c(act, k, 1 - par, k - 1)
                            E_act_d(act, k, 1 - par)
                            E_act_e(act, k, 1 - par)
                        if f:
                            F_act_b(act, k + 2, 1 - par)
                            F_act2(act, k + 2, 1 - par)

                    iterations(act, step)

                @blk.tensor
                def _(pe):
                    pe.wait_ge(s_eps, 4)

                    def step(k, f, sc, e, par):
                        if e:
                            E_pe_a(pe, k, 1 - par)
                            E_pe_b(pe, k, 1 - par)
                        if f:
                            F_pe_a(pe, k + 2, 1 - par)
                        if sc:
                            S_pe(pe, k + 1, par)
                        if e:
                            E_pe_c(pe, k, 1 - par)
                            E_pe_d(pe, k, 1 - par)
                        if f:
                            F_pe_b(pe, k + 2, 1 - par)
                            F_pe_c(pe, k + 2, 1 - par)

                    iterations(pe, step)

                @blk.gpsimd
                def _(pool):
                    def step(k, f, sc, e, par):
                        if e:
                            E_pool_a(pool, k, 1 - par, k - 1)
                        if sc:
                            S_pool(pool, k + 1, par)
                        if e:
                            E_pool_b(pool, k, 1 - par)

                    iterations(pool, step)
                    for p in range(2):
                        pool.wait_ge(s_sent[p], 16 * C * TOP * NB // 2)

        tab = sb("tab", [P, TILES, 2], I32)
        with ExitStack() as stage:
            def st(name, shape, dt=F32):
                return stage.enter_context(nc.sbuf_tensor(name, shape, dt))

            cnt, tiles_of, ends, one = (st(n, [P, E]) for n in ("cnt", "tiles_of", "ends", "one"))
            jt = st("jt", [P, E, NT])
            over = st("over", [P, E, NT])
            tj = st("tj", [P, TILES, E])
            le = st("le", [P, TILES, E])
            te, first, tnum, start = (st(n, [P, TILES]) for n in ("te", "first", "tnum", "start"))
            pnum = st("pnum", [P, 1])
            padrow = st("padrow", [P, W])
            padat = st("padat", [P, E], I32)
            t_const, t_chain, t_pad = sem("t_const"), sem("t_chain"), sem("t_pad")

            with nc.Block() as blk:
                @blk.gpsimd
                def _(pool):
                    pool.iota(jt[:], pattern=[[0, E], [P, NT]], base=0, channel_multiplier=0,
                              allow_small_or_imprecise_dtypes=True).then_inc(t_const, 1)
                    pool.iota(tj[:], pattern=[[1, TILES], [0, E]], base=0, channel_multiplier=0,
                              allow_small_or_imprecise_dtypes=True).then_inc(t_const, 1)
                    pool.iota(tnum[:], pattern=[[1, TILES]], base=0, channel_multiplier=0,
                              allow_small_or_imprecise_dtypes=True).then_inc(t_const, 1)
                    pool.iota(pnum[:], pattern=[[0, 1]], base=0, channel_multiplier=1,
                              allow_small_or_imprecise_dtypes=True).then_inc(t_const, 1)
                    pool.memset(one[:], 1.0).then_inc(t_const, 1)
                    pool.memset(padrow[:, 0:P + 1], 0.0)
                    pool.memset(padrow[:, P + 1:W], FAR).then_inc(t_const, 1)
                    pool.wait_ge(t_const, 6)
                    pool.wait_ge(t_chain, 1)
                    for e in range(E):
                        pool.indirect_dma_start(
                            rows, bass.IndirectOffsetOnAxis(ap=padat[:, e:e + 1], axis=0),
                            padrow[:], None).then_inc(t_pad, 16)
                    pool.wait_ge(t_pad, 16 * E)

                @blk.vector
                def _(dve):
                    link = [0]

                    def then(ins):
                        link[0] += 1
                        ins.then_inc(t_chain, 1)
                        dve.wait_ge(t_chain, link[0])

                    dve.wait_ge(t_const, 6)
                    then(dve.tensor_scalar(padat[:], count[:], pnum[:, 0:1], None, ALU.add))
                    then(dve.tensor_tensor(cnt[:], count[:], region0[:], ALU.subtract))
                    then(dve.tensor_tensor(over[:], cnt[:].unsqueeze(2).to_broadcast([P, E, NT]), jt[:], ALU.is_gt))
                    then(dve.tensor_reduce(tiles_of[:], over[:], AX.X, ALU.add))
                    then(dve.tensor_tensor_scan(ends[:], one[:], tiles_of[:], 0.0, ALU.mult, ALU.add))
                    ends_b = ends[:].unsqueeze(1).to_broadcast([P, TILES, E])
                    then(dve.tensor_tensor(le[:], ends_b, tj[:], ALU.is_le))
                    then(dve.tensor_reduce(te[:], le[:], AX.X, ALU.add))
                    then(dve.tensor_tensor(le[:], le[:], ends_b, ALU.mult))
                    then(dve.tensor_reduce(first[:], le[:], AX.X, ALU.max))
                    then(dve.tensor_tensor(first[:], tnum[:], first[:], ALU.subtract))
                    then(dve.tensor_scalar(first[:], first[:], float(P), None, ALU.mult))
                    then(dve.tensor_scalar(start[:], te[:], float(REGION), None, ALU.mult))
                    then(dve.tensor_tensor(tab[:, :, 0], start[:], first[:], ALU.add))
                    then(dve.tensor_scalar(tab[:, :, 1], te[:], float(E - 1), None, ALU.min))

        with ExitStack() as stage:
            def st(name, shape, dt=F32):
                return stage.enter_context(nc.sbuf_tensor(name, shape, dt))

            RING = 4
            G = st("G", [P, RING, W])
            thi, tlo = st("thi", [P, 2, P], F16), st("tlo", [P, 2, P], F16)
            gate, lin, sig, hid = (st(n, [P, 2, HID]) for n in ("gate", "lin", "sig", "hid"))
            hhi, hlo = st("hhi", [P, 2, 2 * P], F16), st("hlo", [P, 2, 2 * P], F16)
            yw = st("yw", [P, RING, P])
            where = st("where", [P, RING], I32)
            m = sems("m_in0 m_in1 m_in2 m_in3 m_T m_hi m_lo m_h m_gate m_lin m_e1 m_e2 m_sig m_gs m_hid "
                     "m_hT m_hhi m_hlo m_y m_yw m_where m_out0 m_out1 m_out2 m_out3")
            m_in = (m["m_in0"], m["m_in1"], m["m_in2"], m["m_in3"])
            m_out = (m["m_out0"], m["m_out1"], m["m_out2"], m["m_out3"])
            B_H, B_HT, B_Y = (bank[1], bank[2]), (bank[3], bank[4]), (bank[5], bank[6])

            def tiles(eng, step):
                step(-1, True, False, False, 3)
                step(0, True, True, False, 0)
                for k in range(1, 4):
                    step(k, True, True, True, k)
                with eng.Fori(1, TILES // 4 - 1) as r:
                    for i in range(4):
                        step(4 * r + i, True, True, True, i)
                for k in range(TILES - 4, TILES - 1):
                    step(k, True, True, True, k % 4)
                step(TILES - 1, False, True, True, 3)
                step(TILES, False, False, True, 0)

            def filled(n, q):
                return 4 * (n - 1 - q) + 16

            with nc.Block() as blk:
                @blk.sync
                def _(sp):
                    def load(j, q):
                        if not (isinstance(j, int) and j < RING):
                            sp.wait_ge(m["m_T"], j - RING + 1)
                            sp.wait_ge(m["m_yw"], j - RING + 1)
                            sp.wait_ge(m["m_where"], j - RING + 1)
                        at = sp.value_load(tab[0:1, bass.ds(j, 1), 0:1], min_val=0,
                                           max_val=E * REGION + (SPARE - 1) * P)
                        sp.dma_start(G[:, q, :], rows[bass.ds(at, P), :]).then_inc(m_in[q], 16)

                    for j in range(4):
                        load(j, j)
                    with sp.Fori(1, TILES // 4) as r:
                        for i in range(4):
                            load(4 * r + i, i)

                @blk.tensor
                def _(pe):
                    def transposes(n, q):
                        p = q % 2
                        pe.wait_ge(m_in[q], filled(n, q))
                        after(pe, m["m_lo"], n - 1)
                        pe.transpose(bank[0][:, 0:P], G[:, q, 0:P], ident[:]).then_inc(m["m_T"], 1)

                    def first_product(n, q):
                        p = q % 2
                        e = pe.value_load(tab[0:1, bass.ds(n - 1, 1), 1:2], min_val=0, max_val=E - 1)
                        pe.wait_ge(m["m_lo"], n)
                        pe.wait_ge(m["m_hi"], n)
                        after(pe, m["m_lin"], n - 2)
                        to = B_H[p][:]
                        w_hi = w1hi[:, bass.ds(e, 1), :].rearrange("p a f -> p (a f)")
                        w_lo = w1lo[:, bass.ds(e, 1), :].rearrange("p a f -> p (a f)")
                        bias = b1p[:, bass.ds(e, 1), :].rearrange("p a f -> p (a f)")
                        pe.matmul(to, ones16[:], bias, start=True, stop=False)
                        pe.matmul(to, thi[:, p], w_hi, start=False, stop=False)
                        pe.matmul(to, thi[:, p], w_lo, start=False, stop=False)
                        pe.matmul(to, tlo[:, p], w_hi, start=False, stop=True).then_inc(m["m_h"], 1)

                    def second_product(n, q):
                        p = q % 2
                        e = pe.value_load(tab[0:1, bass.ds(n - 1, 1), 1:2], min_val=0, max_val=E - 1)
                        pe.wait_ge(m["m_hid"], n)
                        after(pe, m["m_hlo"], n - 2)
                        pe.transpose(B_HT[p][:, 0:P], hid[:, p, 0:P], ident[:])
                        pe.transpose(B_HT[p][:, P:2 * P], hid[:, p, P:2 * P], ident[:]).then_inc(m["m_hT"], 1)
                        to = B_Y[p][:, 0:P]
                        after(pe, m["m_yw"], n - 2)
                        pe.matmul(to, ones16[:], b2p[:, bass.ds(e, 1), :].rearrange("p a f -> p (a f)"),
                                  start=True, stop=False)
                        pe.wait_ge(m["m_hhi"], n)
                        pe.wait_ge(m["m_hlo"], n)
                        for c in range(2):
                            hi, lo = hhi[:, p, c * P:(c + 1) * P], hlo[:, p, c * P:(c + 1) * P]
                            w_hi = w2hi[:, bass.ds(e, 1), c, :].rearrange("p a f -> p (a f)")
                            w_lo = w2lo[:, bass.ds(e, 1), c, :].rearrange("p a f -> p (a f)")
                            pe.matmul(to, hi, w_hi, start=False, stop=False)
                            pe.matmul(to, hi, w_lo, start=False, stop=False)
                            last = pe.matmul(to, lo, w_hi, start=False, stop=c == 1)
                        last.then_inc(m["m_y"], 1)

                    def step(k, a, b, c, q):
                        if a:
                            transposes(k + 2, (q + 1) % 4)
                        if b:
                            first_product(k + 1, q)
                        if c:
                            second_product(k, (q + 3) % 4)

                    tiles(pe, step)

                @blk.vector
                def _(dve):
                    def step(k, a, b, c, q):
                        p = q % 2
                        if b:
                            n = k + 1
                            dve.wait_ge(m["m_h"], n)
                            after(dve, m["m_gs"], n - 2)
                            dve.tensor_scalar(gate[:, p], B_H[p][:, 0:HID], LIMIT, GUARD, ALU.min,
                                              ALU.max).then_inc(m["m_gate"], 1)
                            after(dve, m["m_hid"], n - 2)
                            dve.tensor_scalar(lin[:, p], B_H[p][:, HID:], LIMIT, -LIMIT, ALU.min,
                                              ALU.max).then_inc(m["m_lin"], 1)
                        if c:
                            n = k
                            dve.wait_ge(m["m_hhi"], n)
                            dve.tensor_tensor(hlo[:, 1 - p], B_HT[1 - p][:, 0:HID], hhi[:, 1 - p],
                                              ALU.subtract).then_inc(m["m_hlo"], 1)
                        if a:
                            n = k + 2
                            dve.wait_ge(m["m_hi"], n)
                            after(dve, m["m_h"], n - 2)
                            dve.tensor_tensor(tlo[:, 1 - p], bank[0][:, 0:P], thi[:, 1 - p],
                                              ALU.subtract).then_inc(m["m_lo"], 1)
                        if b:
                            n = k + 1
                            dve.wait_ge(m["m_gs"], n)
                            dve.wait_ge(m["m_lin"], n)
                            after(dve, m["m_hT"], n - 2)
                            dve.scalar_tensor_tensor(hid[:, p], lin[:, p], 1.0, sig[:, p], ALU.add,
                                                     ALU.mult).then_inc(m["m_hid"], 1)

                    tiles(dve, step)

                @blk.scalar
                def _(act):
                    def step(k, a, b, c, q):
                        p = q % 2
                        n = k + 1
                        if b:
                            act.wait_ge(m["m_gate"], n)
                            after(act, m["m_hid"], n - 2)
                            act.activation(sig[:, p], gate[:, p], ACT.Exp, scale=-ALPHA).then_inc(m["m_e1"], 1)
                        if a:
                            act.wait_ge(m["m_T"], n + 1)
                            after(act, m["m_h"], n - 1)
                            act.activation(thi[:, 1 - p], bank[0][:, 0:P], ACT.Copy).then_inc(m["m_hi"], 1)
                        if b:
                            act.wait_ge(m["m_e1"], n)
                            act.activation(sig[:, p], sig[:, p], ACT.Ln, bias=1.0).then_inc(m["m_e2"], 1)
                        if c:
                            act.wait_ge(m["m_hT"], n - 1)
                            after(act, m["m_y"], n - 3)
                            act.activation(hhi[:, 1 - p], B_HT[1 - p][:, 0:HID], ACT.Copy).then_inc(m["m_hhi"], 1)
                        if b:
                            act.wait_ge(m["m_e2"], n)
                            act.activation(sig[:, p], sig[:, p], ACT.Exp, scale=-1.0).then_inc(m["m_sig"], 1)
                        if c:
                            act.wait_ge(m["m_y"], n - 1)
                            qc = (q + 3) % 4
                            if not (isinstance(k, int) and k <= RING):
                                act.wait_ge(m_out[qc], filled(k, qc) - 16)
                            act.activation(yw[:, qc], B_Y[1 - p][:, 0:P], ACT.Copy,
                                           scale=G[:, qc, P:P + 1]).then_inc(m["m_yw"], 1)

                    tiles(act, step)

                @blk.gpsimd
                def _(pool):
                    def step(k, a, b, c, q):
                        p = q % 2
                        if b:
                            n = k + 1
                            pool.wait_ge(m["m_sig"], n)
                            pool.tensor_tensor(sig[:, p], gate[:, p], sig[:, p], ALU.mult).then_inc(m["m_gs"], 1)
                            fence(pool, m_in[q], filled(n, q))
                            fence(pool, m_out[q], filled(n, q) - 16)
                            pool.tensor_copy(where[:, q:q + 1], G[:, q, P + 1:W]).then_inc(m["m_where"], 1)
                        if c:
                            qc = (q + 3) % 4
                            pool.wait_ge(m["m_yw"], k)
                            fence(pool, m["m_where"], k)
                            pool.indirect_dma_start(
                                results, bass.IndirectOffsetOnAxis(ap=where[:, qc:qc + 1], axis=0),
                                yw[:, qc], None, bounds_check=TOP * N - 1,
                                oob_is_err=False).then_inc(m_out[qc], 16)

                    tiles(pool, step)
                    for q in range(4):
                        pool.wait_ge(m_out[q], 16 * (TILES // RING))

        with ExitStack() as stage:
            def st(name, shape, dt=F32):
                return stage.enter_context(nc.sbuf_tensor(name, shape, dt))

            Y = st("Y", [P, 2, TOP, C, P])
            U4, Z4, O4 = st("U4", [P, 2, C, P]), st("Z4", [P, 2, C, P]), st("O4", [P, 2, C, P])
            st4, mv4, rs4 = st("st4", [P, C, 6]), st("mv4", [P, C, 2]), st("rs4", [P, C])
            o = sems("o_sum o_u o_z o_st o_mv o_ln o_rs o_n o_x o_const")
            o_in, o_out = (sem("o_in0"), sem("o_in1")), (sem("o_out0"), sem("o_out1"))
            eps4 = st("eps4", [P, 1])

            def both(eng, step):
                step(0, 0)
                step(1, 1)
                with eng.Fori(1, NB // 2) as r:
                    for i in range(2):
                        step(2 * r + i, i)

            with nc.Block() as blk:
                @blk.sync
                def _(sp):
                    def step(b, p):
                        after(sp, o["o_z"], b - 1)
                        for k in range(TOP):
                            sp.dma_start(Y[:, p, k], rv[:, k, bass.ds(b * C, C), :]).then_inc(o_in[p], 16)

                    both(sp, step)

                @blk.gpsimd
                def _(pool):
                    def step(b, p):
                        pool.wait_ge(o_in[p], 16 * b - 16 * p + 32)
                        pool.tensor_tensor(Y[:, p, 0], Y[:, p, 0], Y[:, p, 1], ALU.add).then_inc(o["o_sum"], 1)

                    both(pool, step)

                @blk.vector
                def _(dve):
                    dve.memset(eps4[:], EPS_LN).then_inc(o["o_const"], 1)

                    def step(b, p):
                        n = b + 1
                        after(dve, o["o_z"], n - 2)
                        for c in range(C):
                            last = dve.tensor_scalar(U4[:, p, c], X[:, bass.ds(b * C + c, 1), :],
                                                     NORM3[:, bass.ds(b * C + c, 1), 0],
                                                     NORM3[:, bass.ds(b * C + c, 1), 1],
                                                     ALU.subtract, ALU.mult)
                        last.then_inc(o["o_u"], 1)
                        dve.wait_ge(o["o_u"], n)
                        dve.wait_ge(o["o_sum"], n)
                        after(dve, o["o_n"], n - 2)
                        dve.tensor_tensor(Z4[:, p], U4[:, p], Y[:, p, 0], ALU.add).then_inc(o["o_z"], 1)
                        dve.wait_ge(o["o_z"], n)
                        after(dve, o["o_mv"], n - 1)
                        for c in range(C):
                            last = dve.bn_stats(st4[:, c], Z4[:, p, c])
                        last.then_inc(o["o_st"], 1)
                        after(dve, o["o_ln"], n - 1)
                        after(dve, o["o_n"], n - 1)
                        fence(dve, o["o_st"], n)
                        for c in range(C):
                            last = dve.bn_aggr(mv4[:, c], st4[:, c])
                        last.then_inc(o["o_mv"], 1)
                        dve.wait_ge(o["o_rs"], n)
                        after(dve, o["o_x"], n - 2)
                        for c in range(C):
                            last = dve.tensor_scalar(U4[:, p, c], Z4[:, p, c], mv4[:, c, 0:1], rs4[:, c:c + 1],
                                                     ALU.subtract, ALU.mult)
                        last.then_inc(o["o_n"], 1)
                        dve.wait_ge(o["o_n"], n)
                        after(dve, o_out[p], 16 * (b - p) // 2 if isinstance(b, int) else 8 * b - 8 * p)
                        dve.tensor_tensor(O4[:, p], X[:, bass.ds(b * C, C), :], U4[:, p], ALU.add).then_inc(o["o_x"], 1)

                    both(dve, step)

                @blk.scalar
                def _(act):
                    act.wait_ge(o["o_const"], 1)

                    def step(b, p):
                        n = b + 1
                        act.wait_ge(o["o_mv"], n)
                        after(act, o["o_n"], n - 1)
                        act.activation(rs4[:], mv4[:, :, 1], ACT.Ln, bias=eps4[:, 0:1]).then_inc(o["o_ln"], 1)
                        act.wait_ge(o["o_ln"], n)
                        act.activation(rs4[:], rs4[:], ACT.Exp, scale=-0.5).then_inc(o["o_rs"], 1)
                        act.wait_ge(o["o_x"], n)
                        act.dma_start(ov[:, bass.ds(b * C, C), :], O4[:, p]).then_inc(o_out[p], 16)

                    both(act, step)
                    for p in range(2):
                        act.wait_ge(o_out[p], 16 * (NB // 2))


_INS = ["L0_attn_x", "L0_attn_W_qkv", "L0_attn_conv_w", "L0_attn_W_z", "L0_attn_W_b", "L0_attn_W_a",
        "L0_attn_dt_bias", "L0_attn_A_log", "L0_attn_W_out", "L0_ffn_norm_scale", "L0_ffn_gate_w",
        "L0_ffn_gate_b", "L0_ffn_mlp1_w", "L0_ffn_mlp1_b", "L0_ffn_mlp2_w", "L0_ffn_mlp2_b"]


def kernel(**inputs):
    import numpy as _np
    import concourse.bacc as _bacc
    from concourse import mybir as _mybir
    from concourse.bass_utils import run_bass_kernel_spmd as _run

    nc = _bacc.Bacc("TRN2", target_bir_lowering=False, num_devices=1)
    arrays, args = {}, []
    for name in _INS:
        a = _np.ascontiguousarray(inputs[name])
        arrays[f"in_{name}_dram"] = a
        args.append(nc.dram_tensor(f"in_{name}_dram", a.shape, _mybir.dt.from_np(a.dtype), kind="ExternalInput").ap())
    shape = inputs["L0_attn_x"].shape
    args.append(nc.dram_tensor("out_0_dram", shape, _mybir.dt.float32, kind="ExternalOutput").ap())
    build_program(nc, *args)
    r = _run(nc, [arrays], core_ids=[0])
    return r.results[0]["out_0_dram"]
```

```python
from contextlib import ExitStack

import concourse.bass as bass
from concourse import mybir

F32 = mybir.dt.float32
F16 = mybir.dt.float16
BF16 = mybir.dt.bfloat16
I32 = mybir.dt.int32
ALU = mybir.AluOpType
ACT = mybir.ActivationFunctionType
AX = mybir.AxisListType

P = 128
EPS_LN = 1e-5
EPS_L2 = 1e-6
EPS_MS = 1e-6
EPS_RMS = 1e-5
LIMIT = 7.0
ALPHA = 1.702
GUARD = -25.0
FAR = float(1 << 20)


def build_program(nc, x, W_qkv, conv_w, W_z, W_b, W_a, dt_bias, A_log, W_out,
                  norm_scale, gate_w, gate_b, mlp1_w, mlp1_b, mlp2_w, mlp2_b, out):
    NB, T, D = x.shape
    H = W_a.shape[0]
    HD = D // H
    K = conv_w.shape[2]
    E = mlp1_w.shape[0]
    HID = mlp2_w.shape[1]
    C = T // P
    N = NB * T
    NT = N // P
    TOP = 2
    W = P + 2
    REGION = N + P
    TILES = (TOP * N + E * (P - 1)) // P + 1
    TILES += TILES % 2
    SPARE = TILES - TOP * NT
    assert D == P and T == 512 and HD == 8 and K == 4 and 2 * HID == 512 and NB % 2 == 0

    rows = nc.dram_tensor("routed_rows", [E * REGION + SPARE * P, W], F32, kind="Internal").ap()
    results = nc.dram_tensor("expert_results", [TOP * N, P], F32, kind="Internal").ap()

    xv = x.rearrange("b (c p) d -> p (b c) d", p=P)
    ov = out.rearrange("b (c p) d -> p (b c) d", p=P)
    rv = results.rearrange("(k n p) d -> p k n d", k=TOP, p=P)

    with ExitStack() as ctx:
        def sb(name, shape, dt=F32):
            return ctx.enter_context(nc.sbuf_tensor(name, shape, dt))

        def sem(name):
            return ctx.enter_context(nc.semaphore(name))

        def sems(names):
            return {n: sem(n) for n in names.split()}

        bank = [ctx.enter_context(nc.psum_tensor(f"bank{i}", [P, 512], F32)) for i in range(8)]
        B_T, B_P0, B_P1, B_N, B_B0, B_B1, B_O, B_W = bank

        X = sb("X", [P, NT, P])
        NORM3 = sb("NORM3", [P, NT, 2])
        w1hi = sb("w1hi", [P, E, 512], F16)
        w1lo = sb("w1lo", [P, E, 512], F16)
        w2hi = sb("w2hi", [P, E, 2, P], F16)
        w2lo = sb("w2lo", [P, E, 2, P], F16)
        b1p = sb("b1p", [P, E, 512], F16)
        b2p = sb("b2p", [P, E, P], F16)
        ones16 = sb("ones16", [P, P], F16)
        ident = sb("ident", [P, P])
        wchi = sb("wchi", [P, K, 3, P], F16)
        wclo = sb("wclo", [P, K, 3, P], F16)
        wphi = sb("wphi", [P, 3, P], F16)
        wplo = sb("wplo", [P, 3, P], F16)
        woT = sb("woT", [P, P])
        gw = sb("gw", [P, E])
        gb = sb("gb", [P, E])
        block = sb("block", [P, H, HD])
        blockms = sb("blockms", [P, H, HD])
        sel = sb("sel", [P, HD, H, HD], F16)
        red = sb("red", [P, HD, H, HD])
        rep = sb("rep", [H, H, HD])
        hb = sb("hb", [P, 2])
        negA = sb("negA", [P, 1])
        tri = sb("tri", [P, P], BF16)
        ones_b = sb("ones_b", [P, P], BF16)
        rank = sb("rank", [P, C, E])
        region0 = sb("region0", [P, E])
        token = sb("token", [P, C, TOP])
        count = sb("count", [P, E])

        s = sems(
            "x_in w_in const_pool setup_pe setup_act setup_dve wstage bias_row "
            "f_stats f_rstd f_u f_uT f_xhi f_xlo f_pa f_pb f_pv f_pk f_pq f_pz "
            "f_ea f_dec f_eb f_beta f_ev f_sv f_ek f_sk f_eq f_sq f_ez f_sz f_vs f_vb f_ks f_qs f_zs "
            "f_vhi f_vlo f_k2 f_q2 f_nk f_nq f_lk f_lq f_rk f_rq f_kn f_qn "
            "e_o2 e_no e_lo e_ro e_og e_gz e_wo e_st2 e_rs2 e_y e_x1 e_st3 e_rs3 e_ms e_rr e_tsc e_t e_t2 "
            "e_tT e_tTs e_lg e_top e_pd e_p1 e_mask e_pos e_slot e_meta "
        )
        s_bc = [sem(f"s_bc{v}") for v in range(2)]
        s_kv, s_scan, s_qs, s_red = sem("s_kv"), sem("s_scan"), sem("s_qs"), sem("s_red")
        r_chain = sem("r_chain")
        s_sent = [sem(f"s_sent{p}") for p in range(2)]
        passed = sem("passed")

        def sent(n, p):
            return 8 * C * TOP * (n - 1 - p)

        def fence(eng, semaphore, n):
            if isinstance(n, int) and n <= 0:
                return
            eng.wait_ge(semaphore, n)
            eng.sem_inc(passed, 1)

        def after(eng, semaphore, n):
            if isinstance(n, int) and n <= 0:
                return
            eng.wait_ge(semaphore, n)

        with ExitStack() as stage:
            def st(name, shape, dt=F32):
                return stage.enter_context(nc.sbuf_tensor(name, shape, dt))

            wq = st("wq", [P, 3, P])
            cw = st("cw", [P, 3, K])
            wt = st("wt", [P, K, 3, P])
            wz = st("wz", [P, P])
            wo = st("wo", [P, P])
            wab = st("wab", [H, 2, P])
            hb0 = st("hb0", [H, 2])
            ns = st("ns", [P, 1])
            gw0 = st("gw0", [P, E])
            w1 = st("w1", [P, E, 512])
            w2 = st("w2", [P, E, 2, P])
            b1 = st("b1", [1, E, 512])
            b2 = st("b2", [1, E, P])
            b1l = st("b1l", [1, E, 512], F16)
            b2l = st("b2l", [1, E, P], F16)
            pad = st("pad", [P, W])

            with nc.Block() as blk:
                @blk.sync
                def _(sp):
                    loads = [
                        (wq[:], W_qkv.rearrange("(g p) d -> p g d", p=P)),
                        (cw[:], conv_w.rearrange("(g p) o k -> p g (o k)", p=P)),
                        (wz[:], W_z), (wo[:], W_out), (wab[:, 0, :], W_a), (wab[:, 1, :], W_b),
                        (hb0[:, 0:1], dt_bias.rearrange("(h a) -> h a", a=1)),
                        (hb0[:, 1:2], A_log.rearrange("(h a) -> h a", a=1)),
                        (ns[:], norm_scale.rearrange("(d a) -> d a", a=1)),
                        (gw0[:], gate_w), (gb[:], gate_b.rearrange("(a e) -> a e", a=1).to_broadcast([P, E])),
                        (w1[:], mlp1_w.rearrange("e d f -> d e f")),
                        (w2[:], mlp2_w.rearrange("e (c p) d -> p e c d", p=P)),
                        (b1[:], mlp1_b.rearrange("(a e) f -> a e f", a=1)),
                        (b2[:], mlp2_b.rearrange("(a e) f -> a e f", a=1)),
                    ]
                    assert len(loads) == 15
                    for to, of in loads:
                        sp.dma_start(to, of).then_inc(s["w_in"], 16)
                    for q in range(4):
                        a, b = q * NT // 4, (q + 1) * NT // 4
                        sp.dma_start(X[:, a:b, :], xv[:, a:b, :]).then_inc(s["x_in"], 16)
                    sp.wait_ge(s["setup_dve"], 3)
                    sp.dma_start(b1p[1:2], b1l[:]).then_inc(s["bias_row"], 16)
                    sp.dma_start(b2p[1:2], b2l[:]).then_inc(s["bias_row"], 16)
                    sp.wait_ge(s["const_pool"], 2)
                    for n in range(SPARE):
                        a = E * REGION + n * P
                        sp.dma_start(rows[a:a + P, :], pad[:]).then_inc(s["bias_row"], 16)
                    sp.wait_ge(s["bias_row"], 16 * (2 + SPARE))
                    sp.wait_ge(s["w_in"], 16 * len(loads))
                    sp.wait_ge(s["x_in"], 64)

                @blk.gpsimd
                def _(pool):
                    n = 0

                    def step(ins):
                        nonlocal n
                        n += 1
                        ins.then_inc(s["wstage"], 1)

                    step(pool.memset(pad[:], 0.0))
                    pool.wait_ge(s["wstage"], n)
                    pool.memset(pad[:, P + 1:P + 2], FAR).then_inc(s["const_pool"], 2)
                    step(pool.memset(ident[:], 0.0))
                    step(pool.memset(block[:], 1.0))
                    step(pool.memset(sel[:], 0.0))
                    step(pool.memset(red[:], 0.0))
                    step(pool.memset(rep[:], 1.0))
                    step(pool.memset(ones_b[:], 1.0))
                    step(pool.memset(tri[:], 1.0))
                    step(pool.memset(ones16[:], 1.0))
                    step(pool.memset(b1p[:], 0.0))
                    step(pool.memset(b2p[:], 0.0))
                    step(pool.memset(count[:], 0.0))
                    pool.wait_ge(s["wstage"], n)
                    step(pool.affine_select(out=ident[:], in_=ident[:], compare_op=ALU.not_equal, fill=1.0,
                                            base=0, pattern=[[-1, P]], channel_multiplier=1))
                    step(pool.affine_select(out=block[:], in_=block[:], compare_op=ALU.is_ge, fill=0.0,
                                            base=0, pattern=[[-HD, H], [0, HD]], channel_multiplier=1))
                    step(pool.affine_select(out=rep[:], in_=rep[:], compare_op=ALU.is_equal, fill=0.0,
                                            base=0, pattern=[[-1, H], [0, HD]], channel_multiplier=1))
                    step(pool.affine_select(out=tri[:], in_=tri[:], compare_op=ALU.is_gt, fill=0.0,
                                            base=0, pattern=[[1, P]], channel_multiplier=-1))
                    for v in range(HD):
                        step(pool.affine_select(out=sel[:, v], in_=sel[:, v], compare_op=ALU.not_equal, fill=1.0,
                                                base=-v, pattern=[[-HD, H], [0, HD]], channel_multiplier=1))
                    step(pool.iota(rank[:], pattern=[[0, C], [-1, E]], base=E, channel_multiplier=0,
                                   allow_small_or_imprecise_dtypes=True))
                    for e in range(E):
                        step(pool.memset(region0[:, e:e + 1], float(e * REGION)))
                    for k in range(TOP):
                        step(pool.iota(token[:, :, k:k + 1], pattern=[[P, C], [0, 1]], base=k * N,
                                       channel_multiplier=1, allow_small_or_imprecise_dtypes=True))
                    pool.wait_ge(s["wstage"], n)
                    step(pool.affine_select(out=block[:], in_=block[:], compare_op=ALU.is_ge, fill=0.0,
                                            base=HD - 1, pattern=[[HD, H], [0, HD]], channel_multiplier=-1))
                    pool.wait_ge(s["wstage"], n)
                    for v in range(HD):
                        step(pool.tensor_copy(red[:, v, :, v:v + 1], block[:, :, v:v + 1]))
                    step(pool.tensor_scalar(blockms[:], block[:], 1.0 / HD, None, ALU.mult))
                    pool.wait_ge(s["wstage"], n)
                    pool.memset(ones16[:, 0:1], 1.0).then_inc(s["const_pool"], 1)

                @blk.vector
                def _(dve):
                    dve.wait_ge(s["w_in"], 16 * 15)
                    for j in range(K):
                        for g in range(3):
                            dve.tensor_scalar(wt[:, j, g, :], wq[:, g, :], cw[:, g, j:j + 1], None, ALU.mult)
                    dve.tensor_scalar(gw[:], gw0[:], ns[:, 0:1], None, ALU.mult)
                    dve.tensor_scalar(w1[:], w1[:], ns[:, 0:1], None, ALU.mult).then_inc(s["setup_dve"], 1)
                    dve.wait_ge(s["const_pool"], 3)
                    dve.wait_ge(s["setup_dve"], 1)
                    dve.tensor_copy(b2p[0:1], b2[:])
                    for h in range(2):
                        last = dve.tensor_copy(b1p[0:1, :, h * HID:(h + 1) * HID],
                                               b1[:, :, h:512:2])
                    last.then_inc(s["setup_dve"], 1)
                    dve.wait_ge(s["setup_dve"], 2)
                    dve.tensor_tensor(b2l[:], b2[:], b2p[0:1], ALU.subtract)
                    for h in range(2):
                        last = dve.tensor_tensor(b1l[:, :, h * HID:(h + 1) * HID], b1[:, :, h:512:2],
                                                 b1p[0:1, :, h * HID:(h + 1) * HID], ALU.subtract)
                    last.then_inc(s["setup_dve"], 1)
                    dve.wait_ge(s["setup_act"], 3)
                    for h in range(2):
                        cut = slice(h * HID, (h + 1) * HID)
                        dve.tensor_tensor(w1lo[:, :, cut], w1[:, :, h:512:2], w1hi[:, :, cut], ALU.subtract)
                    dve.tensor_tensor(w2lo[:], w2[:], w2hi[:], ALU.subtract)
                    for j in range(K):
                        dve.wait_ge(s["setup_act"], 4 + j)
                        dve.tensor_tensor(wclo[:, j], bank[j][:, 0:3 * P], wchi[:, j], ALU.subtract)
                    dve.wait_ge(s["setup_act"], 4 + K)
                    dve.tensor_tensor(wplo[:], bank[4][:, 0:3 * P], wphi[:], ALU.subtract)

                @blk.scalar
                def _(act):
                    act.preload_act_table_set("natural_log_exp_and_others")
                    act.wait_ge(s["setup_dve"], 1)
                    for h in range(2):
                        act.activation(w1hi[:, :, h * HID:(h + 1) * HID], w1[:, :, h:512:2],
                                       ACT.Copy).then_inc(s["setup_act"], 1)
                    act.activation(w2hi[:], w2[:], ACT.Copy).then_inc(s["setup_act"], 1)
                    for j in range(K):
                        act.wait_ge(s["setup_pe"], j + 1)
                        act.activation(wchi[:, j], bank[j][:, 0:3 * P], ACT.Copy).then_inc(s["setup_act"], 1)
                    act.wait_ge(s["setup_pe"], K + 1)
                    act.activation(wphi[:], bank[4][:, 0:3 * P], ACT.Copy).then_inc(s["setup_act"], 1)
                    act.wait_ge(s["setup_pe"], K + 2)
                    act.activation(woT[:], bank[5][:, 0:P], ACT.Copy)
                    act.activation(hb[:], bank[5][:, P:P + 2], ACT.Copy).then_inc(s["setup_act"], 1)
                    act.wait_ge(s["setup_act"], 5 + K)
                    act.activation(negA[:], hb[:, 1:2], ACT.Exp).then_inc(s["setup_act"], 1)
                    act.wait_ge(s["setup_act"], 6 + K)
                    act.activation(negA[:], negA[:], ACT.Copy, scale=-1.0).then_inc(s["setup_act"], 1)

                @blk.tensor
                def _(pe):
                    pe.wait_ge(s["const_pool"], 3)
                    pe.wait_ge(s["setup_dve"], 1)
                    for j in range(K):
                        for g in range(3):
                            last = pe.transpose(bank[j][:, g * P:(g + 1) * P], wt[:, j, g, :], ident[:])
                        last.then_inc(s["setup_pe"], 1)
                    for a in range(2):
                        pe.matmul(bank[4][:, a * P:(a + 1) * P], wab[:, a, :],
                                  rep[:].rearrange("h a b -> h (a b)"), start=True, stop=True)
                    pe.transpose(bank[4][:, 2 * P:3 * P], wz[:], ident[:]).then_inc(s["setup_pe"], 1)
                    pe.transpose(bank[5][:, 0:P], wo[:], ident[:])
                    pe.matmul(bank[5][:, P:P + 2], rep[:].rearrange("h a b -> h (a b)"), hb0[:],
                              start=True, stop=True).then_inc(s["setup_pe"], 1)

        with ExitStack() as stage:
            def st(name, shape, dt=F32):
                return stage.enter_context(nc.sbuf_tensor(name, shape, dt))

            stats = st("stats", [P, C, 6])
            mv1 = st("mv1", [P, C, 2])
            rs1 = st("rs1", [P, C])
            U = st("U", [P, C, P])
            xhi = st("xhi", [P, 2, K - 1 + T], F16)
            xlo = st("xlo", [P, 2, K - 1 + T], F16)
            dec = st("dec", [P, 2, T])
            beta = st("beta", [P, T])
            sg = [st(f"sg{i}", [P, T]) for i in range(4)]
            vs, vb, ks, qs, sq1, sq2 = (st(n, [P, T]) for n in ("vs", "vb", "ks", "qs", "sq1", "sq2"))
            rk, rq = st("rk", [P, T]), st("rq", [P, T])
            kn, qn, zs = (st(n, [P, 2, T]) for n in ("kn", "qn", "zs"))
            vhi = st("vhi", [P, 2, T], F16)
            vlo = st("vlo", [P, 2, T], F16)
            kv = st("kv", [P, 2, T])
            Sv = st("Sv", [P, 2, T])
            qS = st("qS", [P, 2, T])
            osq, ro, og, gz = (st(n, [P, T]) for n in ("osq", "ro", "og", "gz"))
            st2 = st("st2", [P, C, 6])
            mv2 = st("mv2", [P, C, 2])
            rs2 = st("rs2", [P, C])
            st3 = st("st3", [P, C, 6])
            mv3 = st("mv3", [P, C, 2])
            rs3 = st("rs3", [P, C])
            yn = st("yn", [P, C, P])
            ms, rr, tsc = st("ms", [P, C]), st("rr", [P, C]), st("tsc", [P, C])
            tr = st("tr", [P, 2, C, TOP, W])
            tTs = st("tTs", [P, T])
            lg = st("lg", [P, C, E])
            lg2 = st("lg2", [P, C, E])
            eq, one1, one2 = st("eq", [P, C, E]), st("one1", [P, C, E]), st("one2", [P, C, E])
            mask = st("mask", [P, C, E], BF16)
            place = st("place", [P, C, E])
            m1, m2, wm, pd, p0 = (st(n, [P, C]) for n in ("m1", "m2", "wm", "pd", "p0"))
            slot = st("slot", [P, 2, C, TOP], I32)
            slotf = st("slotf", [P, C, TOP])
            dest = st("dest", [P, C, TOP])

            NR = 19

            def F_dve_a(dve, n, p, b):
                if isinstance(b, int):
                    dve.wait_ge(s["x_in"], 64)
                after(dve, s["f_rstd"], n - 1)
                for c in range(C):
                    dve.bn_stats(stats[:, c, :], X[:, bass.ds(b * C + c, 1), :]).then_inc(s["f_stats"], 1)
                fence(dve, s["f_stats"], n * 8 - 4)
                for c in range(C):
                    dve.bn_aggr(mv1[:, c, :], stats[:, c, :]).then_inc(s["f_stats"], 1)

            def F_dve_b(dve, n, p, b):
                dve.wait_ge(s["f_rstd"], n)
                after(dve, s["f_uT"], n - 1)
                for c in range(C):
                    last = dve.tensor_scalar(U[:, c, :], X[:, bass.ds(b * C + c, 1), :], mv1[:, c, 0:1],
                                             rs1[:, c:c + 1], ALU.subtract, ALU.mult)
                last.then_inc(s["f_u"], 1)

            def F_dve_c(dve, n, p):
                dve.wait_ge(s["f_xhi"], n)
                after(dve, s["f_pz"], n - 2)
                dve.tensor_tensor(xlo[:, p, K - 1:], B_T[:], xhi[:, p, K - 1:], ALU.subtract).then_inc(s["f_xlo"], 1)

            def F_dve_v(dve, n, p):
                dve.wait_ge(s["f_sv"], n)
                dve.tensor_tensor(vs[:], B_P0[:], sg[0][:], ALU.mult).then_inc(s["f_vs"], 1)
                dve.wait_ge(s["f_vs"], n)
                dve.wait_ge(s["f_beta"], 2 * n)
                dve.tensor_tensor(vb[:], vs[:], beta[:], ALU.mult).then_inc(s["f_vb"], 1)

            def F_dve_k(dve, n, p):
                dve.wait_ge(s["f_sk"], n)
                dve.tensor_tensor(ks[:], B_P1[:], sg[1][:], ALU.mult).then_inc(s["f_ks"], 1)

            def F_dve_q(dve, n, p):
                dve.wait_ge(s["f_sq"], n)
                dve.tensor_tensor(qs[:], B_P0[:], sg[2][:], ALU.mult).then_inc(s["f_qs"], 1)
                dve.wait_ge(s["f_vhi"], n)
                dve.tensor_tensor(vlo[:, p], vb[:], vhi[:, p], ALU.subtract).then_inc(s["f_vlo"], 1)

            def F_dve_z(dve, n, p):
                dve.wait_ge(s["f_sz"], n)
                dve.tensor_tensor(zs[:, p], B_P1[:], sg[3][:], ALU.mult).then_inc(s["f_zs"], 1)

            def F_dve_kn(dve, n, p):
                dve.wait_ge(s["f_rk"], n)
                dve.tensor_tensor(kn[:, p], ks[:], rk[:], ALU.mult).then_inc(s["f_kn"], 1)

            def F_dve_qn(dve, n, p):
                dve.wait_ge(s["f_rq"], n)
                after(dve, s_qs, (n - 2) * HD)
                dve.tensor_tensor(qn[:, p], qs[:], rq[:], ALU.mult).then_inc(s["f_qn"], 1)

            def F_act(act, n, p):
                act.wait_ge(s["f_stats"], n * 8)
                after(act, s["f_u"], n - 1)
                act.activation(rs1[:], mv1[:, :, 1], ACT.Ln, bias=epsc[:, 0:1]).then_inc(s["f_ea"], 1)
                act.wait_ge(s["f_ea"], n * 2 - 1)
                act.activation(rs1[:], rs1[:], ACT.Exp, scale=-0.5).then_inc(s["f_rstd"], 1)
            def F_act_x(act, n, p):
                act.wait_ge(s["f_uT"], n)
                after(act, s["f_pz"], n - 2)
                act.activation(xhi[:, p, K - 1:], B_T[:], ACT.Copy).then_inc(s["f_xhi"], 1)

            def F_act_b(act, n, p):
                act.wait_ge(s["f_pa"], n)
                after(act, s_scan, (n - 2) * HD)
                act.activation(dec[:, p], B_P0[:], ACT.Exp, bias=hb[:, 0:1]).then_inc(s["f_ea"], 1)
                act.wait_ge(s["f_pb"], n)
                after(act, s["f_vb"], n - 1)
                act.activation(beta[:], B_P1[:], ACT.Exp, scale=-1.0).then_inc(s["f_eb"], 1)
                act.wait_ge(s["f_ea"], n * 2)
                act.activation(dec[:, p], dec[:, p], ACT.Ln, bias=1.0).then_inc(s["f_dec"], 1)
                act.wait_ge(s["f_eb"], n)
                act.activation(beta[:], beta[:], ACT.Ln, bias=1.0).then_inc(s["f_beta"], 1)
                act.wait_ge(s["f_dec"], 2 * n - 1)
                act.activation(dec[:, p], dec[:, p], ACT.Exp, scale=negA[:, 0:1]).then_inc(s["f_dec"], 1)
                act.wait_ge(s["f_beta"], 2 * n - 1)
                act.activation(beta[:], beta[:], ACT.Exp, scale=-1.0).then_inc(s["f_beta"], 1)

            def sigmoid(act, n, ready, src, used, link, done, to):
                act.wait_ge(ready, n)
                after(act, used, n - 1)
                act.activation(to[:], src[:], ACT.Exp, scale=-1.0).then_inc(link, 1)
                act.wait_ge(link, 2 * n - 1)
                act.activation(to[:], to[:], ACT.Ln, bias=1.0).then_inc(link, 1)
                act.wait_ge(link, 2 * n)
                act.activation(to[:], to[:], ACT.Exp, scale=-1.0).then_inc(done, 1)

            def F_act_v(act, n, p):
                sigmoid(act, n, s["f_pv"], B_P0, s["f_vs"], s["f_ev"], s["f_sv"], sg[0])

            def F_act_k(act, n, p):
                sigmoid(act, n, s["f_pk"], B_P1, s["f_ks"], s["f_ek"], s["f_sk"], sg[1])

            def F_act_q(act, n, p):
                act.wait_ge(s["f_vb"], n)
                after(act, s_bc[1], (n - 2) * (HD // 2))
                act.activation(vhi[:, p], vb[:], ACT.Copy).then_inc(s["f_vhi"], 1)
                sigmoid(act, n, s["f_pq"], B_P0, s["f_qs"], s["f_eq"], s["f_sq"], sg[2])

            def F_act_z(act, n, p):
                act.wait_ge(s["f_ks"], n)
                after(act, s["f_nk"], n - 1)
                act.activation(sq1[:], ks[:], ACT.Square).then_inc(s["f_k2"], 1)
                sigmoid(act, n, s["f_pz"], B_P1, s["f_zs"], s["f_ez"], s["f_sz"], sg[3])

            def F_act_nk(act, n, p):
                act.wait_ge(s["f_qs"], n)
                after(act, s["f_nq"], n - 1)
                act.activation(sq2[:], qs[:], ACT.Square).then_inc(s["f_q2"], 1)
                act.wait_ge(s["f_nk"], n)
                after(act, s["f_kn"], n - 1)
                act.activation(rk[:], B_N[:], ACT.Ln, bias=epsc[:, 1:2]).then_inc(s["f_lk"], 1)
                act.wait_ge(s["f_lk"], n)
                act.activation(rk[:], rk[:], ACT.Exp, scale=-0.5).then_inc(s["f_rk"], 1)

            def F_act_nq(act, n, p):
                act.wait_ge(s["f_nq"], n)
                after(act, s["f_qn"], n - 1)
                act.activation(rq[:], B_N[:], ACT.Ln, bias=epsc[:, 1:2]).then_inc(s["f_lq"], 1)
                act.wait_ge(s["f_lq"], n)
                act.activation(rq[:], rq[:], ACT.Exp, scale=-0.5, bias=epsc[:, 2:3]).then_inc(s["f_rq"], 1)

            def F_pe_a(pe, n, p):
                pe.wait_ge(s["f_u"], n)
                after(pe, s["e_slot"], n - 4)
                for c in range(C):
                    last = pe.transpose(B_T[:, c * P:(c + 1) * P], U[:, c, :], ident[:])
                last.then_inc(s["f_uT"], 1)

            def project(pe, to, hi, lo, xh, xl, first, last):
                pe.matmul(to, hi, xh, start=first, stop=False)
                pe.matmul(to, hi, xl, start=False, stop=False)
                return pe.matmul(to, lo, xh, start=False, stop=last)

            now = slice(K - 1, K - 1 + T)

            def F_pe_ab(pe, n, p):
                pe.wait_ge(s["f_xhi"], n)
                pe.wait_ge(s["f_xlo"], n)
                after(pe, s["f_qs"], n - 1)
                project(pe, B_P0[:], wphi[:, 0], wplo[:, 0], xhi[:, p, now], xlo[:, p, now],
                        True, True).then_inc(s["f_pa"], 1)
                after(pe, s["f_zs"], n - 1)
                project(pe, B_P1[:], wphi[:, 1], wplo[:, 1], xhi[:, p, now], xlo[:, p, now],
                        True, True).then_inc(s["f_pb"], 1)

            def conv(pe, p, to, g, done):
                for j in range(K):
                    last = project(pe, to[:], wchi[:, j, g], wclo[:, j, g], xhi[:, p, j:j + T],
                                   xlo[:, p, j:j + T], j == 0, j == K - 1)
                last.then_inc(done, 1)

            def F_pe_v(pe, n, p):
                pe.wait_ge(s["f_ea"], n * 2)
                conv(pe, p, B_P0, 2, s["f_pv"])

            def F_pe_k(pe, n, p):
                pe.wait_ge(s["f_eb"], n)
                conv(pe, p, B_P1, 1, s["f_pk"])

            def F_pe_q(pe, n, p):
                pe.wait_ge(s["f_vs"], n)
                conv(pe, p, B_P0, 0, s["f_pq"])

            def F_pe_z(pe, n, p):
                pe.wait_ge(s["f_ks"], n)
                project(pe, B_P1[:], wphi[:, 2], wplo[:, 2], xhi[:, p, now], xlo[:, p, now],
                        True, True).then_inc(s["f_pz"], 1)

            def F_pe_nk(pe, n, p):
                pe.wait_ge(s["f_k2"], n)
                after(pe, s["e_lo"], n - 2)
                pe.matmul(B_N[:], block[:].rearrange("p a b -> p (a b)"), sq1[:],
                          start=True, stop=True).then_inc(s["f_nk"], 1)

            def F_pe_nq(pe, n, p):
                pe.wait_ge(s["f_q2"], n)
                pe.wait_ge(s["f_lk"], n)
                pe.matmul(B_N[:], block[:].rearrange("p a b -> p (a b)"), sq2[:],
                          start=True, stop=True).then_inc(s["f_nq"], 1)

            BC = (B_B0, B_B1)

            def S_pe(pe, n, p, v):
                base = (n - 1) * HD

                def bcast(v):
                    after(pe, s_kv, base + v - 1)
                    lhs = sel[:, v].rearrange("p a b -> p (a b)")
                    pe.matmul(BC[v % 2][:], lhs, vhi[:, p], start=True, stop=False)
                    pe.matmul(BC[v % 2][:], lhs, vlo[:, p], start=False, stop=True).then_inc(s_bc[v % 2], 1)

                if v < 0:
                    pe.wait_ge(s["f_vhi"], n)
                    pe.wait_ge(s["f_vlo"], n)
                    bcast(0)
                    bcast(1)
                    return
                if v + 2 < HD:
                    bcast(v + 2)
                pe.wait_ge(s_qs, base + v + 1)
                if v == 0:
                    after(pe, s["e_og"], n - 1)
                pe.matmul(B_O[:], red[:, v].rearrange("p a b -> p (a b)"), qS[:, v % 2],
                          start=v == 0, stop=v == HD - 1).then_inc(s_red, 1)

            def S_dve(dve, n, p, v):
                base = (n - 1) * HD

                def product(v):
                    dve.wait_ge(s_bc[v % 2], (n - 1) * (HD // 2) + v // 2 + 1)
                    after(dve, s_scan, base + v - 1)
                    dve.tensor_tensor(kv[:, v % 2], BC[v % 2][:], kn[:, p], ALU.mult).then_inc(s_kv, 1)

                if v < 0:
                    dve.wait_ge(s["f_kn"], n)
                    dve.wait_ge(s["f_dec"], 2 * n)
                    product(0)
                    return
                if v + 1 < HD:
                    product(v + 1)
                dve.wait_ge(s_kv, base + v + 1)
                after(dve, s_qs, base + v - 1)
                dve.tensor_tensor_scan(Sv[:, v % 2], dec[:, p], kv[:, v % 2], 0.0,
                                       ALU.mult, ALU.add).then_inc(s_scan, 1)

            def S_pool(pool, n, p, v):
                base = (n - 1) * HD
                if v == 0:
                    pool.wait_ge(s["f_qn"], n)
                pool.wait_ge(s_scan, base + v + 1)
                after(pool, s_red, base + v - 1)
                pool.tensor_tensor(qS[:, v % 2], Sv[:, v % 2], qn[:, p], ALU.mult).then_inc(s_qs, 1)

            def E_act_a(act, n, p):
                act.wait_ge(s_red, n * HD)
                after(act, s["e_no"], n - 1)
                act.activation(osq[:], B_O[:], ACT.Square).then_inc(s["e_o2"], 1)

            def E_act_r(act, n, p):
                act.wait_ge(s["e_no"], n)
                after(act, s["e_og"], n - 1)
                act.activation(ro[:], B_N[:], ACT.Ln, bias=epsc[:, 1:2]).then_inc(s["e_lo"], 1)
                act.wait_ge(s["e_lo"], n)
                act.activation(ro[:], ro[:], ACT.Exp, scale=-0.5).then_inc(s["e_ro"], 1)

            def E_pe_a(pe, n, p):
                pe.wait_ge(s["e_o2"], n)
                pe.wait_ge(s["f_lq"], min(n + 1, NB) if isinstance(n, int) else n + 1)
                pe.matmul(B_N[:], blockms[:].rearrange("p a b -> p (a b)"), osq[:],
                          start=True, stop=True).then_inc(s["e_no"], 1)

            def E_dve_a(dve, n, p):
                dve.wait_ge(s["e_ro"], n)
                dve.wait_ge(s["f_zs"], n)
                after(dve, s["e_gz"], n - 1)
                dve.tensor_tensor(og[:], B_O[:], ro[:], ALU.mult).then_inc(s["e_og"], 1)
                dve.wait_ge(s["e_og"], n)
                after(dve, s["e_wo"], n - 1)
                dve.tensor_tensor(gz[:], og[:], zs[:, p], ALU.mult).then_inc(s["e_gz"], 1)

            def E_pe_b(pe, n, p):
                pe.wait_ge(s["e_gz"], n)
                after(pe, s["e_y"], n - 1)
                for c in range(C):
                    last = pe.matmul(B_W[:, c * P:(c + 1) * P], gz[:, c * P:(c + 1) * P], woT[:],
                                     start=True, stop=True)
                last.then_inc(s["e_wo"], 1)

            def E_dve_b(dve, n, p):
                dve.wait_ge(s["e_wo"], n)
                for c in range(C):
                    dve.bn_stats(st2[:, c, :], B_W[:, c * P:(c + 1) * P]).then_inc(s["e_st2"], 1)
                after(dve, s["e_rs2"], 2 * (n - 1))
                fence(dve, s["e_st2"], n * 8 - 4)
                for c in range(C):
                    dve.bn_aggr(mv2[:, c, :], st2[:, c, :]).then_inc(s["e_st2"], 1)

            def E_act_b(act, n, p):
                act.wait_ge(s["e_st2"], n * 8)
                after(act, s["e_y"], n - 1)
                act.activation(rs2[:], mv2[:, :, 1], ACT.Ln, bias=epsc[:, 0:1]).then_inc(s["e_rs2"], 1)
                act.wait_ge(s["e_rs2"], 2 * n - 1)
                act.activation(rs2[:], rs2[:], ACT.Exp, scale=-0.5).then_inc(s["e_rs2"], 1)

            def E_dve_c(dve, n, p):
                dve.wait_ge(s["e_rs2"], 2 * n)
                after(dve, s["e_x1"], n - 1)
                for c in range(C):
                    last = dve.tensor_scalar(yn[:, c, :], B_W[:, c * P:(c + 1) * P], mv2[:, c, 0:1],
                                             rs2[:, c:c + 1], ALU.subtract, ALU.mult)
                last.then_inc(s["e_y"], 1)

            def E_pool_a(pool, n, p, b):
                pool.wait_ge(s["e_y"], n)
                at = X[:, bass.ds(b * C, C), :]
                pool.tensor_tensor(at, at, yn[:], ALU.add).then_inc(s["e_x1"], 1)

            def E_dve_d(dve, n, p, b):
                dve.wait_ge(s["e_x1"], n)
                for c in range(C):
                    dve.bn_stats(st3[:, c, :], X[:, bass.ds(b * C + c, 1), :]).then_inc(s["e_st3"], 1)
                after(dve, s["e_t"], n - 1)
                fence(dve, s["e_st3"], n * 8 - 4)
                for c in range(C):
                    dve.bn_aggr(mv3[:, c, :], st3[:, c, :]).then_inc(s["e_st3"], 1)

            def E_act_c(act, n, p, b):
                act.wait_ge(s["e_st3"], n * 8)
                after(act, s["e_t"], n - 1)
                act.activation(rs3[:], mv3[:, :, 1], ACT.Ln, bias=epsc[:, 0:1]).then_inc(s["e_rs3"], 1)
                act.wait_ge(s["e_rs3"], 2 * n - 1)
                act.activation(rs3[:], rs3[:], ACT.Exp, scale=-0.5).then_inc(s["e_rs3"], 1)
            def E_act_rr(act, n, p):
                act.wait_ge(s["e_ms"], 2 * n)
                after(act, s["e_tsc"], n - 1)
                act.activation(rr[:], ms[:], ACT.Ln, bias=epsc[:, 0:1]).then_inc(s["e_rr"], 1)
                act.wait_ge(s["e_rr"], 2 * n - 1)
                act.activation(rr[:], rr[:], ACT.Exp, scale=-0.5).then_inc(s["e_rr"], 1)

            def E_dve_e(dve, n, p, b):
                dve.wait_ge(s["e_rs3"], 2 * n)
                dve.tensor_copy(NORM3[:, bass.ds(b * C, C), 0], mv3[:, :, 0])
                dve.tensor_copy(NORM3[:, bass.ds(b * C, C), 1], rs3[:])
                after(dve, s["e_rr"], 2 * (n - 1))
                dve.tensor_tensor(ms[:], rs3[:], rs3[:], ALU.mult).then_inc(s["e_ms"], 1)
                dve.wait_ge(s["e_ms"], 2 * n - 1)
                dve.tensor_tensor(ms[:], ms[:], mv3[:, :, 1], ALU.mult).then_inc(s["e_ms"], 1)
            def E_dve_t(dve, n, p, b):
                dve.wait_ge(s["e_rr"], 2 * n)
                after(dve, s["e_t"], n - 1)
                dve.tensor_tensor(tsc[:], rr[:], rs3[:], ALU.mult).then_inc(s["e_tsc"], 1)
                dve.wait_ge(s["e_tsc"], n)
                after(dve, s_sent[p], sent(n, p))
                after(dve, s["e_t2"], n - 1)
                for c in range(C):
                    last = dve.tensor_scalar(tr[:, p, c, 0, 0:P], X[:, bass.ds(b * C + c, 1), :],
                                             mv3[:, c, 0:1], tsc[:, c:c + 1],
                                             ALU.subtract, ALU.mult)
                last.then_inc(s["e_t"], 1)

            def R_pe_t(pe, n, p):
                pe.wait_ge(s["e_t"], n)
                pe.wait_ge(s["f_xlo"], min(n + 3, NB) if isinstance(n, int) else n + 3)
                for c in range(C):
                    last = pe.transpose(B_T[:, c * P:(c + 1) * P], tr[:, p, c, 0, 0:P], ident[:])
                last.then_inc(s["e_tT"], 1)

            def R_pe_lg(pe, n, p):
                pe.wait_ge(s["e_tTs"], n)
                for c in range(C):
                    last = pe.matmul(B_T[:, c * E:(c + 1) * E], tTs[:, c * P:(c + 1) * P], gw[:],
                                     start=True, stop=True)
                last.then_inc(s["e_lg"], 1)

            def R_act_t(act, n, p):
                act.wait_ge(s["e_tT"], n)
                after(act, s["e_lg"], n - 1)
                act.activation(tTs[:], B_T[:], ACT.Copy).then_inc(s["e_tTs"], 1)

            def E_act_t2(act, n, p):
                act.wait_ge(s["e_t"], n)
                after(act, s_sent[p], sent(n, p))
                act.activation(tr[:, p, :, 1, 0:P], tr[:, p, :, 0, 0:P], ACT.Copy).then_inc(s["e_t2"], 1)

            def R_act_p(act, n, p):
                act.wait_ge(s["e_pd"], n)
                after(act, s["e_meta"], n - 1)
                act.activation(p0[:], pd[:], ACT.Exp).then_inc(s["e_p1"], 1)

            def wide(ap):
                return ap[:].unsqueeze(2).to_broadcast([P, C, E])

            def R_dve(dve, n, p, part):
                link = [(0, 8, 12)[part]]

                def then(ins):
                    link[0] += 1
                    ins.then_inc(r_chain, 1)
                    dve.wait_ge(r_chain, (n - 1) * NR + link[0])

                if part == 0:
                    dve.wait_ge(s["e_lg"], n)
                    after(dve, s["e_pos"], n - 1)
                    then(dve.tensor_tensor(lg[:], B_T[:, 0:C * E].rearrange("p (c e) -> p c e", e=E),
                                           gb[:].unsqueeze(1).to_broadcast([P, C, E]), ALU.add))
                    then(dve.tensor_reduce(m1[:], lg[:], AX.X, ALU.max))
                    then(dve.tensor_tensor(eq[:], lg[:], wide(m1), ALU.is_equal))
                    then(dve.tensor_tensor(eq[:], eq[:], rank[:], ALU.mult))
                    then(dve.tensor_reduce(wm[:], eq[:], AX.X, ALU.max))
                    then(dve.tensor_tensor(one1[:], rank[:], wide(wm), ALU.is_equal))
                    then(dve.scalar_tensor_tensor(lg2[:], one1[:], -3e38, lg[:], ALU.mult, ALU.add))
                    then(dve.tensor_reduce(m2[:], lg2[:], AX.X, ALU.max))
                    after(dve, s["e_p1"], n - 1)
                    dve.tensor_tensor(pd[:], m2[:], m1[:], ALU.subtract).then_inc(s["e_pd"], 1)
                if part == 1:
                    then(dve.tensor_tensor(eq[:], lg2[:], wide(m2), ALU.is_equal))
                    then(dve.tensor_tensor(eq[:], eq[:], rank[:], ALU.mult))
                    then(dve.tensor_reduce(wm[:], eq[:], AX.X, ALU.max))
                    then(dve.tensor_tensor(one2[:], rank[:], wide(wm), ALU.is_equal))
                    dve.tensor_tensor(mask[:], one1[:], one2[:], ALU.add).then_inc(s["e_mask"], 1)
                if part == 2:
                    dve.wait_ge(s["e_p1"], n)
                    then(dve.tensor_scalar(m1[:], p0[:], 1.0, None, ALU.add))
                    then(dve.reciprocal(m2[:], m1[:]))
                    after(dve, s_sent[p], sent(n, p))
                    dve.tensor_copy(tr[:, p, :, 0, P], m2[:])
                    dve.tensor_tensor(tr[:, p, :, 1, P], m2[:], p0[:], ALU.mult)
                    then(dve.tensor_copy(tr[:, p, :, :, P + 1], dest[:]))
                    then(dve.tensor_scalar(dest[:], dest[:], float(T), None, ALU.add))
                    dve.wait_ge(s["e_pos"], n)
                    then(dve.tensor_tensor(place[:], B_T[:, 64:64 + C * E].rearrange("p (c e) -> p c e", e=E),
                                           count[:].unsqueeze(1).to_broadcast([P, C, E]), ALU.add))
                    dve.tensor_tensor(count[:], count[:], B_T[:, 128:128 + E], ALU.add).then_inc(s["e_slot"], 1)
                    dve.tensor_tensor(one1[:], one1[:], place[:], ALU.mult)
                    then(dve.tensor_tensor(one2[:], one2[:], place[:], ALU.mult))
                    dve.tensor_reduce(slotf[:, :, 0], one1[:], AX.X, ALU.add)
                    then(dve.tensor_reduce(slotf[:, :, 1], one2[:], AX.X, ALU.add))
                    dve.tensor_copy(slot[:, p], slotf[:]).then_inc(s["e_meta"], 1)
                    assert link[0] == NR, link[0]

            def R_pe_pos(pe, n, p):
                pe.wait_ge(s["e_mask"], n)
                flat = mask[:].rearrange("p c e -> p (c e)")
                at = B_T[:, 64:64 + C * E]
                pe.matmul(at, tri[:], flat, start=True, stop=True, skip_group_check=True)
                for c in range(1, C):
                    pe.matmul(at[:, c * E:], ones_b[:], flat[:, 0:(C - c) * E],
                              start=False, stop=True, skip_group_check=True)
                for c in range(C):
                    last = pe.matmul(B_T[:, 128:128 + E], ones_b[:], mask[:, c], start=False, stop=True,
                                     skip_group_check=True)
                last.then_inc(s["e_pos"], 1)

            def R_pool(pool, n, p, some):
                pool.wait_ge(s["e_meta"], n)
                fence(pool, s["e_t2"], n)
                for i in some:
                    for c, k in ((i // TOP, i % TOP),):
                        pool.indirect_dma_start(
                            rows, bass.IndirectOffsetOnAxis(ap=slot[:, p, c, k:k + 1], axis=0),
                            tr[:, p, c, k, :], None).then_inc(s_sent[p], 16)

            def iterations(eng, step):
                for k in range(-2, 3):
                    step(k, stages(k), k % 2)
                with eng.Fori(1, NB // 2 - 2) as i:
                    step(2 * i + 1, "ABSER", 1)
                    step(2 * i + 2, "ABSER", 0)
                for k in range(NB - 3, NB + 2):
                    step(k, stages(k), k % 2)

            def stages(k):
                return "".join(x for x, lead in zip("ABSER", (2, 1, 0, -1, -2)) if 0 <= k + lead < NB)

            epsc = st("epsc", [P, 3])
            s_eps = s["const_pool"]

            with nc.Block() as blk:
                @blk.vector
                def _(dve):
                    for i, value in enumerate((EPS_LN, EPS_L2, -0.5 * 2.0794415416798357)):
                        dve.memset(epsc[:, i:i + 1], value)
                    dve.tensor_tensor(count[:], count[:], region0[:], ALU.add)
                    dve.tensor_copy(dest[:], token[:])
                    dve.memset(xhi[:, :, 0:K - 1], 0.0)
                    dve.memset(xlo[:, :, 0:K - 1], 0.0).then_inc(s_eps, 1)
                    dve.wait_ge(s_eps, 4)

                    def step(k, on, par):
                        a, b, c, e, r = k + 3, k + 2, k + 1, k, k - 1
                        if "S" in on:
                            S_dve(dve, c, par, -1)
                        for v in range(HD):
                            if "S" in on:
                                S_dve(dve, c, par, v)
                            if "E" in on:
                                if v == 0:
                                    E_dve_a(dve, e, 1 - par)
                                if v == 2:
                                    E_dve_b(dve, e, 1 - par)
                                if v == 3:
                                    E_dve_c(dve, e, 1 - par)
                                if v == 4:
                                    E_dve_d(dve, e, 1 - par, k - 1)
                                if v == 5:
                                    E_dve_e(dve, e, 1 - par, k - 1)
                                if v == 6:
                                    E_dve_t(dve, e, 1 - par, k - 1)
                            if "R" in on:
                                if 2 <= v <= 4:
                                    R_dve(dve, r, par, v - 2)
                            if "A" in on:
                                if v == 1:
                                    F_dve_a(dve, a, par, k + 2)
                                if v == 3:
                                    F_dve_b(dve, a, par, k + 2)
                                if v == 6:
                                    F_dve_c(dve, a, par)
                            if "B" in on:
                                if v == 3:
                                    F_dve_v(dve, b, 1 - par)
                                if v == 4:
                                    F_dve_k(dve, b, 1 - par)
                                if v == 5:
                                    F_dve_q(dve, b, 1 - par)
                                if v == 6:
                                    F_dve_z(dve, b, 1 - par)
                                if v == 7:
                                    F_dve_kn(dve, b, 1 - par)
                                    F_dve_qn(dve, b, 1 - par)

                    iterations(dve, step)

                @blk.scalar
                def _(act):
                    act.wait_ge(s_eps, 4)

                    def step(k, on, par):
                        a, b, e, r = k + 3, k + 2, k, k - 1
                        if "E" in on:
                            E_act_a(act, e, 1 - par)
                            E_act_r(act, e, 1 - par)
                        if "R" in on:
                            R_act_t(act, r, par)
                        if "B" in on:
                            F_act_b(act, b, 1 - par)
                            F_act_v(act, b, 1 - par)
                        if "A" in on:
                            F_act(act, a, par)
                        if "E" in on:
                            E_act_b(act, e, 1 - par)
                        if "R" in on:
                            R_act_p(act, r, par)
                        if "B" in on:
                            F_act_k(act, b, 1 - par)
                        if "E" in on:
                            E_act_c(act, e, 1 - par, k - 1)
                        if "B" in on:
                            F_act_q(act, b, 1 - par)
                        if "E" in on:
                            E_act_rr(act, e, 1 - par)
                        if "B" in on:
                            F_act_z(act, b, 1 - par)
                        if "A" in on:
                            F_act_x(act, a, par)
                        if "B" in on:
                            F_act_nk(act, b, 1 - par)
                            F_act_nq(act, b, 1 - par)
                        if "E" in on:
                            E_act_t2(act, e, 1 - par)

                    iterations(act, step)

                @blk.tensor
                def _(pe):
                    pe.wait_ge(s_eps, 4)

                    def step(k, on, par):
                        a, b, c, e, r = k + 3, k + 2, k + 1, k, k - 1
                        if "S" in on:
                            S_pe(pe, c, par, -1)
                        for v in range(HD):
                            if "E" in on:
                                if v == 0:
                                    E_pe_a(pe, e, 1 - par)
                                if v == 2:
                                    E_pe_b(pe, e, 1 - par)
                            if "R" in on:
                                if v == 0:
                                    R_pe_t(pe, r, par)
                                if v == 1:
                                    R_pe_lg(pe, r, par)
                                if v == 4:
                                    R_pe_pos(pe, r, par)
                            if "S" in on:
                                S_pe(pe, c, par, v)
                            if "B" in on:
                                if v == 0:
                                    F_pe_ab(pe, b, 1 - par)
                                if v == 1:
                                    F_pe_v(pe, b, 1 - par)
                                if v == 2:
                                    F_pe_k(pe, b, 1 - par)
                                if v == 3:
                                    F_pe_q(pe, b, 1 - par)
                                if v == 5:
                                    F_pe_z(pe, b, 1 - par)
                                if v == 6:
                                    F_pe_nk(pe, b, 1 - par)
                                if v == 7:
                                    F_pe_nq(pe, b, 1 - par)
                            if "A" in on:
                                if v == 5:
                                    F_pe_a(pe, a, par)

                    iterations(pe, step)

                @blk.gpsimd
                def _(pool):
                    def step(k, on, par):
                        c, e, r = k + 1, k, k - 1
                        for v in range(HD):
                            if "S" in on:
                                S_pool(pool, c, par, v)
                            if "E" in on and v == 3:
                                E_pool_a(pool, e, 1 - par, k - 1)
                            if "R" in on:
                                if v >= 5:
                                    R_pool(pool, r, par, ((0, 1, 2), (3, 4, 5), (6, 7))[v - 5])

                    iterations(pool, step)
                    for p in range(2):
                        pool.wait_ge(s_sent[p], 16 * C * TOP * NB // 2)

        tab = sb("tab", [P, TILES, 2], I32)
        with ExitStack() as stage:
            def st(name, shape, dt=F32):
                return stage.enter_context(nc.sbuf_tensor(name, shape, dt))

            cnt, tiles_of, ends, one = (st(n, [P, E]) for n in ("cnt", "tiles_of", "ends", "one"))
            jt = st("jt", [P, E, NT])
            over = st("over", [P, E, NT])
            tj = st("tj", [P, TILES, E])
            le = st("le", [P, TILES, E])
            te, first, tnum, start = (st(n, [P, TILES]) for n in ("te", "first", "tnum", "start"))
            pnum = st("pnum", [P, 1])
            padrow = st("padrow", [P, W])
            padat = st("padat", [P, E], I32)
            t_const, t_chain, t_pad = sem("t_const"), sem("t_chain"), sem("t_pad")

            with nc.Block() as blk:
                @blk.gpsimd
                def _(pool):
                    pool.iota(jt[:], pattern=[[0, E], [P, NT]], base=0, channel_multiplier=0,
                              allow_small_or_imprecise_dtypes=True).then_inc(t_const, 1)
                    pool.iota(tj[:], pattern=[[1, TILES], [0, E]], base=0, channel_multiplier=0,
                              allow_small_or_imprecise_dtypes=True).then_inc(t_const, 1)
                    pool.iota(tnum[:], pattern=[[1, TILES]], base=0, channel_multiplier=0,
                              allow_small_or_imprecise_dtypes=True).then_inc(t_const, 1)
                    pool.iota(pnum[:], pattern=[[0, 1]], base=0, channel_multiplier=1,
                              allow_small_or_imprecise_dtypes=True).then_inc(t_const, 1)
                    pool.memset(one[:], 1.0).then_inc(t_const, 1)
                    pool.memset(padrow[:, 0:P + 1], 0.0)
                    pool.memset(padrow[:, P + 1:W], FAR).then_inc(t_const, 1)
                    pool.wait_ge(t_const, 6)
                    pool.wait_ge(t_chain, 1)
                    for e in range(E):
                        pool.indirect_dma_start(
                            rows, bass.IndirectOffsetOnAxis(ap=padat[:, e:e + 1], axis=0),
                            padrow[:], None).then_inc(t_pad, 16)
                    pool.wait_ge(t_pad, 16 * E)

                @blk.vector
                def _(dve):
                    link = [0]

                    def then(ins):
                        link[0] += 1
                        ins.then_inc(t_chain, 1)
                        dve.wait_ge(t_chain, link[0])

                    dve.wait_ge(t_const, 6)
                    then(dve.tensor_scalar(padat[:], count[:], pnum[:, 0:1], None, ALU.add))
                    then(dve.tensor_tensor(cnt[:], count[:], region0[:], ALU.subtract))
                    then(dve.tensor_tensor(over[:], cnt[:].unsqueeze(2).to_broadcast([P, E, NT]), jt[:], ALU.is_gt))
                    then(dve.tensor_reduce(tiles_of[:], over[:], AX.X, ALU.add))
                    then(dve.tensor_tensor_scan(ends[:], one[:], tiles_of[:], 0.0, ALU.mult, ALU.add))
                    ends_b = ends[:].unsqueeze(1).to_broadcast([P, TILES, E])
                    then(dve.tensor_tensor(le[:], ends_b, tj[:], ALU.is_le))
                    then(dve.tensor_reduce(te[:], le[:], AX.X, ALU.add))
                    then(dve.tensor_tensor(le[:], le[:], ends_b, ALU.mult))
                    then(dve.tensor_reduce(first[:], le[:], AX.X, ALU.max))
                    then(dve.tensor_tensor(first[:], tnum[:], first[:], ALU.subtract))
                    then(dve.tensor_scalar(first[:], first[:], float(P), None, ALU.mult))
                    then(dve.tensor_scalar(start[:], te[:], float(REGION), None, ALU.mult))
                    then(dve.tensor_tensor(tab[:, :, 0], start[:], first[:], ALU.add))
                    then(dve.tensor_scalar(tab[:, :, 1], te[:], float(E - 1), None, ALU.min))

        with ExitStack() as stage:
            def st(name, shape, dt=F32):
                return stage.enter_context(nc.sbuf_tensor(name, shape, dt))

            RING = 4
            G = st("G", [P, RING, W])
            thi, tlo = st("thi", [P, 2, P], F16), st("tlo", [P, 2, P], F16)
            gate, lin, sig, hid = (st(n, [P, 2, HID]) for n in ("gate", "lin", "sig", "hid"))
            hhi, hlo = st("hhi", [P, 2, 2 * P], F16), st("hlo", [P, 2, 2 * P], F16)
            yw = st("yw", [P, RING, P])
            where = st("where", [P, RING], I32)
            m = sems("m_in0 m_in1 m_in2 m_in3 m_T m_hi m_lo m_h m_gate m_lin m_e1 m_e2 m_sig m_gs m_hid "
                     "m_hT m_hhi m_hlo m_y m_yw m_where m_out0 m_out1 m_out2 m_out3")
            m_in = (m["m_in0"], m["m_in1"], m["m_in2"], m["m_in3"])
            m_out = (m["m_out0"], m["m_out1"], m["m_out2"], m["m_out3"])
            B_H, B_HT, B_Y = (bank[1], bank[2]), (bank[3], bank[4]), (bank[5], bank[6])

            def tiles(eng, step):
                step(-1, True, False, False, 3)
                step(0, True, True, False, 0)
                for k in range(1, 4):
                    step(k, True, True, True, k)
                with eng.Fori(1, TILES // 4 - 1) as r:
                    for i in range(4):
                        step(4 * r + i, True, True, True, i)
                for k in range(TILES - 4, TILES - 1):
                    step(k, True, True, True, k % 4)
                step(TILES - 1, False, True, True, 3)
                step(TILES, False, False, True, 0)

            def filled(n, q):
                return 4 * (n - 1 - q) + 16

            with nc.Block() as blk:
                @blk.sync
                def _(sp):
                    def load(j, q):
                        if not (isinstance(j, int) and j < RING):
                            sp.wait_ge(m["m_T"], j - RING + 1)
                            sp.wait_ge(m["m_yw"], j - RING + 1)
                            sp.wait_ge(m["m_where"], j - RING + 1)
                        at = sp.value_load(tab[0:1, bass.ds(j, 1), 0:1], min_val=0,
                                           max_val=E * REGION + (SPARE - 1) * P)
                        sp.dma_start(G[:, q, :], rows[bass.ds(at, P), :]).then_inc(m_in[q], 16)

                    for j in range(4):
                        load(j, j)
                    with sp.Fori(1, TILES // 4) as r:
                        for i in range(4):
                            load(4 * r + i, i)

                @blk.tensor
                def _(pe):
                    def transposes(n, q):
                        p = q % 2
                        pe.wait_ge(m_in[q], filled(n, q))
                        after(pe, m["m_lo"], n - 1)
                        pe.transpose(bank[0][:, 0:P], G[:, q, 0:P], ident[:]).then_inc(m["m_T"], 1)

                    def first_product(n, q):
                        p = q % 2
                        e = pe.value_load(tab[0:1, bass.ds(n - 1, 1), 1:2], min_val=0, max_val=E - 1)
                        pe.wait_ge(m["m_lo"], n)
                        pe.wait_ge(m["m_hi"], n)
                        after(pe, m["m_lin"], n - 2)
                        to = B_H[p][:]
                        w_hi = w1hi[:, bass.ds(e, 1), :].rearrange("p a f -> p (a f)")
                        w_lo = w1lo[:, bass.ds(e, 1), :].rearrange("p a f -> p (a f)")
                        bias = b1p[:, bass.ds(e, 1), :].rearrange("p a f -> p (a f)")
                        pe.matmul(to, ones16[:], bias, start=True, stop=False)
                        pe.matmul(to, thi[:, p], w_hi, start=False, stop=False)
                        pe.matmul(to, thi[:, p], w_lo, start=False, stop=False)
                        pe.matmul(to, tlo[:, p], w_hi, start=False, stop=True).then_inc(m["m_h"], 1)

                    def second_product(n, q):
                        p = q % 2
                        e = pe.value_load(tab[0:1, bass.ds(n - 1, 1), 1:2], min_val=0, max_val=E - 1)
                        pe.wait_ge(m["m_hid"], n)
                        after(pe, m["m_hlo"], n - 2)
                        pe.transpose(B_HT[p][:, 0:P], hid[:, p, 0:P], ident[:])
                        pe.transpose(B_HT[p][:, P:2 * P], hid[:, p, P:2 * P], ident[:]).then_inc(m["m_hT"], 1)
                        to = B_Y[p][:, 0:P]
                        after(pe, m["m_yw"], n - 2)
                        pe.matmul(to, ones16[:], b2p[:, bass.ds(e, 1), :].rearrange("p a f -> p (a f)"),
                                  start=True, stop=False)
                        pe.wait_ge(m["m_hhi"], n)
                        pe.wait_ge(m["m_hlo"], n)
                        for c in range(2):
                            hi, lo = hhi[:, p, c * P:(c + 1) * P], hlo[:, p, c * P:(c + 1) * P]
                            w_hi = w2hi[:, bass.ds(e, 1), c, :].rearrange("p a f -> p (a f)")
                            w_lo = w2lo[:, bass.ds(e, 1), c, :].rearrange("p a f -> p (a f)")
                            pe.matmul(to, hi, w_hi, start=False, stop=False)
                            pe.matmul(to, hi, w_lo, start=False, stop=False)
                            last = pe.matmul(to, lo, w_hi, start=False, stop=c == 1)
                        last.then_inc(m["m_y"], 1)

                    def step(k, a, b, c, q):
                        if a:
                            transposes(k + 2, (q + 1) % 4)
                        if b:
                            first_product(k + 1, q)
                        if c:
                            second_product(k, (q + 3) % 4)

                    tiles(pe, step)

                @blk.vector
                def _(dve):
                    def step(k, a, b, c, q):
                        p = q % 2
                        if b:
                            n = k + 1
                            dve.wait_ge(m["m_h"], n)
                            after(dve, m["m_gs"], n - 2)
                            dve.tensor_scalar(gate[:, p], B_H[p][:, 0:HID], LIMIT, GUARD, ALU.min,
                                              ALU.max).then_inc(m["m_gate"], 1)
                            after(dve, m["m_hid"], n - 2)
                            dve.tensor_scalar(lin[:, p], B_H[p][:, HID:], LIMIT, -LIMIT, ALU.min,
                                              ALU.max).then_inc(m["m_lin"], 1)
                        if c:
                            n = k
                            dve.wait_ge(m["m_hhi"], n)
                            dve.tensor_tensor(hlo[:, 1 - p], B_HT[1 - p][:, 0:HID], hhi[:, 1 - p],
                                              ALU.subtract).then_inc(m["m_hlo"], 1)
                        if a:
                            n = k + 2
                            dve.wait_ge(m["m_hi"], n)
                            after(dve, m["m_h"], n - 2)
                            dve.tensor_tensor(tlo[:, 1 - p], bank[0][:, 0:P], thi[:, 1 - p],
                                              ALU.subtract).then_inc(m["m_lo"], 1)
                        if b:
                            n = k + 1
                            dve.wait_ge(m["m_gs"], n)
                            dve.wait_ge(m["m_lin"], n)
                            after(dve, m["m_hT"], n - 2)
                            dve.scalar_tensor_tensor(hid[:, p], lin[:, p], 1.0, sig[:, p], ALU.add,
                                                     ALU.mult).then_inc(m["m_hid"], 1)

                    tiles(dve, step)

                @blk.scalar
                def _(act):
                    def step(k, a, b, c, q):
                        p = q % 2
                        n = k + 1
                        if b:
                            act.wait_ge(m["m_gate"], n)
                            after(act, m["m_hid"], n - 2)
                            act.activation(sig[:, p], gate[:, p], ACT.Exp, scale=-ALPHA).then_inc(m["m_e1"], 1)
                        if a:
                            act.wait_ge(m["m_T"], n + 1)
                            after(act, m["m_h"], n - 1)
                            act.activation(thi[:, 1 - p], bank[0][:, 0:P], ACT.Copy).then_inc(m["m_hi"], 1)
                        if b:
                            act.wait_ge(m["m_e1"], n)
                            act.activation(sig[:, p], sig[:, p], ACT.Ln, bias=1.0).then_inc(m["m_e2"], 1)
                        if c:
                            act.wait_ge(m["m_hT"], n - 1)
                            after(act, m["m_y"], n - 3)
                            act.activation(hhi[:, 1 - p], B_HT[1 - p][:, 0:HID], ACT.Copy).then_inc(m["m_hhi"], 1)
                        if b:
                            act.wait_ge(m["m_e2"], n)
                            act.activation(sig[:, p], sig[:, p], ACT.Exp, scale=-1.0).then_inc(m["m_sig"], 1)
                        if c:
                            act.wait_ge(m["m_y"], n - 1)
                            qc = (q + 3) % 4
                            if not (isinstance(k, int) and k <= RING):
                                act.wait_ge(m_out[qc], filled(k, qc) - 16)
                            act.activation(yw[:, qc], B_Y[1 - p][:, 0:P], ACT.Copy,
                                           scale=G[:, qc, P:P + 1]).then_inc(m["m_yw"], 1)

                    tiles(act, step)

                @blk.gpsimd
                def _(pool):
                    def step(k, a, b, c, q):
                        p = q % 2
                        if b:
                            n = k + 1
                            pool.wait_ge(m["m_sig"], n)
                            pool.tensor_tensor(sig[:, p], gate[:, p], sig[:, p], ALU.mult).then_inc(m["m_gs"], 1)
                            fence(pool, m_in[q], filled(n, q))
                            fence(pool, m_out[q], filled(n, q) - 16)
                            pool.tensor_copy(where[:, q:q + 1], G[:, q, P + 1:W]).then_inc(m["m_where"], 1)
                        if c:
                            qc = (q + 3) % 4
                            pool.wait_ge(m["m_yw"], k)
                            fence(pool, m["m_where"], k)
                            pool.indirect_dma_start(
                                results, bass.IndirectOffsetOnAxis(ap=where[:, qc:qc + 1], axis=0),
                                yw[:, qc], None, bounds_check=TOP * N - 1,
                                oob_is_err=False).then_inc(m_out[qc], 16)

                    tiles(pool, step)
                    for q in range(4):
                        pool.wait_ge(m_out[q], 16 * (TILES // RING))

        with ExitStack() as stage:
            def st(name, shape, dt=F32):
                return stage.enter_context(nc.sbuf_tensor(name, shape, dt))

            Y = st("Y", [P, 2, TOP, C, P])
            U4, Z4, O4 = st("U4", [P, 2, C, P]), st("Z4", [P, 2, C, P]), st("O4", [P, 2, C, P])
            st4, mv4, rs4 = st("st4", [P, C, 6]), st("mv4", [P, C, 2]), st("rs4", [P, C])
            o = sems("o_sum o_u o_z o_st o_mv o_ln o_rs o_n o_x o_const")
            o_in, o_out = (sem("o_in0"), sem("o_in1")), (sem("o_out0"), sem("o_out1"))
            eps4 = st("eps4", [P, 1])

            def both(eng, step):
                step(0, 0)
                step(1, 1)
                with eng.Fori(1, NB // 2) as r:
                    for i in range(2):
                        step(2 * r + i, i)

            with nc.Block() as blk:
                @blk.sync
                def _(sp):
                    def step(b, p):
                        after(sp, o["o_z"], b - 1)
                        for k in range(TOP):
                            sp.dma_start(Y[:, p, k], rv[:, k, bass.ds(b * C, C), :]).then_inc(o_in[p], 16)

                    both(sp, step)

                @blk.gpsimd
                def _(pool):
                    def step(b, p):
                        pool.wait_ge(o_in[p], 16 * b - 16 * p + 32)
                        pool.tensor_tensor(Y[:, p, 0], Y[:, p, 0], Y[:, p, 1], ALU.add).then_inc(o["o_sum"], 1)

                    both(pool, step)

                @blk.vector
                def _(dve):
                    dve.memset(eps4[:], EPS_LN).then_inc(o["o_const"], 1)

                    def step(b, p):
                        n = b + 1
                        after(dve, o["o_z"], n - 2)
                        for c in range(C):
                            last = dve.tensor_scalar(U4[:, p, c], X[:, bass.ds(b * C + c, 1), :],
                                                     NORM3[:, bass.ds(b * C + c, 1), 0],
                                                     NORM3[:, bass.ds(b * C + c, 1), 1],
                                                     ALU.subtract, ALU.mult)
                        last.then_inc(o["o_u"], 1)
                        dve.wait_ge(o["o_u"], n)
                        dve.wait_ge(o["o_sum"], n)
                        after(dve, o["o_n"], n - 2)
                        dve.tensor_tensor(Z4[:, p], U4[:, p], Y[:, p, 0], ALU.add).then_inc(o["o_z"], 1)
                        dve.wait_ge(o["o_z"], n)
                        after(dve, o["o_mv"], n - 1)
                        for c in range(C):
                            last = dve.bn_stats(st4[:, c], Z4[:, p, c])
                        last.then_inc(o["o_st"], 1)
                        after(dve, o["o_ln"], n - 1)
                        after(dve, o["o_n"], n - 1)
                        fence(dve, o["o_st"], n)
                        for c in range(C):
                            last = dve.bn_aggr(mv4[:, c], st4[:, c])
                        last.then_inc(o["o_mv"], 1)
                        dve.wait_ge(o["o_rs"], n)
                        after(dve, o["o_x"], n - 2)
                        for c in range(C):
                            last = dve.tensor_scalar(U4[:, p, c], Z4[:, p, c], mv4[:, c, 0:1], rs4[:, c:c + 1],
                                                     ALU.subtract, ALU.mult)
                        last.then_inc(o["o_n"], 1)
                        dve.wait_ge(o["o_n"], n)
                        after(dve, o_out[p], 16 * (b - p) // 2 if isinstance(b, int) else 8 * b - 8 * p)
                        dve.tensor_tensor(O4[:, p], X[:, bass.ds(b * C, C), :], U4[:, p], ALU.add).then_inc(o["o_x"], 1)

                    both(dve, step)

                @blk.scalar
                def _(act):
                    act.wait_ge(o["o_const"], 1)

                    def step(b, p):
                        n = b + 1
                        act.wait_ge(o["o_mv"], n)
                        after(act, o["o_n"], n - 1)
                        act.activation(rs4[:], mv4[:, :, 1], ACT.Ln, bias=eps4[:, 0:1]).then_inc(o["o_ln"], 1)
                        act.wait_ge(o["o_ln"], n)
                        act.activation(rs4[:], rs4[:], ACT.Exp, scale=-0.5).then_inc(o["o_rs"], 1)
                        act.wait_ge(o["o_x"], n)
                        act.dma_start(ov[:, bass.ds(b * C, C), :], O4[:, p]).then_inc(o_out[p], 16)

                    both(act, step)
                    for p in range(2):
                        act.wait_ge(o_out[p], 16 * (NB // 2))


_INS = ["L0_attn_x", "L0_attn_W_qkv", "L0_attn_conv_w", "L0_attn_W_z", "L0_attn_W_b", "L0_attn_W_a",
        "L0_attn_dt_bias", "L0_attn_A_log", "L0_attn_W_out", "L0_ffn_norm_scale", "L0_ffn_gate_w",
        "L0_ffn_gate_b", "L0_ffn_mlp1_w", "L0_ffn_mlp1_b", "L0_ffn_mlp2_w", "L0_ffn_mlp2_b"]


def kernel(**inputs):
    import numpy as _np
    import concourse.bacc as _bacc
    from concourse import mybir as _mybir
    from concourse.bass_utils import run_bass_kernel_spmd as _run

    nc = _bacc.Bacc("TRN2", target_bir_lowering=False, num_devices=1)
    arrays, args = {}, []
    for name in _INS:
        a = _np.ascontiguousarray(inputs[name])
        arrays[f"in_{name}_dram"] = a
        args.append(nc.dram_tensor(f"in_{name}_dram", a.shape, _mybir.dt.from_np(a.dtype), kind="ExternalInput").ap())
    shape = inputs["L0_attn_x"].shape
    args.append(nc.dram_tensor("out_0_dram", shape, _mybir.dt.float32, kind="ExternalOutput").ap())
    build_program(nc, *args)
    r = _run(nc, [arrays], core_ids=[0])
    return r.results[0]["out_0_dram"]
```

```python
from contextlib import ExitStack

import concourse.bass as bass
from concourse import mybir

F32 = mybir.dt.float32
F16 = mybir.dt.float16
BF16 = mybir.dt.bfloat16
I32 = mybir.dt.int32
ALU = mybir.AluOpType
ACT = mybir.ActivationFunctionType
AX = mybir.AxisListType

P = 128
EPS_LN = 1e-5
EPS_L2 = 1e-6
EPS_MS = 1e-6
EPS_RMS = 1e-5
LIMIT = 7.0
ALPHA = 1.702
GUARD = -25.0
FAR = float(1 << 20)


def build_program(nc, x, W_qkv, conv_w, W_z, W_b, W_a, dt_bias, A_log, W_out,
                  norm_scale, gate_w, gate_b, mlp1_w, mlp1_b, mlp2_w, mlp2_b, out):
    NB, T, D = x.shape
    H = W_a.shape[0]
    HD = D // H
    K = conv_w.shape[2]
    E = mlp1_w.shape[0]
    HID = mlp2_w.shape[1]
    C = T // P
    N = NB * T
    NT = N // P
    TOP = 2
    W = P + 2
    REGION = N + P
    TILES = (TOP * N + E * (P - 1)) // P + 1
    TILES += TILES % 2
    SPARE = TILES - TOP * NT
    assert D == P and T == 512 and HD == 8 and K == 4 and 2 * HID == 512 and NB % 2 == 0

    rows = nc.dram_tensor("routed_rows", [E * REGION + SPARE * P, W], F32, kind="Internal").ap()
    results = nc.dram_tensor("expert_results", [TOP * N, P], F32, kind="Internal").ap()

    xv = x.rearrange("b (c p) d -> p (b c) d", p=P)
    ov = out.rearrange("b (c p) d -> p (b c) d", p=P)
    rv = results.rearrange("(k n p) d -> p k n d", k=TOP, p=P)

    with ExitStack() as ctx:
        def sb(name, shape, dt=F32):
            return ctx.enter_context(nc.sbuf_tensor(name, shape, dt))

        def sem(name):
            return ctx.enter_context(nc.semaphore(name))

        def sems(names):
            return {n: sem(n) for n in names.split()}

        bank = [ctx.enter_context(nc.psum_tensor(f"bank{i}", [P, 512], F32)) for i in range(8)]
        B_T, B_P0, B_P1, B_N, B_B0, B_B1, B_O, B_W = bank

        X = sb("X", [P, NT, P])
        NORM3 = sb("NORM3", [P, NT, 2])
        w1hi = sb("w1hi", [P, E, 512], F16)
        w1lo = sb("w1lo", [P, E, 512], F16)
        w2hi = sb("w2hi", [P, E, 2, P], F16)
        w2lo = sb("w2lo", [P, E, 2, P], F16)
        b1p = sb("b1p", [P, E, 512], F16)
        b2p = sb("b2p", [P, E, P], F16)
        ones16 = sb("ones16", [P, P], F16)
        ident = sb("ident", [P, P])
        wchi = sb("wchi", [P, K, 3, P], F16)
        wclo = sb("wclo", [P, K, 3, P], F16)
        wphi = sb("wphi", [P, 3, P], F16)
        wplo = sb("wplo", [P, 3, P], F16)
        woT = sb("woT", [P, P])
        gw = sb("gw", [P, E])
        gb = sb("gb", [P, E])
        block = sb("block", [P, H, HD])
        blockms = sb("blockms", [P, H, HD])
        sel = sb("sel", [P, HD, H, HD], F16)
        red = sb("red", [P, HD, H, HD])
        rep = sb("rep", [H, H, HD])
        hb = sb("hb", [P, 2])
        negA = sb("negA", [P, 1])
        tri = sb("tri", [P, P], BF16)
        ones_b = sb("ones_b", [P, P], BF16)
        rank = sb("rank", [P, C, E])
        region0 = sb("region0", [P, E])
        token = sb("token", [P, C, TOP])
        count = sb("count", [P, E])

        s = sems(
            "x_in w_in const_pool setup_pe setup_act setup_dve wstage bias_row "
            "f_stats f_rstd f_u f_uT f_xhi f_xlo f_pa f_pb f_pv f_pk f_pq f_pz "
            "f_ea f_dec f_eb f_beta f_ev f_sv f_ek f_sk f_eq f_sq f_ez f_sz f_vs f_vb f_ks f_qs f_zs "
            "f_vhi f_vlo f_k2 f_q2 f_nk f_nq f_lk f_lq f_rk f_rq f_kn f_qn "
            "e_o2 e_no e_lo e_ro e_og e_gz e_wo e_st2 e_rs2 e_y e_x1 e_st3 e_rs3 e_ms e_rr e_tsc e_t e_t2 "
            "e_tT e_tTs e_lg e_top e_pd e_p1 e_mask e_pos e_slot e_meta "
        )
        s_bc = [sem(f"s_bc{v}") for v in range(2)]
        s_kv, s_scan, s_qs, s_red = sem("s_kv"), sem("s_scan"), sem("s_qs"), sem("s_red")
        r_chain = sem("r_chain")
        s_sent = [sem(f"s_sent{p}") for p in range(2)]
        passed = sem("passed")

        def sent(n, p):
            return 8 * C * TOP * (n - 1 - p)

        def fence(eng, semaphore, n):
            if isinstance(n, int) and n <= 0:
                return
            eng.wait_ge(semaphore, n)
            eng.sem_inc(passed, 1)

        def after(eng, semaphore, n):
            if isinstance(n, int) and n <= 0:
                return
            eng.wait_ge(semaphore, n)

        with ExitStack() as stage:
            def st(name, shape, dt=F32):
                return stage.enter_context(nc.sbuf_tensor(name, shape, dt))

            wq = st("wq", [P, 3, P])
            cw = st("cw", [P, 3, K])
            wt = st("wt", [P, K, 3, P])
            wz = st("wz", [P, P])
            wo = st("wo", [P, P])
            wab = st("wab", [H, 2, P])
            hb0 = st("hb0", [H, 2])
            ns = st("ns", [P, 1])
            gw0 = st("gw0", [P, E])
            w1 = st("w1", [P, E, 512])
            w2 = st("w2", [P, E, 2, P])
            b1 = st("b1", [1, E, 512])
            b2 = st("b2", [1, E, P])
            b1l = st("b1l", [1, E, 512], F16)
            b2l = st("b2l", [1, E, P], F16)
            pad = st("pad", [P, W])

            with nc.Block() as blk:
                @blk.sync
                def _(sp):
                    loads = [
                        (wq[:], W_qkv.rearrange("(g p) d -> p g d", p=P)),
                        (cw[:], conv_w.rearrange("(g p) o k -> p g (o k)", p=P)),
                        (wz[:], W_z), (wo[:], W_out), (wab[:, 0, :], W_a), (wab[:, 1, :], W_b),
                        (hb0[:, 0:1], dt_bias.rearrange("(h a) -> h a", a=1)),
                        (hb0[:, 1:2], A_log.rearrange("(h a) -> h a", a=1)),
                        (ns[:], norm_scale.rearrange("(d a) -> d a", a=1)),
                        (gw0[:], gate_w), (gb[:], gate_b.rearrange("(a e) -> a e", a=1).to_broadcast([P, E])),
                        (w1[:], mlp1_w.rearrange("e d f -> d e f")),
                        (w2[:], mlp2_w.rearrange("e (c p) d -> p e c d", p=P)),
                        (b1[:], mlp1_b.rearrange("(a e) f -> a e f", a=1)),
                        (b2[:], mlp2_b.rearrange("(a e) f -> a e f", a=1)),
                    ]
                    assert len(loads) == 15
                    for to, of in loads:
                        sp.dma_start(to, of).then_inc(s["w_in"], 16)
                    for q in range(4):
                        a, b = q * NT // 4, (q + 1) * NT // 4
                        sp.dma_start(X[:, a:b, :], xv[:, a:b, :]).then_inc(s["x_in"], 16)
                    sp.wait_ge(s["setup_dve"], 3)
                    sp.dma_start(b1p[1:2], b1l[:]).then_inc(s["bias_row"], 16)
                    sp.dma_start(b2p[1:2], b2l[:]).then_inc(s["bias_row"], 16)
                    sp.wait_ge(s["const_pool"], 2)
                    for n in range(SPARE):
                        a = E * REGION + n * P
                        sp.dma_start(rows[a:a + P, :], pad[:]).then_inc(s["bias_row"], 16)
                    sp.wait_ge(s["bias_row"], 16 * (2 + SPARE))
                    sp.wait_ge(s["w_in"], 16 * len(loads))
                    sp.wait_ge(s["x_in"], 64)

                @blk.gpsimd
                def _(pool):
                    n = 0

                    def step(ins):
                        nonlocal n
                        n += 1
                        ins.then_inc(s["wstage"], 1)

                    step(pool.memset(pad[:], 0.0))
                    pool.wait_ge(s["wstage"], n)
                    pool.memset(pad[:, P + 1:P + 2], FAR).then_inc(s["const_pool"], 2)
                    step(pool.memset(ident[:], 0.0))
                    step(pool.memset(block[:], 1.0))
                    step(pool.memset(sel[:], 0.0))
                    step(pool.memset(red[:], 0.0))
                    step(pool.memset(rep[:], 1.0))
                    step(pool.memset(ones_b[:], 1.0))
                    step(pool.memset(tri[:], 1.0))
                    step(pool.memset(ones16[:], 1.0))
                    step(pool.memset(b1p[:], 0.0))
                    step(pool.memset(b2p[:], 0.0))
                    step(pool.memset(count[:], 0.0))
                    pool.wait_ge(s["wstage"], n)
                    step(pool.affine_select(out=ident[:], in_=ident[:], compare_op=ALU.not_equal, fill=1.0,
                                            base=0, pattern=[[-1, P]], channel_multiplier=1))
                    step(pool.affine_select(out=block[:], in_=block[:], compare_op=ALU.is_ge, fill=0.0,
                                            base=0, pattern=[[-HD, H], [0, HD]], channel_multiplier=1))
                    step(pool.affine_select(out=rep[:], in_=rep[:], compare_op=ALU.is_equal, fill=0.0,
                                            base=0, pattern=[[-1, H], [0, HD]], channel_multiplier=1))
                    step(pool.affine_select(out=tri[:], in_=tri[:], compare_op=ALU.is_gt, fill=0.0,
                                            base=0, pattern=[[1, P]], channel_multiplier=-1))
                    for v in range(HD):
                        step(pool.affine_select(out=sel[:, v], in_=sel[:, v], compare_op=ALU.not_equal, fill=1.0,
                                                base=-v, pattern=[[-HD, H], [0, HD]], channel_multiplier=1))
                    step(pool.iota(rank[:], pattern=[[0, C], [-1, E]], base=E, channel_multiplier=0,
                                   allow_small_or_imprecise_dtypes=True))
                    for e in range(E):
                        step(pool.memset(region0[:, e:e + 1], float(e * REGION)))
                    for k in range(TOP):
                        step(pool.iota(token[:, :, k:k + 1], pattern=[[P, C], [0, 1]], base=k * N,
                                       channel_multiplier=1, allow_small_or_imprecise_dtypes=True))
                    pool.wait_ge(s["wstage"], n)
                    step(pool.affine_select(out=block[:], in_=block[:], compare_op=ALU.is_ge, fill=0.0,
                                            base=HD - 1, pattern=[[HD, H], [0, HD]], channel_multiplier=-1))
                    pool.wait_ge(s["wstage"], n)
                    for v in range(HD):
                        step(pool.tensor_copy(red[:, v, :, v:v + 1], block[:, :, v:v + 1]))
                    step(pool.tensor_scalar(blockms[:], block[:], 1.0 / HD, None, ALU.mult))
                    pool.wait_ge(s["wstage"], n)
                    pool.memset(ones16[:, 0:1], 1.0).then_inc(s["const_pool"], 1)

                @blk.vector
                def _(dve):
                    dve.wait_ge(s["w_in"], 16 * 15)
                    for j in range(K):
                        for g in range(3):
                            dve.tensor_scalar(wt[:, j, g, :], wq[:, g, :], cw[:, g, j:j + 1], None, ALU.mult)
                    dve.tensor_scalar(gw[:], gw0[:], ns[:, 0:1], None, ALU.mult)
                    dve.tensor_scalar(w1[:], w1[:], ns[:, 0:1], None, ALU.mult).then_inc(s["setup_dve"], 1)
                    dve.wait_ge(s["const_pool"], 3)
                    dve.wait_ge(s["setup_dve"], 1)
                    dve.tensor_copy(b2p[0:1], b2[:])
                    for h in range(2):
                        last = dve.tensor_copy(b1p[0:1, :, h * HID:(h + 1) * HID],
                                               b1[:, :, h:512:2])
                    last.then_inc(s["setup_dve"], 1)
                    dve.wait_ge(s["setup_dve"], 2)
                    dve.tensor_tensor(b2l[:], b2[:], b2p[0:1], ALU.subtract)
                    for h in range(2):
                        last = dve.tensor_tensor(b1l[:, :, h * HID:(h + 1) * HID], b1[:, :, h:512:2],
                                                 b1p[0:1, :, h * HID:(h + 1) * HID], ALU.subtract)
                    last.then_inc(s["setup_dve"], 1)
                    dve.wait_ge(s["setup_act"], 3)
                    for h in range(2):
                        cut = slice(h * HID, (h + 1) * HID)
                        dve.tensor_tensor(w1lo[:, :, cut], w1[:, :, h:512:2], w1hi[:, :, cut], ALU.subtract)
                    dve.tensor_tensor(w2lo[:], w2[:], w2hi[:], ALU.subtract)
                    for j in range(K):
                        dve.wait_ge(s["setup_act"], 4 + j)
                        dve.tensor_tensor(wclo[:, j], bank[j][:, 0:3 * P], wchi[:, j], ALU.subtract)
                    dve.wait_ge(s["setup_act"], 4 + K)
                    dve.tensor_tensor(wplo[:], bank[4][:, 0:3 * P], wphi[:], ALU.subtract)

                @blk.scalar
                def _(act):
                    act.preload_act_table_set("natural_log_exp_and_others")
                    act.wait_ge(s["setup_dve"], 1)
                    for h in range(2):
                        act.activation(w1hi[:, :, h * HID:(h + 1) * HID], w1[:, :, h:512:2],
                                       ACT.Copy).then_inc(s["setup_act"], 1)
                    act.activation(w2hi[:], w2[:], ACT.Copy).then_inc(s["setup_act"], 1)
                    for j in range(K):
                        act.wait_ge(s["setup_pe"], j + 1)
                        act.activation(wchi[:, j], bank[j][:, 0:3 * P], ACT.Copy).then_inc(s["setup_act"], 1)
                    act.wait_ge(s["setup_pe"], K + 1)
                    act.activation(wphi[:], bank[4][:, 0:3 * P], ACT.Copy).then_inc(s["setup_act"], 1)
                    act.wait_ge(s["setup_pe"], K + 2)
                    act.activation(woT[:], bank[5][:, 0:P], ACT.Copy)
                    act.activation(hb[:], bank[5][:, P:P + 2], ACT.Copy).then_inc(s["setup_act"], 1)
                    act.wait_ge(s["setup_act"], 5 + K)
                    act.activation(negA[:], hb[:, 1:2], ACT.Exp).then_inc(s["setup_act"], 1)
                    act.wait_ge(s["setup_act"], 6 + K)
                    act.activation(negA[:], negA[:], ACT.Copy, scale=-1.0).then_inc(s["setup_act"], 1)

                @blk.tensor
                def _(pe):
                    pe.wait_ge(s["const_pool"], 3)
                    pe.wait_ge(s["setup_dve"], 1)
                    for j in range(K):
                        for g in range(3):
                            last = pe.transpose(bank[j][:, g * P:(g + 1) * P], wt[:, j, g, :], ident[:])
                        last.then_inc(s["setup_pe"], 1)
                    for a in range(2):
                        pe.matmul(bank[4][:, a * P:(a + 1) * P], wab[:, a, :],
                                  rep[:].rearrange("h a b -> h (a b)"), start=True, stop=True)
                    pe.transpose(bank[4][:, 2 * P:3 * P], wz[:], ident[:]).then_inc(s["setup_pe"], 1)
                    pe.transpose(bank[5][:, 0:P], wo[:], ident[:])
                    pe.matmul(bank[5][:, P:P + 2], rep[:].rearrange("h a b -> h (a b)"), hb0[:],
                              start=True, stop=True).then_inc(s["setup_pe"], 1)

        with ExitStack() as stage:
            def st(name, shape, dt=F32):
                return stage.enter_context(nc.sbuf_tensor(name, shape, dt))

            stats = st("stats", [P, C, 6])
            mv1 = st("mv1", [P, C, 2])
            rs1 = st("rs1", [P, C])
            U = st("U", [P, C, P])
            xhi = st("xhi", [P, 2, K - 1 + T], F16)
            xlo = st("xlo", [P, 2, K - 1 + T], F16)
            dec = st("dec", [P, 2, T])
            beta = st("beta", [P, T])
            sg = [st(f"sg{i}", [P, T]) for i in range(4)]
            vs, vb, ks, qs, sq1, sq2 = (st(n, [P, T]) for n in ("vs", "vb", "ks", "qs", "sq1", "sq2"))
            rk, rq = st("rk", [P, T]), st("rq", [P, T])
            kn, qn, zs = (st(n, [P, 2, T]) for n in ("kn", "qn", "zs"))
            vhi = st("vhi", [P, 2, T], F16)
            vlo = st("vlo", [P, 2, T], F16)
            kv = st("kv", [P, 2, T])
            Sv = st("Sv", [P, 2, T])
            qS = st("qS", [P, 2, T])
            osq, ro, og, gz = (st(n, [P, T]) for n in ("osq", "ro", "og", "gz"))
            st2 = st("st2", [P, C, 6])
            mv2 = st("mv2", [P, C, 2])
            rs2 = st("rs2", [P, C])
            st3 = st("st3", [P, C, 6])
            mv3 = st("mv3", [P, C, 2])
            rs3 = st("rs3", [P, C])
            yn = st("yn", [P, C, P])
            ms, rr, tsc = st("ms", [P, C]), st("rr", [P, C]), st("tsc", [P, C])
            tr = st("tr", [P, 2, C, TOP, W])
            tTs = st("tTs", [P, T])
            lg = st("lg", [P, C, E])
            lg2 = st("lg2", [P, C, E])
            eq, one1, one2 = st("eq", [P, C, E]), st("one1", [P, C, E]), st("one2", [P, C, E])
            mask = st("mask", [P, C, E], BF16)
            place = st("place", [P, C, E])
            m1, m2, wm, pd, p0 = (st(n, [P, C]) for n in ("m1", "m2", "wm", "pd", "p0"))
            slot = st("slot", [P, 2, C, TOP], I32)
            slotf = st("slotf", [P, C, TOP])
            dest = st("dest", [P, C, TOP])

            NR = 19

            def F_dve_a(dve, n, p, b):
                if isinstance(b, int):
                    dve.wait_ge(s["x_in"], 64)
                after(dve, s["f_rstd"], n - 1)
                for c in range(C):
                    dve.bn_stats(stats[:, c, :], X[:, bass.ds(b * C + c, 1), :]).then_inc(s["f_stats"], 1)
                fence(dve, s["f_stats"], n * 8 - 4)
                for c in range(C):
                    dve.bn_aggr(mv1[:, c, :], stats[:, c, :]).then_inc(s["f_stats"], 1)

            def F_dve_b(dve, n, p, b):
                dve.wait_ge(s["f_rstd"], n)
                after(dve, s["f_uT"], n - 1)
                for c in range(C):
                    last = dve.tensor_scalar(U[:, c, :], X[:, bass.ds(b * C + c, 1), :], mv1[:, c, 0:1],
                                             rs1[:, c:c + 1], ALU.subtract, ALU.mult)
                last.then_inc(s["f_u"], 1)

            def F_dve_c(dve, n, p):
                dve.wait_ge(s["f_xhi"], n)
                after(dve, s["f_pz"], n - 2)
                dve.tensor_tensor(xlo[:, p, K - 1:], B_T[:], xhi[:, p, K - 1:], ALU.subtract).then_inc(s["f_xlo"], 1)

            def F_dve_v(dve, n, p):
                dve.wait_ge(s["f_sv"], n)
                dve.tensor_tensor(vs[:], B_P0[:], sg[0][:], ALU.mult).then_inc(s["f_vs"], 1)
                dve.wait_ge(s["f_vs"], n)
                dve.wait_ge(s["f_beta"], 2 * n)
                dve.tensor_tensor(vb[:], vs[:], beta[:], ALU.mult).then_inc(s["f_vb"], 1)

            def F_dve_k(dve, n, p):
                dve.wait_ge(s["f_sk"], n)
                dve.tensor_tensor(ks[:], B_P1[:], sg[1][:], ALU.mult).then_inc(s["f_ks"], 1)

            def F_dve_q(dve, n, p):
                dve.wait_ge(s["f_sq"], n)
                dve.tensor_tensor(qs[:], B_P0[:], sg[2][:], ALU.mult).then_inc(s["f_qs"], 1)
                dve.wait_ge(s["f_vhi"], n)
                dve.tensor_tensor(vlo[:, p], vb[:], vhi[:, p], ALU.subtract).then_inc(s["f_vlo"], 1)

            def F_dve_z(dve, n, p):
                dve.wait_ge(s["f_sz"], n)
                dve.tensor_tensor(zs[:, p], B_P1[:], sg[3][:], ALU.mult).then_inc(s["f_zs"], 1)

            def F_dve_kn(dve, n, p):
                dve.wait_ge(s["f_rk"], n)
                dve.tensor_tensor(kn[:, p], ks[:], rk[:], ALU.mult).then_inc(s["f_kn"], 1)

            def F_dve_qn(dve, n, p):
                dve.wait_ge(s["f_rq"], n)
                after(dve, s_qs, (n - 2) * HD)
                dve.tensor_tensor(qn[:, p], qs[:], rq[:], ALU.mult).then_inc(s["f_qn"], 1)

            def F_act(act, n, p):
                act.wait_ge(s["f_stats"], n * 8)
                after(act, s["f_u"], n - 1)
                act.activation(rs1[:], mv1[:, :, 1], ACT.Ln, bias=epsc[:, 0:1]).then_inc(s["f_ea"], 1)
                act.wait_ge(s["f_ea"], n * 2 - 1)
                act.activation(rs1[:], rs1[:], ACT.Exp, scale=-0.5).then_inc(s["f_rstd"], 1)
            def F_act_x(act, n, p):
                act.wait_ge(s["f_uT"], n)
                after(act, s["f_pz"], n - 2)
                act.activation(xhi[:, p, K - 1:], B_T[:], ACT.Copy).then_inc(s["f_xhi"], 1)

            def F_act_b(act, n, p):
                act.wait_ge(s["f_pa"], n)
                after(act, s_scan, (n - 2) * HD)
                act.activation(dec[:, p], B_P0[:], ACT.Exp, bias=hb[:, 0:1]).then_inc(s["f_ea"], 1)
                act.wait_ge(s["f_pb"], n)
                after(act, s["f_vb"], n - 1)
                act.activation(beta[:], B_P1[:], ACT.Exp, scale=-1.0).then_inc(s["f_eb"], 1)
                act.wait_ge(s["f_ea"], n * 2)
                act.activation(dec[:, p], dec[:, p], ACT.Ln, bias=1.0).then_inc(s["f_dec"], 1)
                act.wait_ge(s["f_eb"], n)
                act.activation(beta[:], beta[:], ACT.Ln, bias=1.0).then_inc(s["f_beta"], 1)
                act.wait_ge(s["f_dec"], 2 * n - 1)
                act.activation(dec[:, p], dec[:, p], ACT.Exp, scale=negA[:, 0:1]).then_inc(s["f_dec"], 1)
                act.wait_ge(s["f_beta"], 2 * n - 1)
                act.activation(beta[:], beta[:], ACT.Exp, scale=-1.0).then_inc(s["f_beta"], 1)

            def sigmoid(act, n, ready, src, used, link, done, to):
                act.wait_ge(ready, n)
                after(act, used, n - 1)
                act.activation(to[:], src[:], ACT.Exp, scale=-1.0).then_inc(link, 1)
                act.wait_ge(link, 2 * n - 1)
                act.activation(to[:], to[:], ACT.Ln, bias=1.0).then_inc(link, 1)
                act.wait_ge(link, 2 * n)
                act.activation(to[:], to[:], ACT.Exp, scale=-1.0).then_inc(done, 1)

            def F_act_v(act, n, p):
                sigmoid(act, n, s["f_pv"], B_P0, s["f_vs"], s["f_ev"], s["f_sv"], sg[0])

            def F_act_k(act, n, p):
                sigmoid(act, n, s["f_pk"], B_P1, s["f_ks"], s["f_ek"], s["f_sk"], sg[1])

            def F_act_q(act, n, p):
                act.wait_ge(s["f_vb"], n)
                after(act, s_bc[1], (n - 2) * (HD // 2))
                act.activation(vhi[:, p], vb[:], ACT.Copy).then_inc(s["f_vhi"], 1)
                sigmoid(act, n, s["f_pq"], B_P0, s["f_qs"], s["f_eq"], s["f_sq"], sg[2])

            def F_act_z(act, n, p):
                act.wait_ge(s["f_ks"], n)
                after(act, s["f_nk"], n - 1)
                act.activation(sq1[:], ks[:], ACT.Square).then_inc(s["f_k2"], 1)
                sigmoid(act, n, s["f_pz"], B_P1, s["f_zs"], s["f_ez"], s["f_sz"], sg[3])

            def F_act_nk(act, n, p):
                act.wait_ge(s["f_qs"], n)
                after(act, s["f_nq"], n - 1)
                act.activation(sq2[:], qs[:], ACT.Square).then_inc(s["f_q2"], 1)
                act.wait_ge(s["f_nk"], n)
                after(act, s["f_kn"], n - 1)
                act.activation(rk[:], B_N[:], ACT.Ln, bias=epsc[:, 1:2]).then_inc(s["f_lk"], 1)
                act.wait_ge(s["f_lk"], n)
                act.activation(rk[:], rk[:], ACT.Exp, scale=-0.5).then_inc(s["f_rk"], 1)

            def F_act_nq(act, n, p):
                act.wait_ge(s["f_nq"], n)
                after(act, s["f_qn"], n - 1)
                act.activation(rq[:], B_N[:], ACT.Ln, bias=epsc[:, 1:2]).then_inc(s["f_lq"], 1)
                act.wait_ge(s["f_lq"], n)
                act.activation(rq[:], rq[:], ACT.Exp, scale=-0.5, bias=epsc[:, 2:3]).then_inc(s["f_rq"], 1)

            def F_pe_a(pe, n, p):
                pe.wait_ge(s["f_u"], n)
                after(pe, s["e_slot"], n - 4)
                for c in range(C):
                    last = pe.transpose(B_T[:, c * P:(c + 1) * P], U[:, c, :], ident[:])
                last.then_inc(s["f_uT"], 1)

            def project(pe, to, hi, lo, xh, xl, first, last):
                pe.matmul(to, hi, xh, start=first, stop=False)
                pe.matmul(to, hi, xl, start=False, stop=False)
                return pe.matmul(to, lo, xh, start=False, stop=last)

            now = slice(K - 1, K - 1 + T)

            def F_pe_ab(pe, n, p):
                pe.wait_ge(s["f_xhi"], n)
                pe.wait_ge(s["f_xlo"], n)
                after(pe, s["f_qs"], n - 1)
                project(pe, B_P0[:], wphi[:, 0], wplo[:, 0], xhi[:, p, now], xlo[:, p, now],
                        True, True).then_inc(s["f_pa"], 1)
                after(pe, s["f_zs"], n - 1)
                project(pe, B_P1[:], wphi[:, 1], wplo[:, 1], xhi[:, p, now], xlo[:, p, now],
                        True, True).then_inc(s["f_pb"], 1)

            def conv(pe, p, to, g, done):
                for j in range(K):
                    last = project(pe, to[:], wchi[:, j, g], wclo[:, j, g], xhi[:, p, j:j + T],
                                   xlo[:, p, j:j + T], j == 0, j == K - 1)
                last.then_inc(done, 1)

            def F_pe_v(pe, n, p):
                pe.wait_ge(s["f_ea"], n * 2)
                conv(pe, p, B_P0, 2, s["f_pv"])

            def F_pe_k(pe, n, p):
                pe.wait_ge(s["f_eb"], n)
                conv(pe, p, B_P1, 1, s["f_pk"])

            def F_pe_q(pe, n, p):
                pe.wait_ge(s["f_vs"], n)
                conv(pe, p, B_P0, 0, s["f_pq"])

            def F_pe_z(pe, n, p):
                pe.wait_ge(s["f_ks"], n)
                project(pe, B_P1[:], wphi[:, 2], wplo[:, 2], xhi[:, p, now], xlo[:, p, now],
                        True, True).then_inc(s["f_pz"], 1)

            def F_pe_nk(pe, n, p):
                pe.wait_ge(s["f_k2"], n)
                after(pe, s["e_lo"], n - 2)
                pe.matmul(B_N[:], block[:].rearrange("p a b -> p (a b)"), sq1[:],
                          start=True, stop=True).then_inc(s["f_nk"], 1)

            def F_pe_nq(pe, n, p):
                pe.wait_ge(s["f_q2"], n)
                pe.wait_ge(s["f_lk"], n)
                pe.matmul(B_N[:], block[:].rearrange("p a b -> p (a b)"), sq2[:],
                          start=True, stop=True).then_inc(s["f_nq"], 1)

            BC = (B_B0, B_B1)

            def S_pe(pe, n, p, v):
                base = (n - 1) * HD

                def bcast(v):
                    after(pe, s_kv, base + v - 1)
                    lhs = sel[:, v].rearrange("p a b -> p (a b)")
                    pe.matmul(BC[v % 2][:], lhs, vhi[:, p], start=True, stop=False)
                    pe.matmul(BC[v % 2][:], lhs, vlo[:, p], start=False, stop=True).then_inc(s_bc[v % 2], 1)

                if v < 0:
                    pe.wait_ge(s["f_vhi"], n)
                    pe.wait_ge(s["f_vlo"], n)
                    bcast(0)
                    bcast(1)
                    return
                if v + 2 < HD:
                    bcast(v + 2)
                pe.wait_ge(s_qs, base + v + 1)
                if v == 0:
                    after(pe, s["e_og"], n - 1)
                pe.matmul(B_O[:], red[:, v].rearrange("p a b -> p (a b)"), qS[:, v % 2],
                          start=v == 0, stop=v == HD - 1).then_inc(s_red, 1)

            def S_dve(dve, n, p, v):
                base = (n - 1) * HD

                def product(v):
                    dve.wait_ge(s_bc[v % 2], (n - 1) * (HD // 2) + v // 2 + 1)
                    after(dve, s_scan, base + v - 1)
                    dve.tensor_tensor(kv[:, v % 2], BC[v % 2][:], kn[:, p], ALU.mult).then_inc(s_kv, 1)

                if v < 0:
                    dve.wait_ge(s["f_kn"], n)
                    dve.wait_ge(s["f_dec"], 2 * n)
                    product(0)
                    return
                if v + 1 < HD:
                    product(v + 1)
                dve.wait_ge(s_kv, base + v + 1)
                after(dve, s_qs, base + v - 1)
                dve.tensor_tensor_scan(Sv[:, v % 2], dec[:, p], kv[:, v % 2], 0.0,
                                       ALU.mult, ALU.add).then_inc(s_scan, 1)

            def S_pool(pool, n, p, v):
                base = (n - 1) * HD
                if v == 0:
                    pool.wait_ge(s["f_qn"], n)
                pool.wait_ge(s_scan, base + v + 1)
                after(pool, s_red, base + v - 1)
                pool.tensor_tensor(qS[:, v % 2], Sv[:, v % 2], qn[:, p], ALU.mult).then_inc(s_qs, 1)

            def E_act_a(act, n, p):
                act.wait_ge(s_red, n * HD)
                after(act, s["e_no"], n - 1)
                act.activation(osq[:], B_O[:], ACT.Square).then_inc(s["e_o2"], 1)

            def E_act_r(act, n, p):
                act.wait_ge(s["e_no"], n)
                after(act, s["e_og"], n - 1)
                act.activation(ro[:], B_N[:], ACT.Ln, bias=epsc[:, 1:2]).then_inc(s["e_lo"], 1)
                act.wait_ge(s["e_lo"], n)
                act.activation(ro[:], ro[:], ACT.Exp, scale=-0.5).then_inc(s["e_ro"], 1)

            def E_pe_a(pe, n, p):
                pe.wait_ge(s["e_o2"], n)
                pe.wait_ge(s["f_lq"], min(n + 1, NB) if isinstance(n, int) else n + 1)
                pe.matmul(B_N[:], blockms[:].rearrange("p a b -> p (a b)"), osq[:],
                          start=True, stop=True).then_inc(s["e_no"], 1)

            def E_dve_a(dve, n, p):
                dve.wait_ge(s["e_ro"], n)
                dve.wait_ge(s["f_zs"], n)
                after(dve, s["e_gz"], n - 1)
                dve.tensor_tensor(og[:], B_O[:], ro[:], ALU.mult).then_inc(s["e_og"], 1)
                dve.wait_ge(s["e_og"], n)
                after(dve, s["e_wo"], n - 1)
                dve.tensor_tensor(gz[:], og[:], zs[:, p], ALU.mult).then_inc(s["e_gz"], 1)

            def E_pe_b(pe, n, p):
                pe.wait_ge(s["e_gz"], n)
                after(pe, s["e_y"], n - 1)
                for c in range(C):
                    last = pe.matmul(B_W[:, c * P:(c + 1) * P], gz[:, c * P:(c + 1) * P], woT[:],
                                     start=True, stop=True)
                last.then_inc(s["e_wo"], 1)

            def E_dve_b(dve, n, p):
                dve.wait_ge(s["e_wo"], n)
                for c in range(C):
                    dve.bn_stats(st2[:, c, :], B_W[:, c * P:(c + 1) * P]).then_inc(s["e_st2"], 1)
                after(dve, s["e_rs2"], 2 * (n - 1))
                fence(dve, s["e_st2"], n * 8 - 4)
                for c in range(C):
                    dve.bn_aggr(mv2[:, c, :], st2[:, c, :]).then_inc(s["e_st2"], 1)

            def E_act_b(act, n, p):
                act.wait_ge(s["e_st2"], n * 8)
                after(act, s["e_y"], n - 1)
                act.activation(rs2[:], mv2[:, :, 1], ACT.Ln, bias=epsc[:, 0:1]).then_inc(s["e_rs2"], 1)
                act.wait_ge(s["e_rs2"], 2 * n - 1)
                act.activation(rs2[:], rs2[:], ACT.Exp, scale=-0.5).then_inc(s["e_rs2"], 1)

            def E_dve_c(dve, n, p):
                dve.wait_ge(s["e_rs2"], 2 * n)
                after(dve, s["e_x1"], n - 1)
                for c in range(C):
                    last = dve.tensor_scalar(yn[:, c, :], B_W[:, c * P:(c + 1) * P], mv2[:, c, 0:1],
                                             rs2[:, c:c + 1], ALU.subtract, ALU.mult)
                last.then_inc(s["e_y"], 1)

            def E_pool_a(pool, n, p, b):
                pool.wait_ge(s["e_y"], n)
                at = X[:, bass.ds(b * C, C), :]
                pool.tensor_tensor(at, at, yn[:], ALU.add).then_inc(s["e_x1"], 1)

            def E_dve_d(dve, n, p, b):
                dve.wait_ge(s["e_x1"], n)
                for c in range(C):
                    dve.bn_stats(st3[:, c, :], X[:, bass.ds(b * C + c, 1), :]).then_inc(s["e_st3"], 1)
                after(dve, s["e_t"], n - 1)
                fence(dve, s["e_st3"], n * 8 - 4)
                for c in range(C):
                    dve.bn_aggr(mv3[:, c, :], st3[:, c, :]).then_inc(s["e_st3"], 1)

            def E_act_c(act, n, p, b):
                act.wait_ge(s["e_st3"], n * 8)
                after(act, s["e_t"], n - 1)
                act.activation(rs3[:], mv3[:, :, 1], ACT.Ln, bias=epsc[:, 0:1]).then_inc(s["e_rs3"], 1)
                act.wait_ge(s["e_rs3"], 2 * n - 1)
                act.activation(rs3[:], rs3[:], ACT.Exp, scale=-0.5).then_inc(s["e_rs3"], 1)
            def E_act_rr(act, n, p):
                act.wait_ge(s["e_ms"], 2 * n)
                after(act, s["e_tsc"], n - 1)
                act.activation(rr[:], ms[:], ACT.Ln, bias=epsc[:, 0:1]).then_inc(s["e_rr"], 1)
                act.wait_ge(s["e_rr"], 2 * n - 1)
                act.activation(rr[:], rr[:], ACT.Exp, scale=-0.5).then_inc(s["e_rr"], 1)

            def E_dve_e(dve, n, p, b):
                dve.wait_ge(s["e_rs3"], 2 * n)
                dve.tensor_copy(NORM3[:, bass.ds(b * C, C), 0], mv3[:, :, 0])
                dve.tensor_copy(NORM3[:, bass.ds(b * C, C), 1], rs3[:])
                after(dve, s["e_rr"], 2 * (n - 1))
                dve.tensor_tensor(ms[:], rs3[:], rs3[:], ALU.mult).then_inc(s["e_ms"], 1)
                dve.wait_ge(s["e_ms"], 2 * n - 1)
                dve.tensor_tensor(ms[:], ms[:], mv3[:, :, 1], ALU.mult).then_inc(s["e_ms"], 1)
            def E_dve_t(dve, n, p, b):
                dve.wait_ge(s["e_rr"], 2 * n)
                after(dve, s["e_t"], n - 1)
                dve.tensor_tensor(tsc[:], rr[:], rs3[:], ALU.mult).then_inc(s["e_tsc"], 1)
                dve.wait_ge(s["e_tsc"], n)
                after(dve, s_sent[p], sent(n, p))
                after(dve, s["e_t2"], n - 1)
                for c in range(C):
                    last = dve.tensor_scalar(tr[:, p, c, 0, 0:P], X[:, bass.ds(b * C + c, 1), :],
                                             mv3[:, c, 0:1], tsc[:, c:c + 1],
                                             ALU.subtract, ALU.mult)
                last.then_inc(s["e_t"], 1)

            def R_pe_t(pe, n, p):
                pe.wait_ge(s["e_t"], n)
                pe.wait_ge(s["f_xlo"], min(n + 3, NB) if isinstance(n, int) else n + 3)
                for c in range(C):
                    last = pe.transpose(B_T[:, c * P:(c + 1) * P], tr[:, p, c, 0, 0:P], ident[:])
                last.then_inc(s["e_tT"], 1)

            def R_pe_lg(pe, n, p):
                pe.wait_ge(s["e_tTs"], n)
                for c in range(C):
                    last = pe.matmul(B_T[:, c * E:(c + 1) * E], tTs[:, c * P:(c + 1) * P], gw[:],
                                     start=True, stop=True)
                last.then_inc(s["e_lg"], 1)

            def R_act_t(act, n, p):
                act.wait_ge(s["e_tT"], n)
                after(act, s["e_lg"], n - 1)
                act.activation(tTs[:], B_T[:], ACT.Copy).then_inc(s["e_tTs"], 1)

            def E_act_t2(act, n, p):
                act.wait_ge(s["e_t"], n)
                after(act, s_sent[p], sent(n, p))
                act.activation(tr[:, p, :, 1, 0:P], tr[:, p, :, 0, 0:P], ACT.Copy).then_inc(s["e_t2"], 1)

            def R_act_p(act, n, p):
                act.wait_ge(s["e_pd"], n)
                after(act, s["e_meta"], n - 1)
                act.activation(p0[:], pd[:], ACT.Exp).then_inc(s["e_p1"], 1)

            def wide(ap):
                return ap[:].unsqueeze(2).to_broadcast([P, C, E])

            def R_dve(dve, n, p, part):
                link = [(0, 8, 12)[part]]

                def then(ins):
                    link[0] += 1
                    ins.then_inc(r_chain, 1)
                    dve.wait_ge(r_chain, (n - 1) * NR + link[0])

                if part == 0:
                    dve.wait_ge(s["e_lg"], n)
                    after(dve, s["e_pos"], n - 1)
                    then(dve.tensor_tensor(lg[:], B_T[:, 0:C * E].rearrange("p (c e) -> p c e", e=E),
                                           gb[:].unsqueeze(1).to_broadcast([P, C, E]), ALU.add))
                    then(dve.tensor_reduce(m1[:], lg[:], AX.X, ALU.max))
                    then(dve.tensor_tensor(eq[:], lg[:], wide(m1), ALU.is_equal))
                    then(dve.tensor_tensor(eq[:], eq[:], rank[:], ALU.mult))
                    then(dve.tensor_reduce(wm[:], eq[:], AX.X, ALU.max))
                    then(dve.tensor_tensor(one1[:], rank[:], wide(wm), ALU.is_equal))
                    then(dve.scalar_tensor_tensor(lg2[:], one1[:], -3e38, lg[:], ALU.mult, ALU.add))
                    then(dve.tensor_reduce(m2[:], lg2[:], AX.X, ALU.max))
                    after(dve, s["e_p1"], n - 1)
                    dve.tensor_tensor(pd[:], m2[:], m1[:], ALU.subtract).then_inc(s["e_pd"], 1)
                if part == 1:
                    then(dve.tensor_tensor(eq[:], lg2[:], wide(m2), ALU.is_equal))
                    then(dve.tensor_tensor(eq[:], eq[:], rank[:], ALU.mult))
                    then(dve.tensor_reduce(wm[:], eq[:], AX.X, ALU.max))
                    then(dve.tensor_tensor(one2[:], rank[:], wide(wm), ALU.is_equal))
                    dve.tensor_tensor(mask[:], one1[:], one2[:], ALU.add).then_inc(s["e_mask"], 1)
                if part == 2:
                    dve.wait_ge(s["e_p1"], n)
                    then(dve.tensor_scalar(m1[:], p0[:], 1.0, None, ALU.add))
                    then(dve.reciprocal(m2[:], m1[:]))
                    after(dve, s_sent[p], sent(n, p))
                    dve.tensor_copy(tr[:, p, :, 0, P], m2[:])
                    dve.tensor_tensor(tr[:, p, :, 1, P], m2[:], p0[:], ALU.mult)
                    then(dve.tensor_copy(tr[:, p, :, :, P + 1], dest[:]))
                    then(dve.tensor_scalar(dest[:], dest[:], float(T), None, ALU.add))
                    dve.wait_ge(s["e_pos"], n)
                    then(dve.tensor_tensor(place[:], B_T[:, 64:64 + C * E].rearrange("p (c e) -> p c e", e=E),
                                           count[:].unsqueeze(1).to_broadcast([P, C, E]), ALU.add))
                    dve.tensor_tensor(count[:], count[:], B_T[:, 128:128 + E], ALU.add).then_inc(s["e_slot"], 1)
                    dve.tensor_tensor(one1[:], one1[:], place[:], ALU.mult)
                    then(dve.tensor_tensor(one2[:], one2[:], place[:], ALU.mult))
                    dve.tensor_reduce(slotf[:, :, 0], one1[:], AX.X, ALU.add)
                    then(dve.tensor_reduce(slotf[:, :, 1], one2[:], AX.X, ALU.add))
                    dve.tensor_copy(slot[:, p], slotf[:]).then_inc(s["e_meta"], 1)
                    assert link[0] == NR, link[0]

            def R_pe_pos(pe, n, p):
                pe.wait_ge(s["e_mask"], n)
                flat = mask[:].rearrange("p c e -> p (c e)")
                at = B_T[:, 64:64 + C * E]
                pe.matmul(at, tri[:], flat, start=True, stop=True, skip_group_check=True)
                for c in range(1, C):
                    pe.matmul(at[:, c * E:], ones_b[:], flat[:, 0:(C - c) * E],
                              start=False, stop=True, skip_group_check=True)
                for c in range(C):
                    last = pe.matmul(B_T[:, 128:128 + E], ones_b[:], mask[:, c], start=False, stop=True,
                                     skip_group_check=True)
                last.then_inc(s["e_pos"], 1)

            def R_pool(pool, n, p, some):
                pool.wait_ge(s["e_meta"], n)
                fence(pool, s["e_t2"], n)
                for i in some:
                    for c, k in ((i // TOP, i % TOP),):
                        pool.indirect_dma_start(
                            rows, bass.IndirectOffsetOnAxis(ap=slot[:, p, c, k:k + 1], axis=0),
                            tr[:, p, c, k, :], None).then_inc(s_sent[p], 16)

            def iterations(eng, step):
                for k in range(-2, 3):
                    step(k, stages(k), k % 2)
                with eng.Fori(1, NB // 2 - 2) as i:
                    step(2 * i + 1, "ABSER", 1)
                    step(2 * i + 2, "ABSER", 0)
                for k in range(NB - 3, NB + 2):
                    step(k, stages(k), k % 2)

            def stages(k):
                return "".join(x for x, lead in zip("ABSER", (2, 1, 0, -1, -2)) if 0 <= k + lead < NB)

            epsc = st("epsc", [P, 3])
            s_eps = s["const_pool"]

            with nc.Block() as blk:
                @blk.vector
                def _(dve):
                    for i, value in enumerate((EPS_LN, EPS_L2, -0.5 * 2.0794415416798357)):
                        dve.memset(epsc[:, i:i + 1], value)
                    dve.tensor_tensor(count[:], count[:], region0[:], ALU.add)
                    dve.tensor_copy(dest[:], token[:])
                    dve.memset(xhi[:, :, 0:K - 1], 0.0)
                    dve.memset(xlo[:, :, 0:K - 1], 0.0).then_inc(s_eps, 1)
                    dve.wait_ge(s_eps, 4)

                    def step(k, on, par):
                        a, b, c, e, r = k + 3, k + 2, k + 1, k, k - 1
                        if "S" in on:
                            S_dve(dve, c, par, -1)
                        for v in range(HD):
                            if "S" in on:
                                S_dve(dve, c, par, v)
                            if "E" in on:
                                if v == 0:
                                    E_dve_a(dve, e, 1 - par)
                                if v == 2:
                                    E_dve_b(dve, e, 1 - par)
                                if v == 3:
                                    E_dve_c(dve, e, 1 - par)
                                if v == 4:
                                    E_dve_d(dve, e, 1 - par, k - 1)
                                if v == 5:
                                    E_dve_e(dve, e, 1 - par, k - 1)
                                if v == 6:
                                    E_dve_t(dve, e, 1 - par, k - 1)
                            if "R" in on:
                                if 2 <= v <= 4:
                                    R_dve(dve, r, par, v - 2)
                            if "A" in on:
                                if v == 1:
                                    F_dve_a(dve, a, par, k + 2)
                                if v == 3:
                                    F_dve_b(dve, a, par, k + 2)
                                if v == 6:
                                    F_dve_c(dve, a, par)
                            if "B" in on:
                                if v == 3:
                                    F_dve_v(dve, b, 1 - par)
                                if v == 4:
                                    F_dve_k(dve, b, 1 - par)
                                if v == 5:
                                    F_dve_q(dve, b, 1 - par)
                                if v == 6:
                                    F_dve_z(dve, b, 1 - par)
                                if v == 7:
                                    F_dve_kn(dve, b, 1 - par)
                                    F_dve_qn(dve, b, 1 - par)

                    iterations(dve, step)

                @blk.scalar
                def _(act):
                    act.wait_ge(s_eps, 4)

                    def step(k, on, par):
                        a, b, e, r = k + 3, k + 2, k, k - 1
                        if "E" in on:
                            E_act_a(act, e, 1 - par)
                            E_act_r(act, e, 1 - par)
                        if "R" in on:
                            R_act_t(act, r, par)
                        if "B" in on:
                            F_act_b(act, b, 1 - par)
                            F_act_v(act, b, 1 - par)
                        if "A" in on:
                            F_act(act, a, par)
                        if "E" in on:
                            E_act_b(act, e, 1 - par)
                        if "R" in on:
                            R_act_p(act, r, par)
                        if "B" in on:
                            F_act_k(act, b, 1 - par)
                        if "E" in on:
                            E_act_c(act, e, 1 - par, k - 1)
                        if "B" in on:
                            F_act_q(act, b, 1 - par)
                        if "E" in on:
                            E_act_rr(act, e, 1 - par)
                        if "B" in on:
                            F_act_z(act, b, 1 - par)
                        if "A" in on:
                            F_act_x(act, a, par)
                        if "B" in on:
                            F_act_nk(act, b, 1 - par)
                            F_act_nq(act, b, 1 - par)
                        if "E" in on:
                            E_act_t2(act, e, 1 - par)

                    iterations(act, step)

                @blk.tensor
                def _(pe):
                    pe.wait_ge(s_eps, 4)

                    def step(k, on, par):
                        a, b, c, e, r = k + 3, k + 2, k + 1, k, k - 1
                        if "S" in on:
                            S_pe(pe, c, par, -1)
                        for v in range(HD):
                            if "E" in on:
                                if v == 0:
                                    E_pe_a(pe, e, 1 - par)
                                if v == 2:
                                    E_pe_b(pe, e, 1 - par)
                            if "R" in on:
                                if v == 0:
                                    R_pe_t(pe, r, par)
                                if v == 1:
                                    R_pe_lg(pe, r, par)
                                if v == 4:
                                    R_pe_pos(pe, r, par)
                            if "S" in on:
                                S_pe(pe, c, par, v)
                            if "B" in on:
                                if v == 0:
                                    F_pe_ab(pe, b, 1 - par)
                                if v == 1:
                                    F_pe_v(pe, b, 1 - par)
                                if v == 2:
                                    F_pe_k(pe, b, 1 - par)
                                if v == 3:
                                    F_pe_q(pe, b, 1 - par)
                                if v == 5:
                                    F_pe_z(pe, b, 1 - par)
                                if v == 6:
                                    F_pe_nk(pe, b, 1 - par)
                                if v == 7:
                                    F_pe_nq(pe, b, 1 - par)
                            if "A" in on:
                                if v == 5:
                                    F_pe_a(pe, a, par)

                    iterations(pe, step)

                @blk.gpsimd
                def _(pool):
                    def step(k, on, par):
                        c, e, r = k + 1, k, k - 1
                        for v in range(HD):
                            if "S" in on:
                                S_pool(pool, c, par, v)
                            if "E" in on and v == 3:
                                E_pool_a(pool, e, 1 - par, k - 1)
                            if "R" in on:
                                if v >= 5:
                                    R_pool(pool, r, par, ((0, 1, 2), (3, 4, 5), (6, 7))[v - 5])

                    iterations(pool, step)
                    for p in range(2):
                        pool.wait_ge(s_sent[p], 16 * C * TOP * NB // 2)

        tab = sb("tab", [P, 2, TILES], I32)
        with ExitStack() as stage:
            def st(name, shape, dt=F32):
                return stage.enter_context(nc.sbuf_tensor(name, shape, dt))

            cnt, tiles_of, ends, one = (st(n, [P, E]) for n in ("cnt", "tiles_of", "ends", "one"))
            jt = st("jt", [P, E, NT])
            over = st("over", [P, E, NT])
            tj = st("tj", [P, TILES, E])
            le = st("le", [P, TILES, E])
            te, first, tnum, start = (st(n, [P, TILES]) for n in ("te", "first", "tnum", "start"))
            pnum = st("pnum", [P, 1])
            padrow = st("padrow", [P, W])
            padat = st("padat", [P, E], I32)
            t_const, t_chain, t_pad = sem("t_const"), sem("t_chain"), sem("t_pad")

            with nc.Block() as blk:
                @blk.gpsimd
                def _(pool):
                    pool.iota(jt[:], pattern=[[0, E], [P, NT]], base=0, channel_multiplier=0,
                              allow_small_or_imprecise_dtypes=True).then_inc(t_const, 1)
                    pool.iota(tj[:], pattern=[[1, TILES], [0, E]], base=0, channel_multiplier=0,
                              allow_small_or_imprecise_dtypes=True).then_inc(t_const, 1)
                    pool.iota(tnum[:], pattern=[[1, TILES]], base=0, channel_multiplier=0,
                              allow_small_or_imprecise_dtypes=True).then_inc(t_const, 1)
                    pool.iota(pnum[:], pattern=[[0, 1]], base=0, channel_multiplier=1,
                              allow_small_or_imprecise_dtypes=True).then_inc(t_const, 1)
                    pool.memset(one[:], 1.0).then_inc(t_const, 1)
                    pool.memset(padrow[:, 0:P + 1], 0.0)
                    pool.memset(padrow[:, P + 1:W], FAR).then_inc(t_const, 1)
                    pool.wait_ge(t_const, 6)
                    pool.wait_ge(t_chain, 1)
                    for e in range(E):
                        pool.indirect_dma_start(
                            rows, bass.IndirectOffsetOnAxis(ap=padat[:, e:e + 1], axis=0),
                            padrow[:], None).then_inc(t_pad, 16)
                    pool.wait_ge(t_pad, 16 * E)

                @blk.vector
                def _(dve):
                    link = [0]

                    def then(ins):
                        link[0] += 1
                        ins.then_inc(t_chain, 1)
                        dve.wait_ge(t_chain, link[0])

                    dve.wait_ge(t_const, 6)
                    then(dve.tensor_scalar(padat[:], count[:], pnum[:, 0:1], None, ALU.add))
                    then(dve.tensor_tensor(cnt[:], count[:], region0[:], ALU.subtract))
                    then(dve.tensor_tensor(over[:], cnt[:].unsqueeze(2).to_broadcast([P, E, NT]), jt[:], ALU.is_gt))
                    then(dve.tensor_reduce(tiles_of[:], over[:], AX.X, ALU.add))
                    then(dve.tensor_tensor_scan(ends[:], one[:], tiles_of[:], 0.0, ALU.mult, ALU.add))
                    ends_b = ends[:].unsqueeze(1).to_broadcast([P, TILES, E])
                    then(dve.tensor_tensor(le[:], ends_b, tj[:], ALU.is_le))
                    then(dve.tensor_reduce(te[:], le[:], AX.X, ALU.add))
                    then(dve.tensor_tensor(le[:], le[:], ends_b, ALU.mult))
                    then(dve.tensor_reduce(first[:], le[:], AX.X, ALU.max))
                    then(dve.tensor_tensor(first[:], tnum[:], first[:], ALU.subtract))
                    then(dve.tensor_scalar(first[:], first[:], float(P), None, ALU.mult))
                    then(dve.tensor_scalar(start[:], te[:], float(REGION), None, ALU.mult))
                    then(dve.tensor_tensor(tab[:, 0, :], start[:], first[:], ALU.add))
                    then(dve.tensor_scalar(tab[:, 1, :], te[:], float(E - 1), None, ALU.min))

        with ExitStack() as stage:
            def st(name, shape, dt=F32):
                return stage.enter_context(nc.sbuf_tensor(name, shape, dt))

            RING = 4
            UNROLL = 8
            G = st("G", [P, UNROLL, W])
            thi, tlo = st("thi", [P, 2, P], F16), st("tlo", [P, 2, P], F16)
            gate, lin, sig, hid = (st(n, [P, 2, HID]) for n in ("gate", "lin", "sig", "hid"))
            hhi, hlo = st("hhi", [P, 2, 2 * P], F16), st("hlo", [P, 2, 2 * P], F16)
            yw = st("yw", [P, RING, P])
            where, wgt = st("where", [P, UNROLL], I32), st("wgt", [P, UNROLL])
            m = sems("m_T m_hi m_lo m_h m_gate m_lin m_e1 m_e2 m_sig m_gs m_hid m_hT m_hhi m_hlo m_y m_yw "
                     "m_where m_out0 m_out1 m_out2 m_out3")
            m_in = [sem(f"m_in{q}") for q in range(UNROLL)]
            m_out = (m["m_out0"], m["m_out1"], m["m_out2"], m["m_out3"])
            B_H, B_HT, B_Y = (bank[1], bank[2]), (bank[3], bank[4]), (bank[5], bank[6])

            def tiles(eng, step, begin=lambda k: None):
                def single(k):
                    if k % UNROLL == 0:
                        begin(k)
                    step(k, k % UNROLL, *(0 <= k + i < TILES for i in (1, 0, -1, -2, -3)))

                for k in range(-1, UNROLL):
                    single(k)
                with eng.Fori(1, TILES // UNROLL - 1) as r:
                    begin(UNROLL * r)
                    for i in range(UNROLL):
                        step(UNROLL * r + i, i, True, True, True, True, True)
                for k in range(TILES - UNROLL, TILES + 3):
                    single(k)

            def filled(t, q):
                return 2 * (t - q) + 16

            def sent_out(t, q):
                return 4 * (t - q) + 16

            with nc.Block() as blk:
                @blk.sync
                def _(sp):
                    def loads(t):
                        _, at = nc.values_load_multi_w_load_instructions(
                            tab[0:1, 0, bass.ds(t, UNROLL)], engines=[mybir.EngineType.SP],
                            min_val=0, max_val=E * REGION + (SPARE - 1) * P)
                        for q in range(UNROLL):
                            after(sp, m["m_T"], t + q - UNROLL + 1)
                            after(sp, m["m_where"], t + q - UNROLL + 1)
                            sp.dma_start(G[:, q, :], rows[bass.ds(at[q], P), :]).then_inc(m_in[q], 16)

                    loads(0)
                    with sp.Fori(1, TILES // UNROLL) as r:
                        loads(UNROLL * r)

                @blk.tensor
                def _(pe):
                    experts = {}

                    def find(k, first, count):
                        _, values = nc.values_load_multi_w_load_instructions(
                            tab[0:1, 1, bass.ds(k + first, count)], engines=[mybir.EngineType.PE],
                            min_val=0, max_val=E - 1)
                        for i in range(count):
                            experts[first + i] = values[i]

                    def begin(k):
                        first = -3 if not isinstance(k, int) or k >= 3 else 0
                        find(k, first, (0 if isinstance(k, int) and k >= TILES else 1) - first)

                    def transposes(t, q):
                        pe.wait_ge(m_in[q], filled(t, q))
                        after(pe, m["m_lo"], t)
                        pe.transpose(bank[0][:, 0:P], G[:, q, 0:P], ident[:]).then_inc(m["m_T"], 1)

                    def first_product(t, p, e):
                        pe.wait_ge(m["m_lo"], t + 1)
                        pe.wait_ge(m["m_hi"], t + 1)
                        after(pe, m["m_lin"], t - 1)
                        to = B_H[p][:]
                        w_hi = w1hi[:, bass.ds(e, 1), :].rearrange("p a f -> p (a f)")
                        w_lo = w1lo[:, bass.ds(e, 1), :].rearrange("p a f -> p (a f)")
                        bias = b1p[:, bass.ds(e, 1), :].rearrange("p a f -> p (a f)")
                        pe.matmul(to, ones16[:], bias, start=True, stop=False)
                        pe.matmul(to, thi[:, p], w_hi, start=False, stop=False)
                        pe.matmul(to, thi[:, p], w_lo, start=False, stop=False)
                        pe.matmul(to, tlo[:, p], w_hi, start=False, stop=True).then_inc(m["m_h"], 1)

                    def hidden_transposes(t, p):
                        pe.wait_ge(m["m_hid"], t + 1)
                        after(pe, m["m_hlo"], t - 1)
                        pe.transpose(B_HT[p][:, 0:P], hid[:, p, 0:P], ident[:])
                        pe.transpose(B_HT[p][:, P:2 * P], hid[:, p, P:2 * P], ident[:]).then_inc(m["m_hT"], 1)

                    def second_product(t, p, e):
                        to = B_Y[p][:, 0:P]
                        after(pe, m["m_yw"], t - 1)
                        pe.matmul(to, ones16[:], b2p[:, bass.ds(e, 1), :].rearrange("p a f -> p (a f)"),
                                  start=True, stop=False)
                        pe.wait_ge(m["m_hhi"], t + 1)
                        pe.wait_ge(m["m_hlo"], t + 1)
                        for c in range(2):
                            hi, lo = hhi[:, p, c * P:(c + 1) * P], hlo[:, p, c * P:(c + 1) * P]
                            w_hi = w2hi[:, bass.ds(e, 1), c, :].rearrange("p a f -> p (a f)")
                            w_lo = w2lo[:, bass.ds(e, 1), c, :].rearrange("p a f -> p (a f)")
                            pe.matmul(to, hi, w_hi, start=False, stop=False)
                            pe.matmul(to, hi, w_lo, start=False, stop=False)
                            last = pe.matmul(to, lo, w_hi, start=False, stop=c == 1)
                        last.then_inc(m["m_y"], 1)

                    def step(k, q, ahead, now, back1, back2, back3):
                        if ahead:
                            transposes(k + 1, (q + 1) % UNROLL)
                        if now:
                            first_product(k, q % 2, experts[q])
                        if back2:
                            hidden_transposes(k - 2, q % 2)
                        if back3:
                            second_product(k - 3, (q + 1) % 2, experts[q - 3])
                        if ahead and q + 1 < UNROLL and not (isinstance(k, int) and k < 0):
                            find(k - q, q + 1, 1)

                    tiles(pe, step, begin)

                @blk.vector
                def _(dve):
                    def step(k, q, ahead, now, back1, back2, back3):
                        p = q % 2
                        if now:
                            dve.wait_ge(m["m_h"], k + 1)
                            after(dve, m["m_gs"], k - 1)
                            dve.tensor_scalar(gate[:, p], B_H[p][:, 0:HID], LIMIT, GUARD, ALU.min,
                                              ALU.max).then_inc(m["m_gate"], 1)
                        if ahead:
                            dve.wait_ge(m["m_hi"], k + 2)
                            after(dve, m["m_h"], k)
                            dve.tensor_tensor(tlo[:, 1 - p], bank[0][:, 0:P], thi[:, 1 - p],
                                              ALU.subtract).then_inc(m["m_lo"], 1)
                        if now:
                            after(dve, m["m_hid"], k - 1)
                            dve.tensor_scalar(lin[:, p], B_H[p][:, HID:], LIMIT, -LIMIT, ALU.min,
                                              ALU.max).then_inc(m["m_lin"], 1)
                        if back1:
                            dve.wait_ge(m["m_gs"], k)
                            dve.wait_ge(m["m_lin"], k)
                            after(dve, m["m_hT"], k - 2)
                            dve.scalar_tensor_tensor(hid[:, 1 - p], lin[:, 1 - p], 1.0, sig[:, 1 - p], ALU.add,
                                                     ALU.mult).then_inc(m["m_hid"], 1)
                        if back2:
                            dve.wait_ge(m["m_hhi"], k - 1)
                            after(dve, m["m_y"], k - 3)
                            dve.tensor_tensor(hlo[:, p], B_HT[p][:, 0:HID], hhi[:, p],
                                              ALU.subtract).then_inc(m["m_hlo"], 1)

                    tiles(dve, step)

                @blk.scalar
                def _(act):
                    def step(k, q, ahead, now, back1, back2, back3):
                        p = q % 2
                        if now:
                            act.wait_ge(m["m_gate"], k + 1)
                            after(act, m["m_hid"], k - 1)
                            act.activation(sig[:, p], gate[:, p], ACT.Exp, scale=-ALPHA).then_inc(m["m_e1"], 1)
                        if ahead:
                            act.wait_ge(m["m_T"], k + 2)
                            after(act, m["m_h"], k)
                            act.activation(thi[:, 1 - p], bank[0][:, 0:P], ACT.Copy).then_inc(m["m_hi"], 1)
                        if now:
                            act.wait_ge(m["m_e1"], k + 1)
                            act.activation(sig[:, p], sig[:, p], ACT.Ln, bias=1.0).then_inc(m["m_e2"], 1)
                        if back2:
                            act.wait_ge(m["m_hT"], k - 1)
                            after(act, m["m_y"], k - 3)
                            act.activation(hhi[:, p], B_HT[p][:, 0:HID], ACT.Copy).then_inc(m["m_hhi"], 1)
                        if now:
                            act.wait_ge(m["m_e2"], k + 1)
                            act.activation(sig[:, p], sig[:, p], ACT.Exp, scale=-1.0).then_inc(m["m_sig"], 1)
                        if back3:
                            t, q8 = k - 3, (q + 5) % 8
                            qt = q8 % RING
                            act.wait_ge(m["m_where"], k - 2)
                            act.wait_ge(m["m_y"], k - 2)
                            if not (isinstance(k, int) and t < RING):
                                act.wait_ge(m_out[qt], sent_out(t, qt) - 16)
                            act.activation(yw[:, qt], B_Y[1 - p][:, 0:P], ACT.Copy,
                                           scale=wgt[:, q8:q8 + 1]).then_inc(m["m_yw"], 1)

                    tiles(act, step)

                @blk.gpsimd
                def _(pool):
                    def step(k, q, ahead, now, back1, back2, back3):
                        p, qt = q % 2, q % RING
                        if now:
                            pool.wait_ge(m["m_sig"], k + 1)
                            pool.tensor_tensor(sig[:, p], gate[:, p], sig[:, p], ALU.mult).then_inc(m["m_gs"], 1)
                            fence(pool, m_in[q], filled(k, q))
                            fence(pool, m_out[qt], sent_out(k, qt) - 32)
                            pool.tensor_copy(wgt[:, q:q + 1], G[:, q, P:P + 1])
                            pool.tensor_copy(where[:, q:q + 1], G[:, q, P + 1:W]).then_inc(m["m_where"], 1)
                        if back3:
                            q8 = (q + 5) % 8
                            pool.wait_ge(m["m_yw"], k - 2)
                            fence(pool, m["m_where"], k - 2)
                            pool.indirect_dma_start(
                                results, bass.IndirectOffsetOnAxis(ap=where[:, q8:q8 + 1], axis=0),
                                yw[:, q8 % RING], None, bounds_check=TOP * N - 1,
                                oob_is_err=False).then_inc(m_out[q8 % RING], 16)

                    tiles(pool, step)
                    for q in range(RING):
                        pool.wait_ge(m_out[q], 16 * (TILES // RING))

        with ExitStack() as stage:
            def st(name, shape, dt=F32):
                return stage.enter_context(nc.sbuf_tensor(name, shape, dt))

            Y = st("Y", [P, 2, TOP, C, P])
            U4, Z4, O4 = st("U4", [P, 2, C, P]), st("Z4", [P, 2, C, P]), st("O4", [P, 2, C, P])
            st4, mv4, rs4 = st("st4", [P, 2, C, 6]), st("mv4", [P, 2, C, 2]), st("rs4", [P, 2, C])
            o = sems("o_sum o_u o_z o_st o_mv o_ln o_rs o_n o_x o_const")
            o_in, o_out = (sem("o_in0"), sem("o_in1")), (sem("o_out0"), sem("o_out1"))
            eps4 = st("eps4", [P, 1])

            def both(eng, step):
                step(0, 0)
                step(1, 1)
                with eng.Fori(1, NB // 2) as r:
                    for i in range(2):
                        step(2 * r + i, i)

            def staggered(eng, first, second):
                def step(b, p):
                    first(b, p)
                    second(b - 1, 1 - p)

                first(0, 0)
                for b in range(1, 4):
                    step(b, b % 2)
                with eng.Fori(2, NB // 2) as r:
                    for i in range(2):
                        step(2 * r + i, i)
                second(NB - 1, 1)

            with nc.Block() as blk:
                @blk.sync
                def _(sp):
                    def step(b, p):
                        after(sp, o["o_z"], b - 1)
                        for k in range(TOP):
                            sp.dma_start(Y[:, p, k], rv[:, k, bass.ds(b * C, C), :]).then_inc(o_in[p], 16)

                    both(sp, step)

                @blk.gpsimd
                def _(pool):
                    def step(b, p):
                        pool.wait_ge(o_in[p], 16 * b - 16 * p + 32)
                        pool.tensor_tensor(Y[:, p, 0], Y[:, p, 0], Y[:, p, 1], ALU.add).then_inc(o["o_sum"], 1)

                    both(pool, step)

                @blk.vector
                def _(dve):
                    dve.memset(eps4[:], EPS_LN).then_inc(o["o_const"], 1)

                    def statistics(b, p):
                        n = b + 1
                        after(dve, o["o_x"], n - 2)
                        for c in range(C):
                            last = dve.tensor_scalar(U4[:, p, c], X[:, bass.ds(b * C + c, 1), :],
                                                     NORM3[:, bass.ds(b * C + c, 1), 0],
                                                     NORM3[:, bass.ds(b * C + c, 1), 1],
                                                     ALU.subtract, ALU.mult)
                        last.then_inc(o["o_u"], 1)
                        dve.wait_ge(o["o_u"], n)
                        dve.wait_ge(o["o_sum"], n)
                        after(dve, o["o_n"], n - 2)
                        dve.tensor_tensor(Z4[:, p], U4[:, p], Y[:, p, 0], ALU.add).then_inc(o["o_z"], 1)
                        dve.wait_ge(o["o_z"], n)
                        after(dve, o["o_mv"], n - 2)
                        for c in range(C):
                            last = dve.bn_stats(st4[:, p, c], Z4[:, p, c])
                        last.then_inc(o["o_st"], 1)
                        after(dve, o["o_ln"], n - 2)
                        after(dve, o["o_n"], n - 2)
                        fence(dve, o["o_st"], n)
                        for c in range(C):
                            last = dve.bn_aggr(mv4[:, p, c], st4[:, p, c])
                        last.then_inc(o["o_mv"], 1)

                    def finish(b, p):
                        n = b + 1
                        dve.wait_ge(o["o_rs"], n)
                        for c in range(C):
                            last = dve.tensor_scalar(U4[:, p, c], Z4[:, p, c], mv4[:, p, c, 0:1],
                                                     rs4[:, p, c:c + 1], ALU.subtract, ALU.mult)
                        last.then_inc(o["o_n"], 1)
                        dve.wait_ge(o["o_n"], n)
                        after(dve, o_out[p], 16 * (b - p) // 2 if isinstance(b, int) else 8 * b - 8 * p)
                        dve.tensor_tensor(O4[:, p], X[:, bass.ds(b * C, C), :], U4[:, p], ALU.add).then_inc(o["o_x"], 1)

                    staggered(dve, statistics, finish)

                @blk.scalar
                def _(act):
                    act.wait_ge(o["o_const"], 1)

                    def deviations(b, p):
                        n = b + 1
                        act.wait_ge(o["o_mv"], n)
                        after(act, o["o_n"], n - 2)
                        act.activation(rs4[:, p], mv4[:, p, :, 1], ACT.Ln, bias=eps4[:, 0:1]).then_inc(o["o_ln"], 1)
                        act.wait_ge(o["o_ln"], n)
                        act.activation(rs4[:, p], rs4[:, p], ACT.Exp, scale=-0.5).then_inc(o["o_rs"], 1)

                    def store(b, p):
                        act.wait_ge(o["o_x"], b + 1)
                        act.dma_start(ov[:, bass.ds(b * C, C), :], O4[:, p]).then_inc(o_out[p], 16)

                    staggered(act, deviations, store)
                    for p in range(2):
                        act.wait_ge(o_out[p], 16 * (NB // 2))


_INS = ["L0_attn_x", "L0_attn_W_qkv", "L0_attn_conv_w", "L0_attn_W_z", "L0_attn_W_b", "L0_attn_W_a",
        "L0_attn_dt_bias", "L0_attn_A_log", "L0_attn_W_out", "L0_ffn_norm_scale", "L0_ffn_gate_w",
        "L0_ffn_gate_b", "L0_ffn_mlp1_w", "L0_ffn_mlp1_b", "L0_ffn_mlp2_w", "L0_ffn_mlp2_b"]


def kernel(**inputs):
    import numpy as _np
    import concourse.bacc as _bacc
    from concourse import mybir as _mybir
    from concourse.bass_utils import run_bass_kernel_spmd as _run

    nc = _bacc.Bacc("TRN2", target_bir_lowering=False, num_devices=1)
    arrays, args = {}, []
    for name in _INS:
        a = _np.ascontiguousarray(inputs[name])
        arrays[f"in_{name}_dram"] = a
        args.append(nc.dram_tensor(f"in_{name}_dram", a.shape, _mybir.dt.from_np(a.dtype), kind="ExternalInput").ap())
    shape = inputs["L0_attn_x"].shape
    args.append(nc.dram_tensor("out_0_dram", shape, _mybir.dt.float32, kind="ExternalOutput").ap())
    build_program(nc, *args)
    r = _run(nc, [arrays], core_ids=[0])
    return r.results[0]["out_0_dram"]
```
